# Optimizing a Trainium2 kernel written in Bass

```python
import numpy as np
import jax
import jax.numpy as jnp

def _softmax(x, axis=-1):
    return jax.nn.softmax(x, axis=axis)

def _gelu(x):
    return jax.nn.gelu(x, approximate=True)

def _silu(x):
    return jax.nn.silu(x)

def _sigmoid(x):
    return jax.nn.sigmoid(x)

def _layernorm(x, axis=-1, eps=1e-05):
    m = jnp.mean(x, axis=axis, keepdims=True)
    v = jnp.var(x, axis=axis, keepdims=True)
    return (x - m) / jnp.sqrt(v + eps)

def _scatter_add(tgt, idx, src, axis=0):
    return tgt.at[idx].add(src)

def _segment_sum(src, seg, n):
    return jax.ops.segment_sum(src, seg, n)
kernel_name = 'mk_xattn_ffn_d2_seqx_r8_adae6a'

def setup_inputs(seed: int=0):
    np.random.seed(seed)
    _w = jnp.asarray

    def _rec_inputs():
        import jax
        import jax.numpy as jnp
        _rk = jax.random.key(seed)
        x = -0.0002928 + 1 * jax.random.normal(jax.random.fold_in(_rk, 1), (4, 512, 128), jnp.float32)
        _lenS = 512 - jax.random.randint(jax.random.fold_in(_rk, 7), (4,), 0, max(1, 512 // 4) + 1, jnp.int32)
        _lenS2 = 77 - jax.random.randint(jax.random.fold_in(_rk, 8), (4,), 0, max(1, 77 // 4) + 1, jnp.int32)
        _ctx_1024P = jax.random.normal(jax.random.fold_in(_rk, 11), (4, 16, 128), jnp.float32)
        _ctx_1024c = jax.random.dirichlet(jax.random.fold_in(_rk, 511), 0.3 * jnp.ones((16,), jnp.float32), (4, 77))
        _ctx_1024t = jnp.einsum('bsk,bkd->bsd', _ctx_1024c, _ctx_1024P)
        _ctx_1024t = _ctx_1024t * jax.lax.rsqrt(jnp.mean(jnp.square(_ctx_1024t)) + 1e-12) * 0.953939
        ctx_1024 = 4.13588e-05 + 0.999923 * (_ctx_1024t + 0.3 * jax.random.normal(jax.random.fold_in(_rk, 611), (4, 77, 128), jnp.float32))
        fside_SxS2_0 = 0.00086875 + 0.999764 * jax.random.normal(jax.random.fold_in(_rk, 12), (512, 77), jnp.float32)
        return (x, ctx_1024, fside_SxS2_0)
    x, ctx_1024, fside_SxS2_0 = _rec_inputs()

    def _L0_xattn_setup():
        import jax, jax.numpy as jnp
        import numpy as np
        NUM_HEADS = 16
        EPS = 1e-12
        MAX_SCALE_MUL = float(np.log(100.0))

        def _l2norm(t):
            n = jnp.sqrt(jnp.sum(t * t, axis=-1, keepdims=True))
            return t / jnp.maximum(n, EPS)
        key = jax.random.key(seed)
        ks = jax.random.split(key, 10)
        B, Lq, Ly, C = (4, 128, 256, 128)
        s = 1.0 / np.sqrt(C)
        return {'x': jax.random.normal(ks[0], (B, Lq, C), jnp.float32), 'y': jax.random.normal(ks[1], (B, Ly, C), jnp.float32), 'attn_bias': jax.random.normal(ks[2], (Lq, Ly), jnp.float32), 'Wq': jax.random.normal(ks[3], (C, C), jnp.float32) * s, 'bq': jnp.zeros((C,), jnp.float32), 'Wk': jax.random.normal(ks[4], (C, C), jnp.float32) * s, 'Wv': jax.random.normal(ks[5], (C, C), jnp.float32) * s, 'Wo': jax.random.normal(ks[6], (C, C), jnp.float32) * s, 'bo': jnp.zeros((C,), jnp.float32), 'scale_mul_log': jnp.full((1, NUM_HEADS, 1, 1), np.log(4.0), jnp.float32)}
    _L0_xattn_all = _L0_xattn_setup()
    _L0_xattn_in = {k: v for k, v in _L0_xattn_all.items() if k in ('Wq', 'bq', 'Wk', 'Wv', 'Wo', 'bo', 'scale_mul_log')}
    del _L0_xattn_all

    def _L0_ffn_setup():
        import jax, jax.numpy as jnp
        import numpy as np
        DIM = 128
        HIDDEN = 256
        NUM_EXPERTS = 8
        TOP_K = 2
        key = jax.random.key(seed)
        ks = jax.random.split(key, 5)
        x = jax.random.normal(ks[0], (4, 128, DIM), dtype=jnp.float32)
        Wr = jax.random.normal(ks[1], (DIM, NUM_EXPERTS), dtype=jnp.float32) * 0.02
        W1 = jax.random.normal(ks[2], (NUM_EXPERTS, DIM, HIDDEN), dtype=jnp.float32) * 0.02
        W3 = jax.random.normal(ks[3], (NUM_EXPERTS, DIM, HIDDEN), dtype=jnp.float32) * 0.02
        W2 = jax.random.normal(ks[4], (NUM_EXPERTS, HIDDEN, DIM), dtype=jnp.float32) * 0.02
        return {'x': x, 'Wr': Wr, 'W1': W1, 'W2': W2, 'W3': W3}
    _L0_ffn_all = _L0_ffn_setup()
    _L0_ffn_in = {k: v for k, v in _L0_ffn_all.items() if k in ('Wr', 'W1', 'W2', 'W3')}
    del _L0_ffn_all

    def _L1_xattn_setup():
        import jax, jax.numpy as jnp
        import numpy as np
        DIM = 128
        CTX_DIM = 128
        HEADS = 16
        DIM_HEAD = 64
        INNER = HEADS * DIM_HEAD
        FF_INNER = 4 * DIM
        EPS = 1e-05

        def layer_norm(x, g, b):
            mu = jnp.mean(x, axis=-1, keepdims=True)
            var = jnp.var(x, axis=-1, keepdims=True)
            return (x - mu) * jax.lax.rsqrt(var + EPS) * g + b
        key = jax.random.key(seed)
        ks = jax.random.split(key, 9)
        b, n, j = (4, 256, 128)
        inp = {'x': jax.random.normal(ks[0], (b, n, DIM), dtype=jnp.float32), 'context': jax.random.normal(ks[1], (b, j, CTX_DIM), dtype=jnp.float32), 'ln_g': jnp.ones((DIM,), jnp.float32), 'ln_b': jnp.zeros((DIM,), jnp.float32), 'cln_g': jnp.ones((CTX_DIM,), jnp.float32), 'cln_b': jnp.zeros((CTX_DIM,), jnp.float32), 'Wq': jax.random.normal(ks[2], (DIM, INNER), dtype=jnp.float32) * DIM ** (-0.5), 'Wkv': jax.random.normal(ks[3], (CTX_DIM, 2 * DIM_HEAD), dtype=jnp.float32) * CTX_DIM ** (-0.5), 'Wo': jax.random.normal(ks[4], (INNER, DIM), dtype=jnp.float32) * INNER ** (-0.5), 'Wff1': jax.random.normal(ks[5], (DIM, 2 * FF_INNER), dtype=jnp.float32) * DIM ** (-0.5), 'Wff2': jax.random.normal(ks[6], (FF_INNER, DIM), dtype=jnp.float32) * FF_INNER ** (-0.5)}
        return inp
    _L1_xattn_all = _L1_xattn_setup()
    _L1_xattn_in = {k: v for k, v in _L1_xattn_all.items() if k in ('ln_g', 'ln_b', 'cln_g', 'cln_b', 'Wq', 'Wkv', 'Wo', 'Wff1', 'Wff2')}
    del _L1_xattn_all

    def _L1_ffn_setup():
        import jax, jax.numpy as jnp
        import numpy as np
        E = 8
        K = 2
        D = 128
        P = 512
        key = jax.random.key(seed)
        ks = jax.random.split(key, 8)
        s = lambda fan_in: 1.0 / np.sqrt(fan_in)
        x = jax.random.normal(ks[0], (2, 256, D), dtype=jnp.float32)
        W1 = jax.random.normal(ks[1], (E, D, P), dtype=jnp.float32) * s(D)
        b1 = jax.random.normal(ks[2], (E, P), dtype=jnp.float32) * 0.01
        W2 = jax.random.normal(ks[3], (E, P, D), dtype=jnp.float32) * s(P)
        b2 = jax.random.normal(ks[4], (E, D), dtype=jnp.float32) * 0.01
        Wr = jax.random.normal(ks[5], (D, E), dtype=jnp.float32) * s(D)
        br = jax.random.normal(ks[6], (E,), dtype=jnp.float32) * 0.01
        return {'x': x, 'W1': W1, 'b1': b1, 'W2': W2, 'b2': b2, 'Wr': Wr, 'br': br}
    _L1_ffn_all = _L1_ffn_setup()
    _L1_ffn_in = {k: v for k, v in _L1_ffn_all.items() if k in ('W1', 'b1', 'W2', 'b2', 'Wr', 'br')}
    del _L1_ffn_all
    return {'x': x, 'ctx_1024': ctx_1024, 'fside_SxS2_0': fside_SxS2_0, 'L0_xattn_Wq': _L0_xattn_in['Wq'], 'L0_xattn_bq': _L0_xattn_in['bq'], 'L0_xattn_Wk': _L0_xattn_in['Wk'], 'L0_xattn_Wv': _L0_xattn_in['Wv'], 'L0_xattn_Wo': _L0_xattn_in['Wo'], 'L0_xattn_bo': _L0_xattn_in['bo'], 'L0_xattn_scale_mul_log': _L0_xattn_in['scale_mul_log'], 'L0_ffn_Wr': _L0_ffn_in['Wr'], 'L0_ffn_W1': _L0_ffn_in['W1'], 'L0_ffn_W2': _L0_ffn_in['W2'], 'L0_ffn_W3': _L0_ffn_in['W3'], 'L1_xattn_ln_g': _L1_xattn_in['ln_g'], 'L1_xattn_ln_b': _L1_xattn_in['ln_b'], 'L1_xattn_cln_g': _L1_xattn_in['cln_g'], 'L1_xattn_cln_b': _L1_xattn_in['cln_b'], 'L1_xattn_Wq': _L1_xattn_in['Wq'], 'L1_xattn_Wkv': _L1_xattn_in['Wkv'], 'L1_xattn_Wo': _L1_xattn_in['Wo'], 'L1_xattn_Wff1': _L1_xattn_in['Wff1'], 'L1_xattn_Wff2': _L1_xattn_in['Wff2'], 'L1_ffn_W1': _L1_ffn_in['W1'], 'L1_ffn_b1': _L1_ffn_in['b1'], 'L1_ffn_W2': _L1_ffn_in['W2'], 'L1_ffn_b2': _L1_ffn_in['b2'], 'L1_ffn_Wr': _L1_ffn_in['Wr'], 'L1_ffn_br': _L1_ffn_in['br']}

def reference(x, ctx_1024, fside_SxS2_0, L0_xattn_Wq, L0_xattn_bq, L0_xattn_Wk, L0_xattn_Wv, L0_xattn_Wo, L0_xattn_bo, L0_xattn_scale_mul_log, L0_ffn_Wr, L0_ffn_W1, L0_ffn_W2, L0_ffn_W3, L1_xattn_ln_g, L1_xattn_ln_b, L1_xattn_cln_g, L1_xattn_cln_b, L1_xattn_Wq, L1_xattn_Wkv, L1_xattn_Wo, L1_xattn_Wff1, L1_xattn_Wff2, L1_ffn_W1, L1_ffn_b1, L1_ffn_W2, L1_ffn_b2, L1_ffn_Wr, L1_ffn_br):
    import jax
    import jax.numpy as jnp

    def _L0_xattn_ref(x, y, attn_bias, Wq, bq, Wk, Wv, Wo, bo, scale_mul_log):
        import jax, jax.numpy as jnp
        import numpy as np
        NUM_HEADS = 16
        EPS = 1e-12
        MAX_SCALE_MUL = float(np.log(100.0))

        def _l2norm(t):
            n = jnp.sqrt(jnp.sum(t * t, axis=-1, keepdims=True))
            return t / jnp.maximum(n, EPS)
        B, Lq, C = x.shape
        Ly = y.shape[1]
        H = NUM_HEADS
        D = C // H
        q = (x @ Wq + bq).reshape(B, Lq, H, D).transpose(0, 2, 1, 3)
        k = (y @ Wk).reshape(B, Ly, H, D).transpose(0, 2, 1, 3)
        v = (y @ Wv).reshape(B, Ly, H, D).transpose(0, 2, 1, 3)
        scale_mul = jnp.exp(jnp.minimum(scale_mul_log, MAX_SCALE_MUL))
        q = _l2norm(q) * scale_mul
        k = _l2norm(k)
        attn = jnp.einsum('bhqd,bhkd->bhqk', q, k) + attn_bias
        attn = jax.nn.softmax(attn, axis=-1)
        oup = jnp.einsum('bhqk,bhkd->bhqd', attn, v)
        oup = oup.transpose(0, 2, 1, 3).reshape(B, Lq, C)
        return oup @ Wo + bo

    def _L0_ffn_ref(x, Wr, W1, W2, W3):
        import jax, jax.numpy as jnp
        import numpy as np
        DIM = 128
        HIDDEN = 256
        NUM_EXPERTS = 8
        TOP_K = 2
        B, S, D = x.shape
        T = B * S
        xf = x.reshape(T, D)
        probs = jax.nn.softmax(xf @ Wr, axis=-1)
        topk_p, topk_i = jax.lax.top_k(probs, TOP_K)
        topk_p = topk_p / jnp.sum(topk_p, axis=-1, keepdims=True)
        gate = jnp.sum(jax.nn.one_hot(topk_i, NUM_EXPERTS, dtype=xf.dtype) * topk_p[:, :, None], axis=1)
        h = jax.nn.silu(jnp.einsum('td,edh->teh', xf, W1)) * jnp.einsum('td,edh->teh', xf, W3)
        out_e = jnp.einsum('teh,ehd->ted', h, W2)
        out = jnp.einsum('ted,te->td', out_e, gate)
        return out.reshape(B, S, D)

    def _L1_xattn_ref(x, context, ln_g, ln_b, cln_g, cln_b, Wq, Wkv, Wo, Wff1, Wff2):
        import jax, jax.numpy as jnp
        import numpy as np
        DIM = 128
        CTX_DIM = 128
        HEADS = 16
        DIM_HEAD = 64
        INNER = HEADS * DIM_HEAD
        FF_INNER = 4 * DIM
        EPS = 1e-05

        def layer_norm(x, g, b):
            mu = jnp.mean(x, axis=-1, keepdims=True)
            var = jnp.var(x, axis=-1, keepdims=True)
            return (x - mu) * jax.lax.rsqrt(var + EPS) * g + b
        scale = DIM_HEAD ** (-0.5)
        xn = layer_norm(x, ln_g, ln_b)
        cn = layer_norm(context, cln_g, cln_b)
        b, n, _ = xn.shape
        q = (xn @ Wq).reshape(b, n, HEADS, DIM_HEAD).transpose(0, 2, 1, 3) * scale
        kv = cn @ Wkv
        k, v = (kv[..., :DIM_HEAD], kv[..., DIM_HEAD:])
        sim = jnp.einsum('bhid,bjd->bhij', q, k)
        attn = jax.nn.softmax(sim, axis=-1)
        out = jnp.einsum('bhij,bjd->bhid', attn, v)
        out = out.transpose(0, 2, 1, 3).reshape(b, n, INNER) @ Wo
        ff = xn @ Wff1
        h, gate = (ff[..., :FF_INNER], ff[..., FF_INNER:])
        out = out + jax.nn.silu(gate) * h @ Wff2
        return out

    def _L1_ffn_ref(x, W1, b1, W2, b2, Wr, br):
        import jax, jax.numpy as jnp
        import numpy as np
        E = 8
        K = 2
        D = 128
        P = 512
        B, S, _ = x.shape
        xf = x.reshape(B * S, D)
        scores = xf @ Wr + br
        _, top_idx = jax.lax.top_k(scores, K)
        mask = jax.nn.one_hot(top_idx, E, dtype=scores.dtype).sum(-2) > 0
        router_weights = jax.nn.softmax(jnp.where(mask, scores, -jnp.inf), axis=-1)
        h = jax.nn.gelu(jnp.einsum('td,edp->etp', xf, W1) + b1[:, None, :])
        y = jnp.einsum('etp,epd->etd', h, W2) + b2[:, None, :]
        out = jnp.einsum('te,etd->td', router_weights, y)
        return out.reshape(B, S, D)
    x = x + _L0_xattn_ref(_layernorm(x, axis=-1), ctx_1024, fside_SxS2_0, L0_xattn_Wq, L0_xattn_bq, L0_xattn_Wk, L0_xattn_Wv, L0_xattn_Wo, L0_xattn_bo, L0_xattn_scale_mul_log)
    x = x + _L0_ffn_ref(_layernorm(x, axis=-1), L0_ffn_Wr, L0_ffn_W1, L0_ffn_W2, L0_ffn_W3)
    x = x + _L1_xattn_ref(_layernorm(x, axis=-1), ctx_1024, L1_xattn_ln_g, L1_xattn_ln_b, L1_xattn_cln_g, L1_xattn_cln_b, L1_xattn_Wq, L1_xattn_Wkv, L1_xattn_Wo, L1_xattn_Wff1, L1_xattn_Wff2)
    x = x + _L1_ffn_ref(_layernorm(x, axis=-1), L1_ffn_W1, L1_ffn_b1, L1_ffn_W2, L1_ffn_b2, L1_ffn_Wr, L1_ffn_br)
    return x

_drawn_inputs = setup_inputs


def setup_inputs(seed=0):
    import zlib

    import numpy as np

    out = dict(_drawn_inputs(seed))
    spreads = {'L0_xattn_bq': (0.0, 0.1),
     'L0_xattn_bo': (0.0, 0.1),
     'L0_xattn_scale_mul_log': (1.3862943649291992, 0.2),
     'L1_xattn_ln_g': (1.0, 0.2),
     'L1_xattn_ln_b': (0.0, 0.1),
     'L1_xattn_cln_g': (1.0, 0.2),
     'L1_xattn_cln_b': (0.0, 0.1)}
    factors = {'L0_ffn_Wr': 3.881,
     'L0_ffn_W1': 3.922,
     'L0_ffn_W2': 3.767,
     'L0_ffn_W3': 3.444,
     'L1_ffn_b1': 8.0,
     'L1_ffn_b2': 8.0,
     'L1_ffn_br': 2.808}
    for name, (base, spread) in spreads.items():
        noise = np.random.default_rng([zlib.crc32(name.encode()), seed]).standard_normal(out[name].shape)
        drawn = base * np.exp(spread * noise) if base else spread * noise
        out[name] = jnp.asarray(drawn.astype(out[name].dtype))
    for name, factor in factors.items():
        out[name] = (out[name] * factor).astype(out[name].dtype)
    return out
```

```python
from contextlib import ExitStack

import numpy as np
import concourse.bass as bass
from concourse import mybir

F32 = mybir.dt.float32
F32R = mybir.dt.float32r
BF16 = mybir.dt.bfloat16
I32 = mybir.dt.int32
U32 = mybir.dt.uint32
ACT = mybir.ActivationFunctionType
ALU = mybir.AluOpType
AX = mybir.AxisListType.X

P = 128
EPS = 1e-5
NORM_FLOOR = 1e-24
MAX_LOG_SCALE = float(np.log(100.0))
NCONST = 4


def bass_xattn_moe_two_layers(nc, x_in, ctx_in, bias_in, Wq0, bq0, Wk0, Wv0, Wo0, bo0, scale_log,
                              Wr0, W1_0, W2_0, W3_0, ln_g, ln_b, cln_g, cln_b, Wq1, Wkv1, Wo1,
                              Wff1, Wff2, W1_1, b1_1, W2_1, b2_1, Wr1, br1, out):
    NBATCH, SEQ, D = x_in.shape
    KEYS = ctx_in.shape[1]
    H = scale_log.shape[1]
    HD0 = D // H
    HD1 = Wq1.shape[1] // H
    E, _, F0 = W1_0.shape
    F1 = W1_1.shape[2]
    FF = Wff2.shape[0]
    T = NBATCH * SEQ
    NT = T // P
    TPB = SEQ // P
    HK = H * KEYS
    CH = -(-HK // P)
    HKP = CH * P
    G = 4
    NG = H // G
    GK = G * KEYS
    VW = HD0 + 1
    BANK_HEADS = [6, 4, 6]
    BANK_AT = [0, 6, 10]
    BK = max(BANK_HEADS) * KEYS
    ROW = D + 1
    NJ = 2 * T // P + E
    REGION = T
    SLOTS = E * REGION + E * P
    NOWHERE = 1 << 20
    XB = 4
    assert D == P and H * HD0 == P and G * 4 * HD0 == P and F0 * 2 == F1 == 512 and TPB == 4 and FF == 512

    def at(i):
        return bass.ds(i, 1)

    with ExitStack() as ctx:
        def sb(name, shape, dt=F32):
            return ctx.enter_context(nc.sbuf_tensor(name, shape, dt))

        def sem(name):
            return ctx.enter_context(nc.semaphore(name))

        x = sb("x", [P, NT, D])
        with ExitStack() as early:
            def sb_early(name, shape, dt=F32):
                return early.enter_context(nc.sbuf_tensor(name, shape, dt))

            keys0 = sb_early("keys0", [P, NBATCH, HK], F32R)
            bias_r = sb_early("bias_r", [P, 2, TPB, GK], F32R)
            qT_both = sb_early("qT", [P, 2, NG * P], F32R)
        qT = [qT_both[:, 0], qT_both[:, 1]]
        w2b = sb("w2b", [P, E, F1 // P, D])
        vals1 = sb("vals1", [P, NBATCH, CH, D])
        region_a = sb("region_a", [P, NBATCH * CH * H * VW])
        vals0 = region_a[:, :].rearrange("p (b c h v) -> p b c h v", b=NBATCH, c=CH, h=H)
        w1b = region_a[:, 0:E * F1].rearrange("p (e f) -> p e f", e=E)
        b2bc = region_a[:, E * F1:E * F1 + E * D].rearrange("p (e d) -> p e d", e=E)
        region_b = sb("region_b", [P, E * 2 * F0])
        w13 = region_b[:, :].rearrange("p (e f) -> p e f", e=E)
        b1bc = region_b[:, :].rearrange("p (e f) -> p e f", e=E)
        w2a = sb("w2a", [P, E, F0 // P, D])
        keys1 = sb("keys1", [P, NBATCH, HK])
        pp = sb("pp", [P, 4, HKP])
        prob = [pp[:, 0, :], pp[:, 1, :]]
        probT = [pp[:, 2, :], pp[:, 3, :]]
        ident = sb("ident", [P, P])
        ident_r = sb("ident_r", [P, P], F32R)
        mask16 = sb("mask16", [P, H])
        mask4 = sb("mask4", [P, G])
        headsel = sb("headsel", [P, CH, H])
        upper = sb("upper", [P, P], BF16)
        ones_b = sb("ones_b", [P, P], BF16)
        mhalf = sb("mhalf", [P, NBATCH * H])
        iota8 = sb("iota8", [P, E])
        iota8i = sb("iota8i", [P, E], I32)
        ebase = sb("ebase", [P, E])
        ebasei = sb("ebasei", [P, E], I32)
        dest = sb("dest", [P, NT, 2], I32)
        jidx = sb("jidx", [1, NJ])
        jidxi = sb("jidxi", [1, NJ], I32)
        ones1 = sb("ones1", [1, E])
        empty = sb("empty", [P, 4, ROW])
        ctx_sb = sb("ctx_sb", [KEYS, NBATCH, D])
        ctxT = sb("ctxT", [P, NBATCH * KEYS])
        bias_sb = sb("bias_sb", [P, TPB, KEYS])
        wk0 = sb("wk0", [P, D])
        wv0 = sb("wv0", [P, D])
        wq0 = sb("wq0", [P, D])
        wo0 = sb("wo0", [P, D])
        bq_bc = sb("bq_bc", [P, D])
        bo_bc = sb("bo_bc", [P, D])
        scl = sb("scl", [KEYS, H])
        wr = [sb("wr0", [P, E]), sb("wr1", [P, E])]
        br_bc = sb("br_bc", [P, E])
        yb_all = sb("yb_all", [P, 4, 2, D])
        yb = [yb_all[:, k] for k in range(4)]
        wq1 = yb_all[:, :, :, :].rearrange("p a b d -> p (a b d)")
        big1 = sb("big1", [P, 2, F1])
        big2 = sb("big2", [P, 2, F1])
        wq1T = big1[:, :, :].rearrange("p a (k c) -> p (a k) c", c=D)
        wkk = sb("wkk", [P, 2, HD1])
        wvv = sb("wvv", [P, 2, HD1])
        wo1 = big2[:, :, :].rearrange("p a (k c) -> p (a k) c", c=D)
        wff1 = sb("wff1", [P, 2 * FF])
        wff2 = sb("wff2", [P, FF // P, D])
        gb = sb("gb", [P, 4])
        kT1 = sb("kT1", [P, NBATCH * KEYS])
        vT1 = sb("vT1", [P, NBATCH * KEYS])
        vT0 = sb("vT0", [P, NBATCH * KEYS])
        k0sq = pp[0:KEYS, 2, 0:NBATCH * D]
        k0n = pp[0:KEYS, 2, NBATCH * D:2 * NBATCH * D]
        k0split = pp[0:KEYS, 0:2, 0:1024].rearrange("p a (r s w d) -> p a r s w d", s=2, w=2, d=HD0)
        vblk = [pp[:, 3, :], pp[:, 2, :]]
        foldT = [pp[:, b, :] for b in range(NBATCH)]
        k0ss = sb("k0ss", [KEYS, NBATCH * H])
        k0sm = sb("k0sm", [KEYS, NBATCH * H])
        k0r = sb("k0r", [KEYS, NBATCH * H])
        k0rs = sb("k0rs", [KEYS, NBATCH * H])
        cstat = sb("cstat", [KEYS, NBATCH, 6])
        cmv = sb("cmv", [KEYS, NBATCH, 2])
        cve = sb("cve", [KEYS, NBATCH])
        crs = sb("crs", [KEYS, NBATCH])
        cn = sb("cn", [KEYS, NBATCH, D])
        def two(name, shape, dt=F32):
            t = sb(name, [shape[0], 2] + shape[1:], dt)
            return [t[:, 0], t[:, 1]]
        stA, mvA, veA, rsA, xnA = two("stA", [P, 6]), two("mvA", [P, 2]), two("veA", [P, 1]), two("rsA", [P, 1]), two("xnA", [P, D])
        stD, mvD, veD, rsD = two("stD", [P, 6]), two("mvD", [P, 2]), two("veD", [P, 1]), two("rsD", [P, 1])
        xT = two("xT", [P, P])
        qb, qsq, qn = two("qb", [P, D]), two("qsq", [P, D]), two("qn", [P, D])
        qss, qsm, qr = two("qss", [P, H]), two("qsm", [P, H]), two("qr", [P, H])
        qsplit = [big1[:, k].rearrange("p (h a b d) -> p h a b d", a=2, b=2, d=HD0) for k in range(2)]
        mx, den, rden = two("mx", [P, H]), two("den", [P, H]), two("rden", [P, H])
        on, oT = two("on", [P, D]), two("oT", [P, P])
        pay = two("pay", [P, 2, ROW])
        x2T = two("x2T", [P, P])
        scr, top, topi = two("scr", [P, E]), two("top", [P, 8]), two("topi", [P, 8], U32)
        oh = two("oh", [P, 2, E])
        picks, before = two("picks", [P, E], BF16), two("before", [P, E], BF16)
        rank, rsel, slotf = two("rank", [P, E]), two("rsel", [P, 2, E]), two("slotf", [P, 2])
        slot = two("slot", [P, 2], I32)
        margin = sb("margin", [P, NT])
        gate = sb("gate", [P, 2, NT])
        gtmp = sb("gtmp", [P, 2, NT])
        ffbuf = [big1[:, 0], big1[:, 1]]
        gT = [big2[:, 0], big2[:, 1]]
        cnt_i = sb("cnt_i", [1, E], I32)
        cnt_s = sb("cnt_s", [1, E], I32)
        ntile = sb("ntile", [1, E])
        cum = sb("cum", [1, E])
        wgt = sb("wgt", [1, E])
        ind = sb("ind", [1, NJ, E - 1])
        ind2 = sb("ind2", [1, NJ, E - 1])
        ef = sb("ef", [1, NJ])
        rf = sb("rf", [1, NJ])
        rf2 = sb("rf2", [1, NJ])
        sched = [sb("sched0", [1, 2, NJ], I32), sb("sched1", [1, 2, NJ], I32)]
        xs = [sb(f"xs{i}", [P, ROW]) for i in range(XB)]
        back = [sb(f"back{i}", [P, 1], I32) for i in range(XB)]
        xsT = two("xsT", [P, P])
        ha = [big1[:, 0], big1[:, 1]]
        hT = [big2[:, 0], big2[:, 1]]
        ysb = two("ysb", [P, D])

        ps = ctx.enter_context(nc.psum_tensor("ps", [P, 8, 512], F32))
        S = [ps[:, k, :] for k in range(3)]
        TP = [ps[:, 3, :], ps[:, 4, :]]
        MA, MC, MD = ps[:, 5, :], ps[:, 6, :], ps[:, 7, :]

        rows = [nc.dram_tensor(f"rows{l}", (SLOTS, ROW), F32, kind="Internal").ap() for l in range(2)]
        ys = [nc.dram_tensor(f"ys{l}", (2 * T, D), F32, kind="Internal").ap() for l in range(2)]

        x_v = x_in.rearrange("b (t p) c -> p (b t) c", p=P)
        out_v = out.rearrange("b (t p) c -> p (b t) c", p=P)
        y_v = [y.rearrange("(t p k) d -> t p k d", p=P, k=2) for y in ys]

        class Stage:
            def __init__(self, tag, names, again=None):
                self.s, self.base = {}, {}
                for n in names:
                    name, self.base[n] = again[n] if again and n in again else (None, 0)
                    self.s[n] = sem(f"{n}_{tag}") if name is None else name

            def __getitem__(self, n):
                return self.s[n]

            def count(self, n, v):
                return self.base[n] + v

        BOTH = ["bnA", "mvA", "veA", "rsA", "xnA", "TxA", "xT", "S", "mx", "sub", "exp", "rden", "TP", "probT", "AV",
                "xa", "bnD", "mvD", "veD", "rsD", "xnD", "ret", "Tx2", "x2T", "route", "scr", "top", "topi", "margin",
                "oh", "picks", "before", "rank", "rankb", "rsel", "slotf", "slot"]
        ONLY0 = ["q", "qb", "qsq", "qss", "qsm", "qr", "qn", "qhi", "qlo", "Tq", "qT", "on", "To", "oT", "Wo"]
        ONLY1 = ["ffg", "ffth", "ffgg", "ffh", "ffo", "Tg", "gT", "comb", "comb1", "den", "norm"]
        MOE = ["back", "Tx", "xsT", "up", "act1", "act2", "Th", "hT", "down", "y"]
        ONCE = {"cnt": 1, "plan": 9, "sched": 1, "g1": 1, "gates": 3}
        PRO0 = {"ctxT": 1, "ctxTs": 1, "k": 1, "ksq": 1, "kss": 1, "ksm": 1, "kr": 1, "krs": 1, "kn": 1, "khi": 1,
                "klo": 1, "kT": NBATCH, "keys0": NBATCH, "v": 1, "vT": 1, "vblk": NBATCH, "vtp": NBATCH * CH,
                "vals0": NBATCH * 3, "ones": NBATCH, "identr": 1, "bhi": 1, "blo": TPB, "scl": 1, "scm": 1, "xbo": NT}
        PRO1 = ["cbn", "cmv", "cve", "crs", "cn", "cT", "cTs", "kv1", "kT1", "vT1", "wqT", "wqTs", "fk", "keys1", "fv",
                "foldT", "fT", "vals1"]
        att0 = Stage("a", BOTH + ONLY0)
        again = {n: (att0[n], 3 * NT if n in ("TP", "probT") else NT) for n in BOTH}
        again.update({n: (att0[o], NT) for n, o in zip(ONLY1, ONLY0)})
        A = [att0, Stage("a", BOTH + ONLY1, again)]
        moe0 = Stage("m", MOE + list(ONCE))
        again = {n: (moe0[n], NJ) for n in MOE}
        again.update({n: (moe0[n], c) for n, c in ONCE.items()})
        M = [moe0, Stage("m", MOE + list(ONCE) + ["fin", "fin0"], again)]
        pro = Stage("p", PRO0)
        pro1 = Stage("p", PRO1, {n: (pro[o], PRO0[o]) for n, o in zip(PRO1, list(PRO0))})
        ld = {n: sem(f"ld_{n}") for n in ("x", "ctx", "q", "o", "moe0", "l1", "l1b", "moe1", "bias")}
        filled = [sem("filled0"), sem("filled1")]
        xs_in = [sem(f"xs_in{i}") for i in range(XB)]
        sent = [sem(f"sent{i}") for i in range(2)]
        sentb = [sem(f"sentb{i}") for i in range(XB)]
        y_in = [sem(f"y_in{i}") for i in range(4)]
        stored = sem("stored")
        const = sem("const")

        def sent_count(l, t):
            return 32 * (l * NT // 2 + t // 2 + 1)

        def sentb_count(l, j):
            return 16 * (l * NJ // XB + j // XB + 1)

        LAG = 5

        def row_of(ap, n):
            return ap.rearrange("(a n) -> a n", a=1).to_broadcast([P, n])

        block = ctx.enter_context(nc.Block())

        @block.sync
        def _(sp):
            sp.dma_start(ctx_sb[:, :, :], ctx_in.rearrange("b k c -> k b c")).then_inc(ld["ctx"], 16)
            sp.dma_start(wk0[:, :], Wk0).then_inc(ld["ctx"], 16)
            sp.dma_start(wv0[:, :], Wv0).then_inc(ld["ctx"], 16)
            sp.dma_start(x[:, :, :], x_v).then_inc(ld["x"], 16)
            sp.wait_ge(const, 1)
            for l in range(2):
                dst = rows[l].rearrange("(n p r) c -> n p (r c)", p=P, r=4)
                for n in range(SLOTS // P // 4):
                    sp.dma_start(dst[n], empty[:, :, :].rearrange("p r c -> p (r c)")).then_inc(filled[l], 16)
                if l == 0:
                    sp.dma_start(w13[:, :, 0:F0], W1_0.rearrange("e c f -> c e f")).then_inc(ld["moe0"], 16)
                    sp.dma_start(w13[:, :, F0:2 * F0], W3_0.rearrange("e c f -> c e f")).then_inc(ld["moe0"], 16)
                    sp.dma_start(w2a[:, :, :, :], W2_0.rearrange("e (k p) d -> p e k d", p=P)).then_inc(ld["moe0"], 16)
                    sp.dma_start(wq1[:, :], Wq1).then_inc(ld["l1"], 16)
                    for r in range(2):
                        sp.dma_start(wkk[:, r, :], Wkv1[:, 0:HD1]).then_inc(ld["l1"], 16)
                        sp.dma_start(wvv[:, r, :], Wkv1[:, HD1:2 * HD1]).then_inc(ld["l1"], 16)
                    sp.dma_start(wo1[:, :, :], Wo1.rearrange("(k p) d -> p k d", p=P)).then_inc(ld["l1"], 16)
                    for n, v in enumerate((ln_g, ln_b, cln_g, cln_b)):
                        sp.dma_start(gb[:, n:n + 1], v.rearrange("(c a) -> c a", a=1)).then_inc(ld["l1"], 16)
                    sp.dma_start(wff1[:, :], Wff1).then_inc(ld["l1b"], 16)
                    sp.dma_start(wff2[:, :, :], Wff2.rearrange("(k p) d -> p k d", p=P)).then_inc(ld["l1b"], 16)
                    sp.dma_start(wr[1][:, :], Wr1).then_inc(ld["l1b"], 16)
                    sp.dma_start(br_bc[:, :], row_of(br1, E)).then_inc(ld["l1b"], 16)
            for l in range(2):
                m = M[l]
                if l == 0:
                    sp.wait_ge(A[0]["AV"], A[0].count("AV", NT))
                    sp.dma_start(w2b[:, :, :, :], W2_1.rearrange("e (k p) d -> p e k d", p=P)).then_inc(ld["moe1"], 16)
                    sp.dma_start(w1b, W1_1.rearrange("e c f -> c e f")).then_inc(ld["moe1"], 16)
                    sp.dma_start(b2bc, b2_1.rearrange("(a e) d -> a e d", a=1).to_broadcast([P, E, D])).then_inc(ld["moe1"], 16)
                else:
                    sp.wait_ge(M[0]["up"], M[0].count("up", NJ))
                    sp.dma_start(b1bc, b1_1.rearrange("(a e) f -> a e f", a=1).to_broadcast([P, E, F1])).then_inc(ld["moe1"], 16)
                sp.wait_ge(m["sched"], m.count("sched", 1))
                for t in (NT - 2, NT - 1):
                    sp.wait_ge(sent[(t) % 2], sent_count(l, t))
                sp.wait_ge(filled[l], 16 * (SLOTS // P // 4))
                for j in range(NJ):
                    k = j % XB
                    if j >= XB:
                        sp.wait_ge(m["Tx"], m.count("Tx", j - XB + 1))
                    if j >= XB:
                        sp.wait_ge(m["back"], m.count("back", j - XB + 1))
                    r = sp.value_load(sched[l][0:1, 1, at(j)], min_val=0, max_val=SLOTS - P)
                    sp.dma_start(xs[k][:, :], rows[l][bass.ds(r, P), :]).then_inc(xs_in[k], 16)
                for j in range(NJ - XB, NJ):
                    sp.wait_ge(sentb[(j) % XB], sentb_count(l, j))
                for t in range(NT):
                    if t >= 4:
                        if l == 0:
                            sp.wait_ge(A[1]["comb"], A[1].count("comb", t - 3))
                        else:
                            sp.wait_ge(m["fin"], m.count("fin", t - 3))
                    sp.dma_start(yb[t % 4][:, :, :], y_v[l][t]).then_inc(y_in[t % 4], 16)
                    if l == 1 and t >= 1:
                        if t >= 1:
                            sp.wait_ge(m["fin"], m.count("fin", t))
                        sp.dma_start(out_v[:, t - 1, :], x[:, t - 1, :]).then_inc(stored, 16)
            sp.wait_ge(M[1]["fin"], M[1].count("fin", NT))
            sp.dma_start(out_v[:, NT - 1, :], x[:, NT - 1, :]).then_inc(stored, 16)
            sp.wait_ge(stored, 16 * NT)

        @block.gpsimd
        def _(pool):
            pool.memset(empty[:, :, 0:D], 0.0)
            pool.iota(empty[:, :, D:ROW].bitcast(I32), [[0, 4], [0, 1]], base=NOWHERE, channel_multiplier=0).then_inc(const, 1)
            pool.memset(ident[:, :], 0.0)
            pool.memset(mask16[:, :], 1.0)
            pool.memset(mask4[:, :], 1.0)
            pool.memset(headsel[:, :, :], 1.0)
            pool.memset(upper[:, :], 1.0)
            pool.memset(ones_b[:, :], 1.0)
            pool.memset(ones1[:, :], 1.0)
            pool.memset(mhalf[:, :], -0.5)
            pool.memset(pp[:, :, HK:HKP], 0.0)
            pool.iota(iota8i[:, :], [[1, E]], base=0, channel_multiplier=0)
            pool.iota(ebasei[:, :], [[REGION, E]], base=0, channel_multiplier=0)
            pool.iota(dest[:, :, :], [[2 * P, NT], [1, 2]], base=0, channel_multiplier=2)
            pool.iota(jidxi[:, :], [[1, NJ]], base=0, channel_multiplier=0).then_inc(const, 1)
            pool.wait_ge(const, 2)
            pool.affine_select(out=ident[:, :], in_=ident[:, :], compare_op=ALU.not_equal, fill=1.0,
                               base=0, pattern=[[-1, P]], channel_multiplier=1)
            pool.affine_select(out=upper[:, :], in_=upper[:, :], compare_op=ALU.is_gt, fill=0.0,
                               base=0, pattern=[[1, P]], channel_multiplier=-1)
            pool.affine_select(out=mask16[:, :], in_=mask16[:, :], compare_op=ALU.is_ge, fill=0.0,
                               base=0, pattern=[[-HD0, H]], channel_multiplier=1)
            pool.affine_select(out=mask4[:, :], in_=mask4[:, :], compare_op=ALU.is_ge, fill=0.0,
                               base=0, pattern=[[-4 * HD0, G]], channel_multiplier=1)
            pool.affine_select(out=headsel[:, :, :], in_=headsel[:, :, :], compare_op=ALU.is_ge, fill=0.0,
                               base=0, pattern=[[P, CH], [-KEYS, H]], channel_multiplier=1).then_inc(const, 1)
            pool.wait_ge(const, 3)
            pool.affine_select(out=mask16[:, :], in_=mask16[:, :], compare_op=ALU.is_ge, fill=0.0,
                               base=HD0 - 1, pattern=[[HD0, H]], channel_multiplier=-1)
            pool.affine_select(out=mask4[:, :], in_=mask4[:, :], compare_op=ALU.is_ge, fill=0.0,
                               base=4 * HD0 - 1, pattern=[[4 * HD0, G]], channel_multiplier=-1)
            pool.affine_select(out=headsel[:, :, :], in_=headsel[:, :, :], compare_op=ALU.is_ge, fill=0.0,
                               base=KEYS - 1, pattern=[[-P, CH], [KEYS, H]], channel_multiplier=-1)
            pool.tensor_copy(iota8[:, :], iota8i[:, :])
            pool.tensor_copy(ebase[:, :], ebasei[:, :])
            pool.tensor_copy(jidx[:, :], jidxi[:, :]).then_inc(const, 1)
            pool.wait_ge(const, NCONST)
            pool.wait_ge(ld["o"], 48)
            pool.wait_ge(pro["ksm"], pro.count("ksm", 1))
            pool.tensor_tensor(k0r[:, :], k0sm[:, :], mhalf[0:KEYS, :], ALU.pow).then_inc(pro["kr"], 1)
            pool.wait_ge(pro["kr"], pro.count("kr", 1))
            pool.wait_ge(pro["scl"], pro.count("scl", 1))
            pool.tensor_tensor(k0rs[:, :].rearrange("k (b h) -> k b h", b=NBATCH),
                               k0r[:, :].rearrange("k (b h) -> k b h", b=NBATCH),
                               scl[:, :].unsqueeze(1).to_broadcast([KEYS, NBATCH, H]), ALU.mult).then_inc(pro["krs"], 1)
            pool.wait_ge(pro["bhi"], pro.count("bhi", 1))
            for tt in range(TPB):
                pool.tensor_tensor(bias_r[:, 1, tt, :].rearrange("p (h k) -> p h k", k=KEYS),
                                   bias_sb[:, tt, :].unsqueeze(1).to_broadcast([P, G, KEYS]),
                                   bias_r[:, 0, tt, :].bitcast(F32).rearrange("p (h k) -> p h k", k=KEYS),
                                   ALU.subtract).then_inc(pro["blo"], 1)
            pool.wait_ge(pro["vT"], pro.count("vT", 1))
            pool.wait_ge(pro["keys0"], pro.count("keys0", NBATCH))
            for b in range(NBATCH):
                if b >= 2:
                    pool.wait_ge(pro["vtp"], pro.count("vtp", CH * (b - 1)))
                pool.tensor_tensor(vblk[b % 2][:, 0:HK].rearrange("p (h k) -> p h k", h=H),
                                   mask16[:, :].unsqueeze(2).to_broadcast([P, H, KEYS]),
                                   vT0[:, b * KEYS:(b + 1) * KEYS].unsqueeze(1).to_broadcast([P, H, KEYS]),
                                   ALU.mult).then_inc(pro["vblk"], 1)
            for b in range(NBATCH):
                pool.tensor_copy(vals0[:, b, :, :, HD0], headsel[:, :, :]).then_inc(pro["ones"], 1)

            def step(l, i):
                a = A[l]
                if 0 <= i < NT:
                    s = i % 2
                    pool.wait_ge(a["veA"], a.count("veA", i + 1))
                    pool.tensor_tensor(rsA[s], veA[s], mhalf[:, 0:1], ALU.pow).then_inc(a["rsA"], 1)
                t = i - 1
                if l == 0 and 0 <= t < NT:
                    pool.wait_ge(a["xnA"], a.count("xnA", t + 1))
                    pool.tensor_tensor(x[:, t, :], x[:, t, :], bo_bc[:, :], ALU.add).then_inc(pro["xbo"], 1)
                    s = t % 2
                    pool.wait_ge(a["qsm"], a.count("qsm", t + 1))
                    pool.tensor_tensor(qr[s], qsm[s], mhalf[:, 0:H], ALU.pow).then_inc(a["qr"], 1)
                    pool.wait_ge(a["qr"], a.count("qr", t + 1))
                    pool.tensor_tensor(qn[s].rearrange("p (h d) -> p h d", h=H), qb[s].rearrange("p (h d) -> p h d", h=H),
                                       qr[s].unsqueeze(2).to_broadcast([P, H, HD0]), ALU.mult).then_inc(a["qn"], 1)
                    pool.wait_ge(a["qn"], a.count("qn", t + 1))
                    if t >= 2:
                        pool.wait_ge(a["Tq"], a.count("Tq", t - 1))
                    qn3 = qn[s].rearrange("p (h d) -> p h d", h=H)
                    for w in range(2):
                        ins = pool.tensor_copy(qsplit[s][:, :, 0, w, :].bitcast(F32R), qn3)
                    ins.then_inc(a["qhi"], 1)
                    pool.wait_ge(a["qhi"], a.count("qhi", t + 1))
                    for w in range(2):
                        ins = pool.tensor_tensor(qsplit[s][:, :, 1, w, :], qn3, qsplit[s][:, :, 0, w, :], ALU.subtract)
                    ins.then_inc(a["qlo"], 1)
                t = i - 4
                if 0 <= t < NT:
                    s = t % 2
                    pool.wait_ge(a["veD"], a.count("veD", t + 1))
                    pool.tensor_tensor(rsD[s], veD[s], mhalf[:, 0:1], ALU.pow).then_inc(a["rsD"], 1)
                    if t >= 2:
                        pool.wait_ge(sent[(t - 2) % 2], sent_count(l, t - 2))
                    pool.tensor_copy(pay[s][:, :, D:ROW].bitcast(I32), dest[:, t, :].unsqueeze(2)).then_inc(a["ret"], 1)
                t = i - 2
                if l == 1 and 0 <= t < NT:
                    s = t % 2
                    pool.wait_ge(a["rden"], a.count("rden", t + 1))
                    p3 = prob[s][:, 0:HK].rearrange("p (h k) -> p h k", h=H)
                    pool.tensor_tensor(p3, p3, rden[s].unsqueeze(2).to_broadcast([P, H, KEYS]), ALU.mult).then_inc(a["norm"], 1)
                t = i - 5
                if 0 <= t < NT:
                    s = t % 2
                    if t == 0:
                        pool.wait_ge(filled[l], 16 * (SLOTS // P // 4))
                    pool.wait_ge(a["slot"], a.count("slot", t + 1))
                    pool.wait_ge(a["xnD"], a.count("xnD", t + 1))
                    pool.wait_ge(a["ret"], a.count("ret", t + 1))
                    for k in range(2):
                        pool.indirect_dma_start(rows[l][:, :], bass.IndirectOffsetOnAxis(slot[s][:, k:k + 1], 0),
                                                pay[s][:, k, :], None, bounds_check=SLOTS - 1,
                                                oob_is_err=False).then_inc(sent[s], 16)

            def moe(l):
                m = M[l]

                def send(j):
                    pool.wait_ge(m["y"], m.count("y", j + 1))
                    pool.wait_ge(m["back"], m.count("back", j + 1))
                    pool.indirect_dma_start(ys[l][:, :], bass.IndirectOffsetOnAxis(back[j % XB][:, 0:1], 0),
                                            ysb[j % 2], None, bounds_check=2 * T - 1,
                                            oob_is_err=False).then_inc(sentb[j % XB], 16)
                for j in range(NJ + 3):
                    if j < NJ:
                        pool.wait_ge(xs_in[j % XB], 16 * ((NJ // XB) * l + j // XB + 1))
                        if j >= XB:
                            pool.wait_ge(sentb[(j - XB) % XB], sentb_count(l, j - XB))
                        pool.tensor_copy(back[j % XB][:, :], xs[j % XB][:, D:ROW].bitcast(I32)).then_inc(m["back"], 1)
                    if j >= 3:
                        send(j - 3)

            for l in range(2):
                for i in range(NT + LAG):
                    step(l, i)
                if l == 0:
                    pool.wait_ge(pro1["cve"], pro1.count("cve", 1))
                    pool.tensor_tensor(crs[:, :], cve[:, :], mhalf[0:KEYS, 0:NBATCH], ALU.pow).then_inc(pro1["crs"], 1)
                moe(l)

        @block.scalar
        def _(act):
            act.dma_start(scl[:, :], scale_log.rearrange("a h b c -> a (h b c)").to_broadcast([KEYS, H])).then_inc(ld["q"], 16)
            act.dma_start(wq0[:, :], Wq0).then_inc(ld["q"], 16)
            act.dma_start(bq_bc[:, :], row_of(bq0, D)).then_inc(ld["q"], 16)
            act.dma_start(bias_sb[:, :, :], bias_in.rearrange("(t p) k -> p t k", p=P)).then_inc(ld["bias"], 16)
            act.dma_start(wo0[:, :], Wo0).then_inc(ld["o"], 16)
            act.dma_start(bo_bc[:, :], row_of(bo0, D)).then_inc(ld["o"], 16)
            act.dma_start(wr[0][:, :], Wr0).then_inc(ld["o"], 16)

            act.wait_ge(pro["ctxT"], pro.count("ctxT", 1))
            act.copy(ctxT[:, :], MD[:, 0:NBATCH * KEYS]).then_inc(pro["ctxTs"], 1)
            act.wait_ge(pro["k"], pro.count("k", 1))
            act.activation(k0sq, MC[0:KEYS, :], ACT.Square).then_inc(pro["ksq"], 1)
            act.wait_ge(pro["scm"], pro.count("scm", 1))
            act.activation(scl[:, :], scl[:, :], ACT.Exp).then_inc(pro["scl"], 1)
            act.wait_ge(pro["v"], pro.count("v", 1))
            act.copy(vT0[:, :], MA[:, 0:NBATCH * KEYS]).then_inc(pro["vT"], 1)
            act.wait_ge(ld["bias"], 16)
            for tt in range(TPB):
                ins = act.copy(bias_r[:, 0, tt, :].rearrange("p (h k) -> p h k", k=KEYS),
                               bias_sb[:, tt, :].unsqueeze(1).to_broadcast([P, G, KEYS]))
            ins.then_inc(pro["bhi"], 1)
            act.wait_ge(const, NCONST)
            act.copy(ident_r[:, :], ident[:, :]).then_inc(pro["identr"], 1)
            for n in range(NBATCH * 3):
                b, g = n // 3, n % 3
                w = min(4, CH - 4 * g)
                act.wait_ge(pro["vtp"], pro.count("vtp", b * CH + 4 * g + w))
                act.copy(vals0[:, b, 4 * g:4 * g + w, :, 0:HD0],
                         TP[n % 2][:, 0:w * P].rearrange("p (c h d) -> p c h d", c=w, h=H)).then_inc(pro["vals0"], 1)

            def step(l, i):
                a = A[l]
                t = i - 1
                if 0 <= t < NT:
                    s = t % 2
                    act.wait_ge(a["TxA"], a.count("TxA", t + 1))
                    if l == 0:
                        if t >= 2:
                            act.wait_ge(a["q"], a.count("q", t - 1))
                        act.copy(xT[s], MA[:, 0:P]).then_inc(a["xT"], 1)
                    else:
                        if t >= 2:
                            act.wait_ge(a["S"], a.count("S", t - 1))
                        if t >= 2:
                            act.wait_ge(a["ffh"], a.count("ffh", t - 1))
                        act.activation(xT[s], MA[:, 0:P], ACT.Identity, bias=gb[:, 1:2], scale=gb[:, 0:1]).then_inc(a["xT"], 1)
                u = i - 2
                if l == 1 and 0 <= u < NT:
                    act.wait_ge(a["Tg"], a.count("Tg", u + 1))
                    if u >= 2:
                        act.wait_ge(a["AV"], a.count("AV", u - 1))
                    act.copy(gT[u % 2], TP[1][:, :]).then_inc(a["gT"], 1)
                u = i - 3
                if 0 <= u < NT:
                    if u >= 2:
                        act.wait_ge(a["AV"], a.count("AV", u - 1))
                    for g in range(3):
                        w = min(4, CH - 4 * g)
                        act.wait_ge(a["TP"], a.count("TP", 3 * u + g + 1))
                        bank = (3 * u + g) % 2 if l == 0 else g % 2
                        act.copy(probT[u % 2][:, 4 * g * P:(4 * g + w) * P], TP[bank][:, 0:w * P]).then_inc(a["probT"], 1)
                if l == 0 and 0 <= t < NT:
                    act.wait_ge(a["qb"], a.count("qb", t + 1))
                    act.activation(qsq[t % 2], qb[t % 2], ACT.Square).then_inc(a["qsq"], 1)
                if l == 1 and 0 <= t < NT:
                    s = t % 2
                    act.wait_ge(a["ffg"], a.count("ffg", t + 1))
                    if t >= 2:
                        act.wait_ge(a["Tg"], a.count("Tg", t - 1))
                    act.activation(ffbuf[s], MA[:, :], ACT.Tanh, scale=0.5).then_inc(a["ffth"], 1)
                t = i - 2
                if 0 <= t < NT:
                    act.wait_ge(a["sub"], a.count("sub", t + 1))
                    act.activation(prob[t % 2][:, 0:HK], prob[t % 2][:, 0:HK], ACT.Exp).then_inc(a["exp"], 1)
                t = i - 1
                if l == 0 and 0 <= t < NT:
                    act.wait_ge(a["Tq"], a.count("Tq", t + 1))
                    if t >= 2:
                        act.wait_ge(a["S"], a.count("S", t - 1))
                    act.copy(qT[t % 2], MA[:, :]).then_inc(a["qT"], 1)
                t = i - 4
                if 0 <= t < NT:
                    act.wait_ge(a["Tx2"], a.count("Tx2", t + 1))
                    if t >= 2:
                        act.wait_ge(a["route"], a.count("route", t - 1))
                    act.copy(x2T[t % 2], MD[:, P:2 * P]).then_inc(a["x2T"], 1)
                t = i - 3
                if l == 0 and 0 <= t < NT:
                    act.wait_ge(a["To"], a.count("To", t + 1))
                    if t >= 2:
                        act.wait_ge(a["Wo"], a.count("Wo", t - 1))
                    act.copy(oT[t % 2], MC[:, 2 * P:3 * P]).then_inc(a["oT"], 1)

            def moe(l):
                m = M[l]

                for j in range(NJ + 3):
                    if j < NJ:
                        act.wait_ge(m["Tx"], m.count("Tx", j + 1))
                        if j >= 2:
                            act.wait_ge(m["up"], m.count("up", j - 1))
                        act.copy(xsT[j % 2], MA[:, 0:P]).then_inc(m["xsT"], 1)
                    t = j - 1
                    if 0 <= t < NJ:
                        s = t % 2
                        if l == 0:
                            act.wait_ge(m["up"], m.count("up", t + 1))
                            if t >= 2:
                                act.wait_ge(m["Th"], m.count("Th", t - 1))
                            act.activation(ha[s][:, 0:F0], S[s][:, 0:F0], ACT.Silu).then_inc(m["act1"], 1)
                        else:
                            act.wait_ge(m["act1"], m.count("act1", t + 1))
                            act.activation(ha[s], ha[s], ACT.Gelu_apprx_tanh).then_inc(m["act2"], 1)
                    t = j - 2
                    if 0 <= t < NJ:
                        s = t % 2
                        act.wait_ge(m["Th"], m.count("Th", t + 1))
                        if t >= 2:
                            act.wait_ge(m["down"], m.count("down", t - 1))
                        w = F0 if l == 0 else F1
                        act.copy(hT[s][:, 0:w], TP[s][:, 0:w]).then_inc(m["hT"], 1)

            for l in range(2):
                if l == 1:
                    act.wait_ge(ld["l1b"], 16 * 4)
                for i in range(NT + LAG):
                    step(l, i)
                act.wait_ge(A[l]["margin"], A[l].count("margin", NT))
                act.activation(gtmp[:, 0, :], margin[:, :], ACT.Exp).then_inc(M[l]["g1"], 1)
                if l == 0:
                    act.wait_ge(ld["l1"], 16 * 10)
                    act.wait_ge(pro1["cT"], pro1.count("cT", 1))
                    act.activation(ctxT[:, :], MD[:, 0:NBATCH * KEYS], ACT.Identity, bias=gb[:, 3:4], scale=gb[:, 2:3]).then_inc(pro1["cTs"], 1)
                    act.wait_ge(pro1["kv1"], pro1.count("kv1", 1))
                    act.activation(kT1[:, :], MA[:, 0:NBATCH * KEYS], ACT.Copy, scale=float(HD1) ** -0.5).then_inc(pro1["kT1"], 1)
                    act.wait_ge(pro1["kv1"], pro1.count("kv1", 2))
                    act.copy(vT1[:, :], MC[:, 0:NBATCH * KEYS]).then_inc(pro1["vT1"], 1)
                    for g in range(2):
                        act.wait_ge(pro1["wqT"], pro1.count("wqT", g + 1))
                        act.copy(wq1T[:, 4 * g:4 * g + 4, :], TP[g][:, :].rearrange("p (k c) -> p k c", k=4)).then_inc(pro1["wqTs"], 1)
                    for h in range(H):
                        act.wait_ge(pro1["fk"], pro1.count("fk", h + 1))
                        act.copy(keys1[:, :, h * KEYS:(h + 1) * KEYS],
                                 S[h % 2][:, 0:NBATCH * KEYS].rearrange("p (b k) -> p b k", b=NBATCH)).then_inc(pro1["keys1"], 1)
                    for n in range(NBATCH * 3):
                        b, g = n // 3, n % 3
                        w = min(4, CH - 4 * g)
                        act.wait_ge(pro1["fT"], pro1.count("fT", n + 1))
                        act.copy(vals1[:, b, 4 * g:4 * g + w, :],
                                 TP[n % 2][:, 0:w * P].rearrange("p (c d) -> p c d", c=w)).then_inc(pro1["vals1"], 1)
                moe(l)

        @block.vector
        def _(dve):
            dve.wait_ge(ld["q"], 48)
            dve.tensor_scalar(scl[:, :], scl[:, :], MAX_LOG_SCALE, None, ALU.min).then_inc(pro["scm"], 1)
            dve.wait_ge(pro["ksq"], pro.count("ksq", 1))
            dve.reduce_sum(k0ss[:, :], k0sq.rearrange("k (r d) -> k r d", d=HD0), AX).then_inc(pro["kss"], 1)
            dve.wait_ge(pro["kss"], pro.count("kss", 1))
            dve.tensor_scalar(k0sm[:, :], k0ss[:, :], NORM_FLOOR, None, ALU.max).then_inc(pro["ksm"], 1)
            dve.wait_ge(pro["krs"], pro.count("krs", 1))
            dve.tensor_tensor(k0n.rearrange("k (r d) -> k r d", d=HD0), MC[0:KEYS, :].rearrange("k (r d) -> k r d", d=HD0),
                              k0rs[:, :].unsqueeze(2).to_broadcast([KEYS, NBATCH * H, HD0]), ALU.mult).then_inc(pro["kn"], 1)
            dve.wait_ge(pro["kn"], pro.count("kn", 1))
            for half in range(2):
                src = k0n[:, half * 256:half * 256 + 256].rearrange("k (r d) -> k r d", d=HD0)
                for s2 in range(2):
                    ins = dve.tensor_copy(k0split[:, half, :, s2, 0, :].bitcast(F32R), src)
            ins.then_inc(pro["khi"], 1)
            dve.wait_ge(pro["khi"], pro.count("khi", 1))
            for half in range(2):
                src = k0n[:, half * 256:half * 256 + 256].rearrange("k (r d) -> k r d", d=HD0)
                for s2 in range(2):
                    ins = dve.tensor_tensor(k0split[:, half, :, s2, 1, :], src, k0split[:, half, :, s2, 0, :], ALU.subtract)
            ins.then_inc(pro["klo"], 1)
            dve.wait_ge(const, NCONST)
            for b in range(NBATCH):
                dve.wait_ge(pro["kT"], pro.count("kT", b + 1))
                src = (S + [TP[0]])[b]
                for g in range(NG):
                    ins = dve.tensor_tensor(keys0[:, b, g * GK:(g + 1) * GK].rearrange("p (h k) -> p h k", h=G),
                                      src[:, g * KEYS:(g + 1) * KEYS].unsqueeze(1).to_broadcast([P, G, KEYS]),
                                      mask4[:, :].unsqueeze(2).to_broadcast([P, G, KEYS]),
                                      ALU.mult)
                ins.then_inc(pro["keys0"], 1)

            dve.wait_ge(ld["x"], 16)
            dve.wait_ge(ld["o"], 48)

            def step(l, i):
                a = A[l]
                t = i - 5
                if 0 <= t < NT:
                    s = t % 2
                    dve.wait_ge(a["rank"], a.count("rank", t + 1))
                    dve.tensor_tensor(rank[s], MD[:, 2 * P + E:2 * P + 2 * E], ebase[:, :], ALU.add).then_inc(a["rankb"], 1)
                    dve.wait_ge(a["rankb"], a.count("rankb", t + 1))
                    dve.tensor_tensor(rsel[s], oh[s], rank[s].unsqueeze(1).to_broadcast([P, 2, E]), ALU.mult).then_inc(a["rsel"], 1)
                    dve.wait_ge(a["rsel"], a.count("rsel", t + 1))
                    dve.reduce_sum(slotf[s], rsel[s], AX).then_inc(a["slotf"], 1)
                    dve.wait_ge(a["slotf"], a.count("slotf", t + 1))
                    if t >= 2:
                        dve.wait_ge(sent[(t - 2) % 2], sent_count(l, t - 2))
                    dve.tensor_copy(slot[s], slotf[s]).then_inc(a["slot"], 1)
                if 0 <= i < NT:
                    s = i % 2
                    if l == 1:
                        dve.wait_ge(y_in[i % 4], 16 * (i // 4 + 1))
                        dve.scalar_tensor_tensor(yb[i % 4][:, 0, :], yb[i % 4][:, 0, :], gate[:, 0, i:i + 1], x[:, i, :], ALU.mult, ALU.add).then_inc(a["comb1"], 1)
                        dve.wait_ge(a["comb1"], a.count("comb1", i + 1))
                        dve.scalar_tensor_tensor(x[:, i, :], yb[i % 4][:, 1, :], gate[:, 1, i:i + 1], yb[i % 4][:, 0, :], ALU.mult, ALU.add).then_inc(a["comb"], 1)
                        dve.wait_ge(a["comb"], a.count("comb", i + 1))
                    dve.bn_stats(stA[s], x[:, i, :]).then_inc(a["bnA"], 1)
                    dve.wait_ge(a["bnA"], a.count("bnA", i + 1))
                    dve.bn_aggr(mvA[s], stA[s]).then_inc(a["mvA"], 1)
                    dve.wait_ge(a["mvA"], a.count("mvA", i + 1))
                    c1, c0 = (1.0, EPS) if l == 0 else (1.0 + EPS, EPS * EPS)
                    dve.tensor_scalar(veA[s], mvA[s][:, 1:2], c1, c0, ALU.mult, ALU.add).then_inc(a["veA"], 1)
                t = i - 1
                if l == 0 and 0 <= t < NT:
                    s = t % 2
                    dve.wait_ge(a["q"], a.count("q", t + 1))
                    dve.tensor_tensor(qb[s], MA[:, P:2 * P], bq_bc[:, :], ALU.add).then_inc(a["qb"], 1)
                if l == 1 and 0 <= t < NT:
                    s = t % 2
                    dve.wait_ge(a["ffth"], a.count("ffth", t + 1))
                    dve.scalar_tensor_tensor(ffbuf[s], ffbuf[s], 1.0, MA[:, :], ALU.add, ALU.mult).then_inc(a["ffgg"], 1)
                t = i - 2
                if 0 <= t < NT:
                    s = t % 2
                    dve.wait_ge(a["S"], a.count("S", t + 1))
                    for n, h in zip(BANK_HEADS, BANK_AT):
                        ins = dve.reduce_max(mx[s][:, h:h + n], S[BANK_AT.index(h)][:, 0:n * KEYS].rearrange("p (h k) -> p h k", k=KEYS), AX)
                    ins.then_inc(a["mx"], 1)
                t = i - 1
                if l == 0 and 0 <= t < NT:
                    s = t % 2
                    dve.wait_ge(a["qsq"], a.count("qsq", t + 1))
                    dve.reduce_sum(qss[s], qsq[s].rearrange("p (h d) -> p h d", h=H), AX).then_inc(a["qss"], 1)
                    dve.wait_ge(a["qss"], a.count("qss", t + 1))
                    dve.tensor_scalar(qsm[s], qss[s], NORM_FLOOR, None, ALU.max).then_inc(a["qsm"], 1)
                t = i - 2
                if 0 <= t < NT:
                    s = t % 2
                    dve.wait_ge(a["mx"], a.count("mx", t + 1))
                    if t >= 2:
                        dve.wait_ge(a["TP"], a.count("TP", 3 * (t - 1)))
                    for k, (n, h) in enumerate(zip(BANK_HEADS, BANK_AT)):
                        ins = dve.tensor_tensor(prob[s][:, h * KEYS:(h + n) * KEYS].rearrange("p (h k) -> p h k", k=KEYS),
                                                S[k][:, 0:n * KEYS].rearrange("p (h k) -> p h k", k=KEYS),
                                                mx[s][:, h:h + n].unsqueeze(2).to_broadcast([P, n, KEYS]), ALU.subtract)
                    ins.then_inc(a["sub"], 1)
                if 0 <= i < NT:
                    s = i % 2
                    dve.wait_ge(a["rsA"], a.count("rsA", i + 1))
                    if i >= 2:
                        dve.wait_ge(a["TxA"], a.count("TxA", i - 1))
                    dve.tensor_scalar(xnA[s], x[:, i, :], mvA[s][:, 0:1], rsA[s], ALU.subtract, ALU.mult).then_inc(a["xnA"], 1)
                t = i - 4
                if 0 <= t < NT:
                    s = t % 2
                    src = MD if l == 0 else MC
                    if l == 0:
                        dve.wait_ge(a["Wo"], a.count("Wo", t + 1))
                        dve.wait_ge(pro["xbo"], pro.count("xbo", t + 1))
                    else:
                        dve.wait_ge(a["AV"], a.count("AV", t + 1))
                    dve.tensor_tensor(x[:, t, :], x[:, t, :], src[:, 0:D], ALU.add).then_inc(a["xa"], 1)
                    dve.wait_ge(a["xa"], a.count("xa", t + 1))
                    dve.bn_stats(stD[s], x[:, t, :]).then_inc(a["bnD"], 1)
                    dve.wait_ge(a["bnD"], a.count("bnD", t + 1))
                    dve.bn_aggr(mvD[s], stD[s]).then_inc(a["mvD"], 1)
                    dve.wait_ge(a["mvD"], a.count("mvD", t + 1))
                    dve.tensor_scalar(veD[s], mvD[s][:, 1:2], EPS, None, ALU.add).then_inc(a["veD"], 1)
                t = i - 1
                if l == 1 and 0 <= t < NT:
                    s = t % 2
                    dve.wait_ge(a["ffh"], a.count("ffh", t + 1))
                    dve.scalar_tensor_tensor(ffbuf[s], ffbuf[s], 0.5, MA[:, :], ALU.mult, ALU.mult).then_inc(a["ffo"], 1)
                t = i - 4
                if 0 <= t < NT:
                    s = t % 2
                    dve.wait_ge(a["rsD"], a.count("rsD", t + 1))
                    if t >= 2:
                        dve.wait_ge(sent[(t - 2) % 2], sent_count(l, t - 2))
                    dve.tensor_scalar(pay[s][:, :, 0:D], x[:, t, :].unsqueeze(1).to_broadcast([P, 2, D]),
                                      mvD[s][:, 0:1], rsD[s], ALU.subtract, ALU.mult).then_inc(a["xnD"], 1)
                t = i - 2
                if l == 1 and 0 <= t < NT:
                    s = t % 2
                    dve.wait_ge(a["exp"], a.count("exp", t + 1))
                    dve.reduce_sum(den[s], prob[s][:, 0:HK].rearrange("p (h k) -> p h k", h=H), AX).then_inc(a["den"], 1)
                    dve.wait_ge(a["den"], a.count("den", t + 1))
                    dve.reciprocal(rden[s], den[s]).then_inc(a["rden"], 1)
                t = i - 3
                if l == 0 and 0 <= t < NT:
                    s = t % 2
                    dve.wait_ge(a["AV"], a.count("AV", t + 1))
                    av = MC[:, 0:H * VW].rearrange("p (h v) -> p h v", h=H)
                    dve.reciprocal(rden[s], av[:, :, HD0]).then_inc(a["rden"], 1)
                    dve.wait_ge(a["rden"], a.count("rden", t + 1))
                    dve.tensor_tensor(on[s].rearrange("p (h d) -> p h d", h=H), av[:, :, 0:HD0],
                                      rden[s].unsqueeze(2).to_broadcast([P, H, HD0]), ALU.mult).then_inc(a["on"], 1)
                t = i - 4
                if 0 <= t < NT:
                    s = t % 2
                    dve.wait_ge(a["route"], a.count("route", t + 1))
                    if l == 0:
                        dve.tensor_copy(scr[s], MD[:, 2 * P:2 * P + E]).then_inc(a["scr"], 1)
                    else:
                        dve.tensor_tensor(scr[s], MD[:, 2 * P:2 * P + E], br_bc[:, :], ALU.add).then_inc(a["scr"], 1)
                    dve.wait_ge(a["scr"], a.count("scr", t + 1))
                    dve.max(top[s], scr[s]).then_inc(a["top"], 1)
                    dve.wait_ge(a["top"], a.count("top", t + 1))
                    dve.max_index(topi[s], top[s], scr[s]).then_inc(a["topi"], 1)
                    dve.tensor_tensor(margin[:, at(t)], top[s][:, 1:2], top[s][:, 0:1], ALU.subtract).then_inc(a["margin"], 1)
                    dve.wait_ge(a["topi"], a.count("topi", t + 1))
                    dve.tensor_tensor(oh[s], iota8[:, :].unsqueeze(1).to_broadcast([P, 2, E]),
                                      topi[s][:, 0:2].unsqueeze(2).to_broadcast([P, 2, E]), ALU.is_equal).then_inc(a["oh"], 1)
                    if t == 0:
                        dve.memset(before[s], 0.0).then_inc(a["before"], 1)
                    else:
                        if t == 1:
                            dve.wait_ge(a["before"], a.count("before", 1))
                        if t >= 1:
                            dve.wait_ge(a["picks"], a.count("picks", t))
                        dve.tensor_tensor(before[s], before[1 - s], picks[1 - s], ALU.add).then_inc(a["before"], 1)
                    dve.wait_ge(a["oh"], a.count("oh", t + 1))
                    dve.tensor_tensor(picks[s], oh[s][:, 0, :], oh[s][:, 1, :], ALU.add).then_inc(a["picks"], 1)
                    dve.wait_ge(a["before"], a.count("before", t + 1))

            def schedule(l):
                m = M[l]
                dve.wait_ge(m["cnt"], m.count("cnt", 1))
                dve.tensor_scalar(cnt_i[:, :], MD[0:1, 2 * P + E:2 * P + 2 * E], float(P - 1), None, ALU.add).then_inc(m["plan"], 1)
                dve.wait_ge(m["plan"], m.count("plan", 1))
                dve.tensor_scalar(cnt_s[:, :], cnt_i[:, :], 7, None, ALU.arith_shift_right).then_inc(m["plan"], 1)
                dve.wait_ge(m["plan"], m.count("plan", 2))
                dve.tensor_copy(ntile[:, :], cnt_s[:, :]).then_inc(m["plan"], 1)
                dve.wait_ge(m["plan"], m.count("plan", 3))
                dve.tensor_scalar(wgt[:, :], ntile[:, :], -float(P), float(REGION), ALU.mult, ALU.add).then_inc(m["plan"], 1)
                dve.tensor_tensor_scan(cum[:, :], ones1[:, :], ntile[:, :], 0.0, ALU.mult, ALU.add).then_inc(m["plan"], 1)
                dve.wait_ge(m["plan"], m.count("plan", 5))
                dve.tensor_tensor(ind[:, :, :], jidx[:, :].unsqueeze(2).to_broadcast([1, NJ, E - 1]),
                                  cum[:, 0:E - 1].unsqueeze(1).to_broadcast([1, NJ, E - 1]), ALU.is_ge).then_inc(m["plan"], 1)
                dve.wait_ge(m["plan"], m.count("plan", 6))
                dve.reduce_sum(ef[:, :], ind[:, :, :], AX)
                dve.tensor_tensor(ind2[:, :, :], ind[:, :, :], wgt[:, 0:E - 1].unsqueeze(1).to_broadcast([1, NJ, E - 1]), ALU.mult).then_inc(m["plan"], 1)
                dve.wait_ge(m["plan"], m.count("plan", 7))
                dve.reduce_sum(rf[:, :], ind2[:, :, :], AX).then_inc(m["plan"], 1)
                dve.wait_ge(m["plan"], m.count("plan", 8))
                dve.scalar_tensor_tensor(rf2[:, :], jidx[:, :], float(P), rf[:, :], ALU.mult, ALU.add).then_inc(m["plan"], 1)
                dve.wait_ge(m["plan"], m.count("plan", 9))
                dve.tensor_copy(sched[l][:, 0, :], ef[:, :])
                dve.tensor_copy(sched[l][:, 1, :], rf2[:, :]).then_inc(m["sched"], 1)
                dve.wait_ge(m["g1"], m.count("g1", 1))
                dve.tensor_scalar(gtmp[:, 1, :], gtmp[:, 0, :], 1.0, None, ALU.add).then_inc(m["gates"], 1)
                dve.wait_ge(m["gates"], m.count("gates", 1))
                dve.reciprocal(gate[:, 0, :], gtmp[:, 1, :]).then_inc(m["gates"], 1)
                dve.wait_ge(m["gates"], m.count("gates", 2))
                dve.tensor_tensor(gate[:, 1, :], gtmp[:, 0, :], gate[:, 0, :], ALU.mult).then_inc(m["gates"], 1)

            def moe(l):
                m = M[l]
                for j in range(NJ + 3):
                    t = j - 1
                    if 0 <= t < NJ:
                        s = t % 2
                        if l == 0:
                            dve.wait_ge(m["act1"], m.count("act1", t + 1))
                            dve.tensor_tensor(ha[s][:, 0:F0], ha[s][:, 0:F0], S[s][:, F0:2 * F0], ALU.mult).then_inc(m["act2"], 1)
                        else:
                            if t == 0:
                                dve.wait_ge(ld["moe1"], 64)
                            dve.wait_ge(m["up"], m.count("up", t + 1))
                            if t >= 2:
                                dve.wait_ge(m["Th"], m.count("Th", t - 1))
                            e = dve.value_load(sched[l][0:1, 0, at(t)], min_val=0, max_val=E - 1)
                            dve.tensor_tensor(ha[s], S[s][:, :], b1bc[:, e, :], ALU.add).then_inc(m["act1"], 1)
                    t = j - 3
                    if 0 <= t < NJ:
                        s = t % 2
                        dve.wait_ge(m["down"], m.count("down", t + 1))
                        if t >= 2:
                            dve.wait_ge(sentb[(t - 2) % XB], sentb_count(l, t - 2))
                        src = (MC, MD)[s][:, 0:D]
                        if l == 0:
                            dve.tensor_copy(ysb[s], src).then_inc(m["y"], 1)
                        else:
                            e = dve.value_load(sched[l][0:1, 0, at(t)], min_val=0, max_val=E - 1)
                            dve.tensor_tensor(ysb[s], src, b2bc[:, e, :], ALU.add).then_inc(m["y"], 1)

            for l in range(2):
                if l == 1:
                    dve.wait_ge(M[0]["gates"], M[0].count("gates", 3))
                    dve.wait_ge(ld["l1b"], 16 * 4)
                for i in range(NT + LAG):
                    step(l, i)
                schedule(l)
                if l == 0:
                    for b in range(NBATCH):
                        dve.bn_stats(cstat[:, b, :], ctx_sb[:, b, :]).then_inc(pro1["cbn"], 1)
                    for b in range(NBATCH):
                        dve.wait_ge(pro1["cbn"], pro1.count("cbn", b + 1))
                        dve.bn_aggr(cmv[:, b, :], cstat[:, b, :]).then_inc(pro1["cmv"], 1)
                    dve.wait_ge(pro1["cmv"], pro1.count("cmv", NBATCH))
                    dve.tensor_scalar(cve[:, :], cmv[:, :, 1], EPS, None, ALU.add).then_inc(pro1["cve"], 1)
                    dve.wait_ge(pro1["crs"], pro1.count("crs", 1))
                    for b in range(NBATCH):
                        dve.tensor_scalar(cn[:, b, :], ctx_sb[:, b, :], cmv[:, b, 0:1], crs[:, b:b + 1],
                                          ALU.subtract, ALU.mult).then_inc(pro1["cn"], 1)
                    dve.wait_ge(A[0]["AV"], A[0].count("AV", NT))
                    for h in range(H):
                        dve.wait_ge(pro1["fv"], pro1.count("fv", h + 1))
                        dve.tensor_copy(pp[:, :, h * KEYS:(h + 1) * KEYS],
                                        (S[2], MD)[h % 2][:, 0:NBATCH * KEYS].rearrange("p (b k) -> p b k", b=NBATCH)).then_inc(pro1["foldT"], 1)
                moe(l)
            m = M[1]
            dve.wait_ge(m["gates"], m.count("gates", 3))
            for t in range(NT):
                dve.wait_ge(y_in[t % 4], 16 * (NT // 4 + t // 4 + 1))
                dve.scalar_tensor_tensor(yb[t % 4][:, 0, :], yb[t % 4][:, 0, :], gate[:, 0, t:t + 1], x[:, t, :], ALU.mult, ALU.add).then_inc(m["fin0"], 1)
                dve.wait_ge(m["fin0"], m.count("fin0", t + 1))
                dve.scalar_tensor_tensor(x[:, t, :], yb[t % 4][:, 1, :], gate[:, 1, t:t + 1], yb[t % 4][:, 0, :], ALU.mult, ALU.add).then_inc(m["fin"], 1)

        @block.tensor
        def _(pe):
            mm = nc.tensor.matmul
            tr = nc.tensor.transpose
            pe.wait_ge(const, NCONST)
            pe.wait_ge(ld["ctx"], 48)
            for b in range(NBATCH):
                ins = tr(MD[:, b * KEYS:(b + 1) * KEYS], ctx_sb[:, b, :], ident[0:KEYS, 0:KEYS])
            ins.then_inc(pro["ctxT"], 1)
            pe.wait_ge(pro["ctxTs"], pro.count("ctxTs", 1))
            for b in range(NBATCH):
                ins = mm(MC[0:KEYS, b * D:(b + 1) * D], ctxT[:, b * KEYS:(b + 1) * KEYS], wk0[:, :], start=True, stop=True)
            ins.then_inc(pro["k"], 1)
            mm(MA[:, 0:NBATCH * KEYS], wv0[:, :], ctxT[:, :], start=True, stop=True).then_inc(pro["v"], 1)
            pe.wait_ge(pro["klo"], pro.count("klo", 1))
            for b in range(NBATCH):
                dst = (S + [TP[0]])[b]
                for g in range(NG):
                    n = b * NG + g
                    src = k0split[:, n // 8].rearrange("k r s w d -> k (r s w d)")[:, (n % 8) * P:(n % 8 + 1) * P]
                    ins = tr(dst[:, g * KEYS:(g + 1) * KEYS], src, ident[0:KEYS, 0:KEYS])
                ins.then_inc(pro["kT"], 1)
            pe.wait_ge(pro["keys0"], pro.count("keys0", NBATCH))
            for n in range(NBATCH * 3):
                b, g = n // 3, n % 3
                pe.wait_ge(pro["vblk"], pro.count("vblk", b + 1))
                if n >= 2:
                    pe.wait_ge(pro["vals0"], pro.count("vals0", n - 1))
                for c in range(4 * g, min(4 * g + 4, CH)):
                    tr(TP[n % 2][:, (c - 4 * g) * P:(c - 4 * g + 1) * P], vblk[b % 2][:, c * P:(c + 1) * P], ident[:, :]).then_inc(pro["vtp"], 1)
            pe.wait_ge(ld["q"], 48)
            pe.wait_ge(ld["o"], 48)
            pe.wait_ge(pro["identr"], pro.count("identr", 1))
            pe.wait_ge(pro["blo"], pro.count("blo", TPB))

            def step(l, i):
                a = A[l]
                t = i - 1
                if 0 <= t < NT:
                    pe.wait_ge(a["xnA"], a.count("xnA", t + 1))
                    if t >= 1:
                        pe.wait_ge(a["qT" if l == 0 else "ffo"], a.count("qT" if l == 0 else "ffo", t))
                    if l == 0 and t == 0:
                        pe.wait_ge(pro["vT"], pro.count("vT", 1))
                    tr(MA[:, 0:P], xnA[t % 2], ident[:, :]).then_inc(a["TxA"], 1)
                t = i - 5
                if 0 <= t < NT:
                    s = t % 2
                    pe.wait_ge(a["picks"], a.count("picks", t + 1))
                    pe.wait_ge(a["before"], a.count("before", t + 1))
                    mm(MD[:, 2 * P + E:2 * P + 2 * E], upper[:, :], picks[s], start=True, stop=False)
                    mm(MD[:, 2 * P + E:2 * P + 2 * E], ones_b[:, :], before[s], start=False, stop=True).then_inc(a["rank"], 1)
                t = i - 2
                if 0 <= t < NT:
                    s, b = t % 2, t // TPB
                    pe.wait_ge(a["qT" if l == 0 else "xT"], a.count("qT" if l == 0 else "xT", t + 1))
                    if t >= 1:
                        pe.wait_ge(a["sub"], a.count("sub", t))
                    if l == 0:
                        if t == 0:
                            pe.wait_ge(pro["vals0"], pro.count("vals0", 3 * NBATCH))
                        tt = t % TPB
                        for k, n in enumerate(BANK_HEADS):
                            for half in range(2):
                                for o in range(0, n * KEYS, GK):
                                    w = min(GK, n * KEYS - o)
                                    mm(S[k][:, o:o + w], ident_r[:, :], bias_r[:, half, tt, 0:w], start=half == 0 and o == 0, stop=False)
                            h = BANK_AT[k]
                            while h < BANK_AT[k] + n:
                                g = h // G
                                e_ = min((g + 1) * G, BANK_AT[k] + n)
                                o = (h - BANK_AT[k]) * KEYS
                                ins = mm(S[k][:, o:o + (e_ - h) * KEYS], qT[s][:, g * P:(g + 1) * P],
                                         keys0[:, b, h * KEYS:e_ * KEYS], start=False, stop=e_ == BANK_AT[k] + n)
                                h = e_
                        ins.then_inc(a["S"], 1)
                    else:
                        for k, n in enumerate(BANK_HEADS):
                            h = BANK_AT[k]
                            ins = mm(S[k][:, 0:n * KEYS], xT[s], keys1[:, b, h * KEYS:(h + n) * KEYS], start=True, stop=True)
                        ins.then_inc(a["S"], 1)
                t = i - 1
                if 0 <= t < NT:
                    s = t % 2
                    pe.wait_ge(a["xT"], a.count("xT", t + 1))
                    if l == 0:
                        mm(MA[:, P:2 * P], xT[s], wq0[:, :], start=True, stop=True).then_inc(a["q"], 1)
                    else:
                        mm(MA[:, :], xT[s], wff1[:, FF:2 * FF], start=True, stop=True).then_inc(a["ffg"], 1)
                t = i - 2
                if l == 1 and 0 <= t < NT:
                    pe.wait_ge(a["ffo"], a.count("ffo", t + 1))
                    if t >= 2:
                        pe.wait_ge(a["probT"], a.count("probT", 3 * (t - 1) - 1))
                    for k in range(FF // P):
                        ins = tr(TP[1][:, k * P:(k + 1) * P], ffbuf[t % 2][:, k * P:(k + 1) * P], ident[:, :])
                    ins.then_inc(a["Tg"], 1)
                t = i - 3
                if 0 <= t < NT:
                    s = t % 2
                    pe.wait_ge(a["exp" if l == 0 else "norm"], a.count("exp" if l == 0 else "norm", t + 1))
                    for g in range(3):
                        if l == 0:
                            bank = (3 * t + g) % 2
                            if 3 * t + g >= 2:
                                pe.wait_ge(a["probT"], a.count("probT", 3 * t + g - 1))
                        else:
                            bank = g % 2
                            if g == 0:
                                if t >= 1:
                                    pe.wait_ge(a["probT"], a.count("probT", 3 * t))
                            if g == 1:
                                pe.wait_ge(a["gT"], a.count("gT", min(t + 2, NT)))
                            if g == 2:
                                pe.wait_ge(a["probT"], a.count("probT", 3 * t + 1))
                        for c in range(4 * g, min(4 * g + 4, CH)):
                            ins = tr(TP[bank][:, (c - 4 * g) * P:(c - 4 * g + 1) * P], prob[s][:, c * P:(c + 1) * P], ident[:, :])
                        ins.then_inc(a["TP"], 1)
                t = i - 1
                if l == 1 and 0 <= t < NT:
                    s = t % 2
                    pe.wait_ge(a["ffgg"], a.count("ffgg", t + 1))
                    mm(MA[:, :], xT[s], wff1[:, 0:FF], start=True, stop=True).then_inc(a["ffh"], 1)
                t = i - 4
                if l == 0 and 0 <= t < NT:
                    pe.wait_ge(a["oT"], a.count("oT", t + 1))
                    if t >= 1:
                        pe.wait_ge(a["rankb"], a.count("rankb", t))
                    mm(MD[:, 0:D], oT[t % 2], wo0[:, :], start=True, stop=True).then_inc(a["Wo"], 1)
                t = i - 3
                if 0 <= t < NT:
                    s, b = t % 2, t // TPB
                    pe.wait_ge(a["probT"], a.count("probT", 3 * t + 3))
                    if t >= 1:
                        pe.wait_ge(a["oT" if l == 0 else "xa"], a.count("oT" if l == 0 else "xa", t))
                    if l == 0:
                        if t == 0:
                            pe.wait_ge(pro["ones"], pro.count("ones", NBATCH))
                        for c in range(CH):
                            ins = mm(MC[:, 0:H * VW], probT[s][:, c * P:(c + 1) * P],
                                     vals0[:, b, c, :, :].rearrange("p h v -> p (h v)"), start=c == 0, stop=c == CH - 1)
                    else:
                        for c in range(CH):
                            mm(MC[:, 0:D], probT[s][:, c * P:(c + 1) * P], vals1[:, b, c, :], start=c == 0, stop=False)
                        pe.wait_ge(a["gT"], a.count("gT", t + 1))
                        for k in range(FF // P):
                            ins = mm(MC[:, 0:D], gT[s][:, k * P:(k + 1) * P], wff2[:, k, :], start=False, stop=k == FF // P - 1)
                    ins.then_inc(a["AV"], 1)
                t = i - 1
                if l == 0 and 0 <= t < NT:
                    s = t % 2
                    pe.wait_ge(a["qlo"], a.count("qlo", t + 1))
                    src = qsplit[s].rearrange("p h a b d -> p (h a b d)")
                    for g in range(NG):
                        ins = tr(MA[:, g * P:(g + 1) * P], src[:, g * P:(g + 1) * P], ident[:, :])
                    ins.then_inc(a["Tq"], 1)
                t = i - 4
                if 0 <= t < NT:
                    pe.wait_ge(a["xnD"], a.count("xnD", t + 1))
                    if l == 1:
                        if t >= 1:
                            pe.wait_ge(a["rankb"], a.count("rankb", t))
                    tr(MD[:, P:2 * P], pay[t % 2][:, 0, 0:D], ident[:, :]).then_inc(a["Tx2"], 1)
                t = i - 3
                if l == 0 and 0 <= t < NT:
                    pe.wait_ge(a["on"], a.count("on", t + 1))
                    tr(MC[:, 2 * P:3 * P], on[t % 2], ident[:, :]).then_inc(a["To"], 1)
                t = i - 4
                if 0 <= t < NT:
                    pe.wait_ge(a["x2T"], a.count("x2T", t + 1))
                    mm(MD[:, 2 * P:2 * P + E], x2T[t % 2], wr[l][:, :], start=True, stop=True).then_inc(a["route"], 1)

            def moe(l):
                m = M[l]
                up = w13 if l == 0 else w1b
                w2 = w2a if l == 0 else w2b
                nk = (F0 if l == 0 else F1) // P
                if l == 0:
                    pe.wait_ge(ld["moe0"], 48)
                else:
                    pe.wait_ge(ld["moe1"], 64)
                pe.wait_ge(m["sched"], m.count("sched", 1))
                for j in range(NJ + 3):
                    if j < NJ:
                        pe.wait_ge(xs_in[j % XB], 16 * ((NJ // XB) * l + j // XB + 1))
                        if j >= 1:
                            pe.wait_ge(m["xsT"], m.count("xsT", j))
                        tr(MA[:, 0:P], xs[j % XB][:, 0:D], ident[:, :]).then_inc(m["Tx"], 1)
                    t = j - 1
                    if 0 <= t < NJ:
                        s = t % 2
                        e = pe.value_load(sched[l][0:1, 0, at(t)], min_val=0, max_val=E - 1)
                        pe.wait_ge(m["xsT"], m.count("xsT", t + 1))
                        if t >= 2:
                            pe.wait_ge(m["act2" if l == 0 else "act1"], m.count("act2" if l == 0 else "act1", t - 1))
                        mm(S[s][:, :], xsT[s], up[:, e, :], start=True, stop=True).then_inc(m["up"], 1)
                    t = j - 3
                    if 0 <= t < NJ:
                        s = t % 2
                        e = pe.value_load(sched[l][0:1, 0, at(t)], min_val=0, max_val=E - 1)
                        pe.wait_ge(m["hT"], m.count("hT", t + 1))
                        if t >= 2:
                            pe.wait_ge(m["y"], m.count("y", t - 1))
                        for k in range(nk):
                            ins = mm((MC, MD)[s][:, 0:D], hT[s][:, k * P:(k + 1) * P], w2[:, e, k, :], start=k == 0, stop=k == nk - 1)
                        ins.then_inc(m["down"], 1)
                    t = j - 2
                    if 0 <= t < NJ:
                        s = t % 2
                        pe.wait_ge(m["act2"], m.count("act2", t + 1))
                        if t >= 2:
                            pe.wait_ge(m["hT"], m.count("hT", t - 1))
                        for k in range(nk):
                            ins = tr(TP[s][:, k * P:(k + 1) * P], ha[s][:, k * P:(k + 1) * P], ident[:, :])
                        ins.then_inc(m["Th"], 1)

            for l in range(2):
                for i in range(NT + LAG):
                    step(l, i)
                last = (NT - 1) % 2
                pe.wait_ge(A[l]["rankb"], A[l].count("rankb", NT))
                mm(MD[:, 2 * P + E:2 * P + 2 * E], ones_b[:, :], picks[last], start=True, stop=False)
                mm(MD[:, 2 * P + E:2 * P + 2 * E], ones_b[:, :], before[last], start=False, stop=True).then_inc(M[l]["cnt"], 1)
                if l == 0:
                    pe.wait_ge(M[0]["plan"], M[0].count("plan", 1))
                    pe.wait_ge(pro1["cn"], pro1.count("cn", NBATCH))
                    for b in range(NBATCH):
                        ins = tr(MD[:, b * KEYS:(b + 1) * KEYS], cn[:, b, :], ident[0:KEYS, 0:KEYS])
                    ins.then_inc(pro1["cT"], 1)
                    pe.wait_ge(ld["l1"], 160)
                    for g in range(2):
                        for k in range(4):
                            ins = tr(TP[g][:, k * P:(k + 1) * P], wq1[:, (4 * g + k) * P:(4 * g + k + 1) * P], ident[:, :])
                        ins.then_inc(pro1["wqT"], 1)
                    pe.wait_ge(pro1["cTs"], pro1.count("cTs", 1))
                    mm(MA[:, 0:NBATCH * KEYS], wkk[:, :, :].rearrange("p r d -> p (r d)"), ctxT[:, :], start=True, stop=True).then_inc(pro1["kv1"], 1)
                    mm(MC[:, 0:NBATCH * KEYS], wvv[:, :, :].rearrange("p r d -> p (r d)"), ctxT[:, :], start=True, stop=True).then_inc(pro1["kv1"], 1)
                    pe.wait_ge(pro1["wqTs"], pro1.count("wqTs", 2))
                    pe.wait_ge(pro1["kT1"], pro1.count("kT1", 1))
                    pe.wait_ge(pro1["vT1"], pro1.count("vT1", 1))
                    for h in range(H):
                        r = HD1 * (h % 2)
                        if h >= 2:
                            pe.wait_ge(pro1["keys1"], pro1.count("keys1", h - 1))
                        mm(S[h % 2][:, 0:NBATCH * KEYS], wq1T[r:r + HD1, h // 2, :], kT1[r:r + HD1, :], start=True, stop=True).then_inc(pro1["fk"], 1)
                        if h >= 2:
                            pe.wait_ge(pro1["foldT"], pro1.count("foldT", h - 1))
                        mm((S[2], MD)[h % 2][:, 0:NBATCH * KEYS], wo1[r:r + HD1, h // 2, :], vT1[r:r + HD1, :], start=True, stop=True).then_inc(pro1["fv"], 1)
                    pe.wait_ge(pro1["foldT"], pro1.count("foldT", H))
                    for n in range(NBATCH * 3):
                        b, g = n // 3, n % 3
                        if n >= 2:
                            pe.wait_ge(pro1["vals1"], pro1.count("vals1", n - 1))
                        for c in range(4 * g, min(4 * g + 4, CH)):
                            ins = tr(TP[n % 2][:, (c - 4 * g) * P:(c - 4 * g + 1) * P], foldT[b][:, c * P:(c + 1) * P], ident[:, :])
                        ins.then_inc(pro1["fT"], 1)
                    pe.wait_ge(pro1["vals1"], pro1.count("vals1", 3 * NBATCH))
                moe(l)


_INS = ['x', 'ctx_1024', 'fside_SxS2_0', 'L0_xattn_Wq', 'L0_xattn_bq', 'L0_xattn_Wk', 'L0_xattn_Wv', 'L0_xattn_Wo',
        'L0_xattn_bo', 'L0_xattn_scale_mul_log', 'L0_ffn_Wr', 'L0_ffn_W1', 'L0_ffn_W2', 'L0_ffn_W3', 'L1_xattn_ln_g',
        'L1_xattn_ln_b', 'L1_xattn_cln_g', 'L1_xattn_cln_b', 'L1_xattn_Wq', 'L1_xattn_Wkv', 'L1_xattn_Wo',
        'L1_xattn_Wff1', 'L1_xattn_Wff2', 'L1_ffn_W1', 'L1_ffn_b1', 'L1_ffn_W2', 'L1_ffn_b2', 'L1_ffn_Wr', 'L1_ffn_br']


def kernel(**inputs):
    import numpy as _np
    import concourse.bacc as _bacc
    from concourse import mybir as _mybir
    from concourse.bass_utils import run_bass_kernel_spmd as _run

    nc = _bacc.Bacc("TRN2", target_bir_lowering=False, num_devices=1)
    arrays, args = {}, []
    for name in _INS:
        a = _np.ascontiguousarray(inputs[name])
        arrays[f"in_{name}_dram"] = a
        args.append(nc.dram_tensor(f"in_{name}_dram", a.shape, _mybir.dt.from_np(a.dtype), kind="ExternalInput").ap())
    shape = inputs['x'].shape
    args.append(nc.dram_tensor("out_0_dram", shape, _mybir.dt.from_np(_np.dtype("float32")), kind="ExternalOutput").ap())
    bass_xattn_moe_two_layers(nc, *args)
    r = _run(nc, [arrays], core_ids=[0])
    return r.results[0]["out_0_dram"]
```

```python
from contextlib import ExitStack

import numpy as np
import concourse.bass as bass
from concourse import mybir

F32 = mybir.dt.float32
F32R = mybir.dt.float32r
BF16 = mybir.dt.bfloat16
I32 = mybir.dt.int32
U32 = mybir.dt.uint32
ACT = mybir.ActivationFunctionType
ALU = mybir.AluOpType
AX = mybir.AxisListType.X

P = 128
EPS = 1e-5
NORM_FLOOR = 1e-24
MAX_LOG_SCALE = float(np.log(100.0))
NCONST = 4


def bass_xattn_moe_two_layers(nc, x_in, ctx_in, bias_in, Wq0, bq0, Wk0, Wv0, Wo0, bo0, scale_log,
                              Wr0, W1_0, W2_0, W3_0, ln_g, ln_b, cln_g, cln_b, Wq1, Wkv1, Wo1,
                              Wff1, Wff2, W1_1, b1_1, W2_1, b2_1, Wr1, br1, out):
    NBATCH, SEQ, D = x_in.shape
    KEYS = ctx_in.shape[1]
    H = scale_log.shape[1]
    HD0 = D // H
    HD1 = Wq1.shape[1] // H
    E, _, F0 = W1_0.shape
    F1 = W1_1.shape[2]
    FF = Wff2.shape[0]
    T = NBATCH * SEQ
    NT = T // P
    TPB = SEQ // P
    HK = H * KEYS
    CH = -(-HK // P)
    HKP = CH * P
    G = 4
    NG = H // G
    GK = G * KEYS
    VW = HD0 + 1
    HB = 6
    BANK_AT = range(0, H, HB)
    BANK_HEADS = [min(HB, H - h) for h in BANK_AT]
    BANK_PARTS = [[(g, max(h, g * G), min(h + n, g * G + G)) for g in range(NG) if max(h, g * G) < min(h + n, g * G + G)]
                  for h, n in zip(BANK_AT, BANK_HEADS)]
    ROW = D + 1
    NJ = 2 * T // P + E
    REGION = T
    SLOTS = E * REGION + E * P
    NOWHERE = 1 << 20
    XB = 4
    assert D == P and H * HD0 == P and G * 4 * HD0 == P and F0 * 2 == F1 == 512 and TPB == 4 and FF == 512

    def at(i):
        return bass.ds(i, 1)

    with ExitStack() as ctx:
        def sb(name, shape, dt=F32):
            return ctx.enter_context(nc.sbuf_tensor(name, shape, dt))

        def sem(name):
            return ctx.enter_context(nc.semaphore(name))

        x = sb("x", [P, NT, D])
        with ExitStack() as early:
            def sb_early(name, shape, dt=F32):
                return early.enter_context(nc.sbuf_tensor(name, shape, dt))

            keys0 = sb_early("keys0", [P, NBATCH, HK], F32R)
            bias_r = sb_early("bias_r", [P, 2, TPB, GK], F32R)
            qT_both = sb_early("qT", [P, 2, NG * P], F32R)
        qT = [qT_both[:, 0], qT_both[:, 1]]
        w2b = sb("w2b", [P, E, F1 // P, D])
        vals1 = sb("vals1", [P, NBATCH, CH, D])
        region_a = sb("region_a", [P, NBATCH * CH * H * VW])
        vals0 = region_a[:, :].rearrange("p (b c h v) -> p b c h v", b=NBATCH, c=CH, h=H)
        w1b = region_a[:, 0:E * F1].rearrange("p (e f) -> p e f", e=E)
        b2bc = region_a[:, E * F1:E * F1 + E * D].rearrange("p (e d) -> p e d", e=E)
        region_b = sb("region_b", [P, E * 2 * F0])
        w13 = region_b[:, :].rearrange("p (e f) -> p e f", e=E)
        b1bc = region_b[:, :].rearrange("p (e f) -> p e f", e=E)
        w2a = sb("w2a", [P, E, F0 // P, D])
        keys1 = sb("keys1", [P, NBATCH, HK])
        pp = sb("pp", [P, 4, HKP])
        prob = [pp[:, 0, :], pp[:, 1, :]]
        probT = [pp[:, 2, :], pp[:, 3, :]]
        ident = sb("ident", [P, P])
        ident_r = sb("ident_r", [P, P], F32R)
        mask16 = sb("mask16", [P, H])
        mask4 = sb("mask4", [P, G])
        headsel = sb("headsel", [P, CH, H])
        upper = sb("upper", [P, P], BF16)
        ones_b = sb("ones_b", [P, P], BF16)
        mhalf = sb("mhalf", [P, NBATCH * H])
        iota8 = sb("iota8", [P, E])
        iota8i = sb("iota8i", [P, E], I32)
        ebase_b = sb("ebase_b", [P, E], BF16)
        ones_f = sb("ones_f", [P, P])
        ebasei = sb("ebasei", [P, E], I32)
        dest = sb("dest", [P, NT, 2], I32)
        jidx = sb("jidx", [1, NJ])
        jidxi = sb("jidxi", [1, NJ], I32)
        ones1 = sb("ones1", [1, E])
        empty = sb("empty", [P, 4, ROW])
        ctx_sb = sb("ctx_sb", [KEYS, NBATCH, D])
        ctxT = sb("ctxT", [P, NBATCH * KEYS])
        bias_sb = sb("bias_sb", [P, TPB, KEYS])
        wk0 = sb("wk0", [P, D])
        wv0 = sb("wv0", [P, D])
        wq0 = sb("wq0", [P, D])
        wo0 = sb("wo0", [P, D])
        bq_bc = sb("bq_bc", [P, D])
        bo_bc = sb("bo_bc", [P, D])
        scl = sb("scl", [KEYS, H])
        wr = [sb("wr0", [P, E]), sb("wr1", [P, E])]
        br_bc = sb("br_bc", [P, E])
        yb_all = sb("yb_all", [P, 4, 2, D])
        yb = [yb_all[:, k] for k in range(4)]
        wq1 = yb_all[:, :, :, :].rearrange("p a b d -> p (a b d)")
        big1 = sb("big1", [P, 2, F1])
        big2 = sb("big2", [P, 2, F1])
        wq1T = big1[:, :, :].rearrange("p a (k c) -> p (a k) c", c=D)
        wkk = sb("wkk", [P, 2, HD1])
        wvv = sb("wvv", [P, 2, HD1])
        wo1 = big2[:, :, :].rearrange("p a (k c) -> p (a k) c", c=D)
        wff1 = sb("wff1", [P, 2 * FF])
        wff2 = sb("wff2", [P, FF // P, D])
        gb = sb("gb", [P, 4])
        kT1 = sb("kT1", [P, NBATCH * KEYS])
        vT1 = sb("vT1", [P, NBATCH * KEYS])
        vT0 = sb("vT0", [P, NBATCH * KEYS])
        k0sq = pp[0:KEYS, 2, 0:NBATCH * D]
        k0n = pp[0:KEYS, 2, NBATCH * D:2 * NBATCH * D]
        k0split = pp[0:KEYS, 0:2, 0:1024].rearrange("p a (r s w d) -> p a r s w d", s=2, w=2, d=HD0)
        vblk = [pp[:, 3, :], pp[:, 2, :]]
        foldT = [pp[:, b, :] for b in range(NBATCH)]
        k0ss = sb("k0ss", [KEYS, NBATCH * H])
        k0sm = sb("k0sm", [KEYS, NBATCH * H])
        k0r = sb("k0r", [KEYS, NBATCH * H])
        k0rs = sb("k0rs", [KEYS, NBATCH * H])
        cstat = sb("cstat", [KEYS, NBATCH, 6])
        cmv = sb("cmv", [KEYS, NBATCH, 2])
        cve = sb("cve", [KEYS, NBATCH])
        crs = sb("crs", [KEYS, NBATCH])
        cn = sb("cn", [KEYS, NBATCH, D])
        def two(name, shape, dt=F32):
            t = sb(name, [shape[0], 2] + shape[1:], dt)
            return [t[:, 0], t[:, 1]]
        stA, mvA, veA, rsA, xnA = two("stA", [P, 6]), two("mvA", [P, 2]), two("veA", [P, 1]), two("rsA", [P, 1]), two("xnA", [P, D])
        stD, mvD, veD, rsD = two("stD", [P, 6]), two("mvD", [P, 2]), two("veD", [P, 1]), two("rsD", [P, 1])
        xT = two("xT", [P, P])
        qb, qsq, qn = two("qb", [P, D]), two("qsq", [P, D]), two("qn", [P, D])
        qss, qsm, qr = two("qss", [P, H]), two("qsm", [P, H]), two("qr", [P, H])
        qsplit = [big1[:, k].rearrange("p (h a b d) -> p h a b d", a=2, b=2, d=HD0) for k in range(2)]
        mx, den, rden = two("mx", [P, H]), two("den", [P, H]), two("rden", [P, H])
        on, oT = two("on", [P, D]), two("oT", [P, P])
        pay = two("pay", [P, 2, ROW])
        x2T = two("x2T", [P, P])
        top = sb("top", [P, NT, 8])
        topi = two("topi", [P, 8], U32)
        oh = two("oh", [P, 2, E])
        picks, before = two("picks", [P, E], BF16), two("before", [P, E], BF16)
        rsel, slotf = two("rsel", [P, 2, E]), two("slotf", [P, 2])
        slot = two("slot", [P, 2], I32)
        margin = sb("margin", [P, NT])
        gate = sb("gate", [P, 2, NT])
        gtmp = sb("gtmp", [P, 2, NT])
        ffbuf = [big1[:, 0], big1[:, 1]]
        gT = [big2[:, 0], big2[:, 1]]
        cnt_i = sb("cnt_i", [1, E], I32)
        cnt_s = sb("cnt_s", [1, E], I32)
        ntile = sb("ntile", [1, E])
        cum = sb("cum", [1, E])
        wgt = sb("wgt", [1, E])
        ind = sb("ind", [1, NJ, E - 1])
        ind2 = sb("ind2", [1, NJ, E - 1])
        ef = sb("ef", [1, NJ])
        rf = sb("rf", [1, NJ])
        rf2 = sb("rf2", [1, NJ])
        sched = [sb("sched0", [1, 2, NJ], I32), sb("sched1", [1, 2, NJ], I32)]
        xs = [sb(f"xs{i}", [P, ROW]) for i in range(XB)]
        back = [sb(f"back{i}", [P, 1], I32) for i in range(XB)]
        xsT = two("xsT", [P, P])
        ha = [big1[:, 0], big1[:, 1]]
        hT = [big2[:, 0], big2[:, 1]]
        ysb = two("ysb", [P, D])

        ps = ctx.enter_context(nc.psum_tensor("ps", [P, 8, 512], F32))
        S = [ps[:, k, :] for k in range(3)]
        TP = [ps[:, 3, :], ps[:, 4, :]]
        MA, MC, MD = ps[:, 5, :], ps[:, 6, :], ps[:, 7, :]

        rows = [nc.dram_tensor(f"rows{l}", (SLOTS, ROW), F32, kind="Internal").ap() for l in range(2)]
        ys = [nc.dram_tensor(f"ys{l}", (2 * T, D), F32, kind="Internal").ap() for l in range(2)]

        x_v = x_in.rearrange("b (t p) c -> p (b t) c", p=P)
        out_v = out.rearrange("b (t p) c -> p (b t) c", p=P)
        y_v = [y.rearrange("(t p k) d -> t p k d", p=P, k=2) for y in ys]

        class Stage:
            def __init__(self, tag, names, again=None):
                self.s, self.base = {}, {}
                for n in names:
                    name, self.base[n] = again[n] if again and n in again else (None, 0)
                    self.s[n] = sem(f"{n}_{tag}") if name is None else name

            def __getitem__(self, n):
                return self.s[n]

            def count(self, n, v):
                return self.base[n] + v

        BOTH = ["bnA", "mvA", "veA", "rsA", "xnA", "TxA", "xT", "S", "sub", "exp", "TP0", "PT0", "TP1", "TP2", "PT2",
                "AV", "rden", "xa", "bnD", "mvD", "veD", "rsD", "xnD", "Tx2", "x2T", "route", "top", "topi", "oh",
                "picks", "bef", "rank", "rsel", "slotf", "slot"]
        ONLY0 = ["q", "qb", "qsq", "qss", "qsm", "qr", "qn", "hi", "lo", "Tq", "qT", "on", "To", "oT", "Wo"]
        ONLY1 = ["c1", "comb", "ffg", "th", "gg", "ffh", "fo", "Tg", "gT", "mx", "den", "norm"]
        MOE = ["back", "Tx", "xsT", "up", "act1", "act2", "Th", "hT", "down", "y"]
        ONCE = {"margin": 1, "cnt": 1, "plan": 9, "sched": 1, "g1": 1, "gates": 3, "zero": 1}
        PRO0 = {"ctxT": 1, "ctxTs": 1, "k": 1, "ksq": 1, "kss": 1, "ksm": 1, "kr": 1, "krs": 1, "kn": 1, "khi": 1,
                "klo": 1, "kT": NBATCH, "keys0": NBATCH, "v": 1, "vT": 1, "vblk": NBATCH, "vtp": NBATCH * CH,
                "vals0": NBATCH * 3, "ones": NBATCH, "identr": 1, "bhi": 1, "blo": TPB, "scl": 1, "scm": 1}
        PRO1 = ["cbn", "cmv", "cve", "crs", "cn", "cT", "cTs", "kv1", "kT1", "vT1", "wqT", "wqTs", "fk", "keys1", "fv",
                "foldT", "fT", "vals1"]
        att0 = Stage("a", BOTH + ONLY0)
        again = {n: (att0[n], NT) for n in BOTH}
        again.update({n: (att0[o], NT) for n, o in zip(ONLY1, ONLY0)})
        A = [att0, Stage("a", BOTH + ONLY1, again)]
        moe0 = Stage("m", MOE + list(ONCE))
        again = {n: (moe0[n], NJ) for n in MOE}
        again.update({n: (moe0[n], c) for n, c in ONCE.items()})
        M = [moe0, Stage("m", MOE + list(ONCE) + ["fin", "fin0"], again)]
        pro = Stage("p", PRO0)
        pro1 = Stage("p", PRO1, {n: (pro[o], PRO0[o]) for n, o in zip(PRO1, list(PRO0))})
        ld = {n: sem(f"ld_{n}") for n in ("x", "ctx", "q", "o", "moe0", "l1", "l1b", "moe1", "bias")}
        filled = [sem("filled0"), sem("filled1")]
        xs_in = [sem(f"xs_in{i}") for i in range(XB)]
        sent = [sem(f"sent{i}") for i in range(2)]
        sentb = [sem(f"sentb{i}") for i in range(XB)]
        y_in = [sem(f"y_in{i}") for i in range(4)]
        stored = sem("stored")
        const = sem("const")

        def sent_count(l, t):
            return 32 * (l * NT // 2 + t // 2 + 1)

        def sentb_count(l, j):
            return 16 * (l * NJ // XB + j // XB + 1)

        LAG = (7, 7)
        FILLS = SLOTS // P // 4
        S01 = ps[:, 0:2, 0:HB * KEYS].rearrange("p b (h k) -> p b h k", k=KEYS)
        S2 = ps[:, 2, 0:(H - 2 * HB) * KEYS].rearrange("p (h k) -> p h k", k=KEYS)
        AV0 = MC[:, 0:H * VW].rearrange("p (h v) -> p h v", h=H)
        RANK = MD[:, 2 * P + E:2 * P + 2 * E]

        def row_of(ap, n):
            return ap.rearrange("(a n) -> a n", a=1).to_broadcast([P, n])

        block = ctx.enter_context(nc.Block())

        @block.sync
        def _(sp):
            sp.dma_start(ctx_sb[:, :, :], ctx_in.rearrange("b k c -> k b c")).then_inc(ld["ctx"], 16)
            sp.dma_start(wk0[:, :], Wk0).then_inc(ld["ctx"], 16)
            sp.dma_start(wv0[:, :], Wv0).then_inc(ld["ctx"], 16)
            sp.dma_start(x[:, :, :], x_v).then_inc(ld["x"], 16)
            sp.wait_ge(const, 1)
            for l in range(2):
                dst = rows[l].rearrange("(n p r) c -> n p (r c)", p=P, r=4)
                for n in range(SLOTS // P // 4):
                    sp.dma_start(dst[n], empty[:, :, :].rearrange("p r c -> p (r c)")).then_inc(filled[l], 16)
                if l == 0:
                    sp.dma_start(w13[:, :, 0:F0], W1_0.rearrange("e c f -> c e f")).then_inc(ld["moe0"], 16)
                    sp.dma_start(w13[:, :, F0:2 * F0], W3_0.rearrange("e c f -> c e f")).then_inc(ld["moe0"], 16)
                    sp.dma_start(w2a[:, :, :, :], W2_0.rearrange("e (k p) d -> p e k d", p=P)).then_inc(ld["moe0"], 16)
                    sp.dma_start(wq1[:, :], Wq1).then_inc(ld["l1"], 16)
                    for r in range(2):
                        sp.dma_start(wkk[:, r, :], Wkv1[:, 0:HD1]).then_inc(ld["l1"], 16)
                        sp.dma_start(wvv[:, r, :], Wkv1[:, HD1:2 * HD1]).then_inc(ld["l1"], 16)
                    sp.dma_start(wo1[:, :, :], Wo1.rearrange("(k p) d -> p k d", p=P)).then_inc(ld["l1"], 16)
                    for n, v in enumerate((ln_g, ln_b, cln_g, cln_b)):
                        sp.dma_start(gb[:, n:n + 1], v.rearrange("(c a) -> c a", a=1)).then_inc(ld["l1"], 16)
                    sp.dma_start(wff1[:, :], Wff1).then_inc(ld["l1b"], 16)
                    sp.dma_start(wff2[:, :, :], Wff2.rearrange("(k p) d -> p k d", p=P)).then_inc(ld["l1b"], 16)
                    sp.dma_start(wr[1][:, :], Wr1).then_inc(ld["l1b"], 16)
                    sp.dma_start(br_bc[:, :], row_of(br1, E)).then_inc(ld["l1b"], 16)
            for l in range(2):
                m = M[l]
                if l == 0:
                    sp.wait_ge(A[0]["AV"], A[0].count("AV", NT))
                    sp.dma_start(w2b[:, :, :, :], W2_1.rearrange("e (k p) d -> p e k d", p=P)).then_inc(ld["moe1"], 16)
                    sp.dma_start(w1b, W1_1.rearrange("e c f -> c e f")).then_inc(ld["moe1"], 16)
                    sp.dma_start(b2bc, b2_1.rearrange("(a e) d -> a e d", a=1).to_broadcast([P, E, D])).then_inc(ld["moe1"], 16)
                else:
                    sp.wait_ge(M[0]["up"], M[0].count("up", NJ))
                    sp.dma_start(b1bc, b1_1.rearrange("(a e) f -> a e f", a=1).to_broadcast([P, E, F1])).then_inc(ld["moe1"], 16)
                sp.wait_ge(m["sched"], m.count("sched", 1))
                for t in (NT - 2, NT - 1):
                    sp.wait_ge(sent[(t) % 2], sent_count(l, t))
                sp.wait_ge(filled[l], 16 * FILLS)
                for j in range(NJ):
                    k = j % XB
                    if j >= XB:
                        sp.wait_ge(m["Tx"], m.count("Tx", j - XB + 1))
                    if j >= XB:
                        sp.wait_ge(m["back"], m.count("back", j - XB + 1))
                    r = sp.value_load(sched[l][0:1, 1, at(j)], min_val=0, max_val=SLOTS - P)
                    sp.dma_start(xs[k][:, :], rows[l][bass.ds(r, P), :]).then_inc(xs_in[k], 16)
                for j in range(NJ - XB, NJ):
                    sp.wait_ge(sentb[(j) % XB], sentb_count(l, j))
                for t in range(NT):
                    if t >= 4:
                        if l == 0:
                            sp.wait_ge(A[1]["comb"], A[1].count("comb", t - 3))
                        else:
                            sp.wait_ge(m["fin"], m.count("fin", t - 3))
                    sp.dma_start(yb[t % 4][:, :, :], y_v[l][t]).then_inc(y_in[t % 4], 16)
                    if l == 1 and t >= 1:
                        if t >= 1:
                            sp.wait_ge(m["fin"], m.count("fin", t))
                        sp.dma_start(out_v[:, t - 1, :], x[:, t - 1, :]).then_inc(stored, 16)
            sp.wait_ge(M[1]["fin"], M[1].count("fin", NT))
            sp.dma_start(out_v[:, NT - 1, :], x[:, NT - 1, :]).then_inc(stored, 16)
            sp.wait_ge(stored, 16 * NT)

        @block.gpsimd
        def _(pool):
            pool.memset(empty[:, :, 0:D], 0.0)
            pool.iota(empty[:, :, D:ROW].bitcast(I32), [[0, 4], [0, 1]], base=NOWHERE, channel_multiplier=0).then_inc(const, 1)
            pool.memset(ident[:, :], 0.0)
            pool.memset(mask16[:, :], 1.0)
            pool.memset(mask4[:, :], 1.0)
            pool.memset(headsel[:, :, :], 1.0)
            pool.memset(upper[:, :], 1.0)
            pool.memset(ones_b[:, :], 1.0)
            pool.memset(ones_f[:, :], 1.0)
            pool.memset(before[0], 0.0)
            pool.memset(ones1[:, :], 1.0)
            pool.memset(mhalf[:, :], -0.5)
            pool.memset(pp[:, :, HK:HKP], 0.0)
            pool.iota(iota8i[:, :], [[1, E]], base=0, channel_multiplier=0)
            pool.iota(ebasei[:, :], [[REGION, E]], base=0, channel_multiplier=0)
            pool.iota(dest[:, :, :], [[2 * P, NT], [1, 2]], base=0, channel_multiplier=2)
            pool.iota(jidxi[:, :], [[1, NJ]], base=0, channel_multiplier=0).then_inc(const, 1)
            pool.wait_ge(const, 2)
            pool.affine_select(out=ident[:, :], in_=ident[:, :], compare_op=ALU.not_equal, fill=1.0,
                               base=0, pattern=[[-1, P]], channel_multiplier=1)
            pool.affine_select(out=upper[:, :], in_=upper[:, :], compare_op=ALU.is_gt, fill=0.0,
                               base=0, pattern=[[1, P]], channel_multiplier=-1)
            pool.affine_select(out=mask16[:, :], in_=mask16[:, :], compare_op=ALU.is_ge, fill=0.0,
                               base=0, pattern=[[-HD0, H]], channel_multiplier=1)
            pool.affine_select(out=mask4[:, :], in_=mask4[:, :], compare_op=ALU.is_ge, fill=0.0,
                               base=0, pattern=[[-4 * HD0, G]], channel_multiplier=1)
            pool.affine_select(out=headsel[:, :, :], in_=headsel[:, :, :], compare_op=ALU.is_ge, fill=0.0,
                               base=0, pattern=[[P, CH], [-KEYS, H]], channel_multiplier=1).then_inc(const, 1)
            pool.wait_ge(const, 3)
            pool.affine_select(out=mask16[:, :], in_=mask16[:, :], compare_op=ALU.is_ge, fill=0.0,
                               base=HD0 - 1, pattern=[[HD0, H]], channel_multiplier=-1)
            pool.affine_select(out=mask4[:, :], in_=mask4[:, :], compare_op=ALU.is_ge, fill=0.0,
                               base=4 * HD0 - 1, pattern=[[4 * HD0, G]], channel_multiplier=-1)
            pool.affine_select(out=headsel[:, :, :], in_=headsel[:, :, :], compare_op=ALU.is_ge, fill=0.0,
                               base=KEYS - 1, pattern=[[-P, CH], [KEYS, H]], channel_multiplier=-1)
            pool.tensor_copy(iota8[:, :], iota8i[:, :])
            pool.tensor_copy(ebase_b[:, :], ebasei[:, :])
            pool.tensor_copy(jidx[:, :], jidxi[:, :]).then_inc(const, 1)
            pool.wait_ge(const, NCONST)
            pool.wait_ge(ld["o"], 48)
            pool.wait_ge(pro["ksm"], pro.count("ksm", 1))
            pool.tensor_tensor(k0r[:, :], k0sm[:, :], mhalf[0:KEYS, :], ALU.pow).then_inc(pro["kr"], 1)
            pool.wait_ge(pro["kr"], pro.count("kr", 1))
            pool.wait_ge(pro["scl"], pro.count("scl", 1))
            pool.tensor_tensor(k0rs[:, :].rearrange("k (b h) -> k b h", b=NBATCH),
                               k0r[:, :].rearrange("k (b h) -> k b h", b=NBATCH),
                               scl[:, :].unsqueeze(1).to_broadcast([KEYS, NBATCH, H]), ALU.mult).then_inc(pro["krs"], 1)
            pool.wait_ge(pro["bhi"], pro.count("bhi", 1))
            for tt in range(TPB):
                pool.tensor_tensor(bias_r[:, 1, tt, :].rearrange("p (h k) -> p h k", k=KEYS),
                                   bias_sb[:, tt, :].unsqueeze(1).to_broadcast([P, G, KEYS]),
                                   bias_r[:, 0, tt, :].bitcast(F32).rearrange("p (h k) -> p h k", k=KEYS),
                                   ALU.subtract).then_inc(pro["blo"], 1)
            pool.wait_ge(pro["vT"], pro.count("vT", 1))
            pool.wait_ge(pro["keys0"], pro.count("keys0", NBATCH))
            for b in range(NBATCH):
                if b >= 2:
                    pool.wait_ge(pro["vtp"], pro.count("vtp", CH * (b - 1)))
                pool.tensor_tensor(vblk[b % 2][:, 0:HK].rearrange("p (h k) -> p h k", h=H),
                                   mask16[:, :].unsqueeze(2).to_broadcast([P, H, KEYS]),
                                   vT0[:, b * KEYS:(b + 1) * KEYS].unsqueeze(1).to_broadcast([P, H, KEYS]),
                                   ALU.mult).then_inc(pro["vblk"], 1)
            for b in range(NBATCH):
                pool.tensor_copy(vals0[:, b, :, :, HD0], headsel[:, :, :]).then_inc(pro["ones"], 1)

            def step0(i):
                a = A[0]
                t = i
                if 0 <= t < NT:
                    s = t % 2
                    pool.wait_ge(a["veA"], a.count("veA", t + 1))
                    pool.tensor_tensor(rsA[s], veA[s], mhalf[:, 0:1], ALU.pow).then_inc(a["rsA"], 1)
                t = i - 2
                if 0 <= t < NT:
                    s = t % 2
                    pool.wait_ge(a["qsm"], a.count("qsm", t + 1))
                    pool.tensor_tensor(qr[s], qsm[s], mhalf[:, 0:H], ALU.pow).then_inc(a["qr"], 1)
                t = i - 6
                if 0 <= t < NT:
                    s = t % 2
                    pool.wait_ge(a["veD"], a.count("veD", t + 1))
                    pool.tensor_tensor(rsD[s], veD[s], mhalf[:, 0:1], ALU.pow).then_inc(a["rsD"], 1)
                t = i - 7
                if 0 <= t < NT:
                    s = t % 2
                    if t == 0:
                        pool.wait_ge(filled[0], 16 * FILLS)
                    pool.wait_ge(a["slot"], a.count("slot", t + 1))
                    for k in range(2):
                        pool.indirect_dma_start(rows[0][:, :], bass.IndirectOffsetOnAxis(slot[s][:, k:k + 1], 0), pay[s][:, k, :], None,
                                                bounds_check=SLOTS - 1, oob_is_err=False).then_inc(sent[s], 16)

            def step1(i):
                a = A[1]
                t = i - 4
                if 0 <= t < NT:
                    s = t % 2
                    pool.wait_ge(a["rden"], a.count("rden", t + 1))
                    p3 = prob[s][:, 0:HK].rearrange("p (h k) -> p h k", h=H)
                    pool.tensor_tensor(p3, p3, rden[s].unsqueeze(2).to_broadcast([P, H, KEYS]), ALU.mult).then_inc(a["norm"], 1)
                t = i - 7
                if 0 <= t < NT:
                    s = t % 2
                    if t == 0:
                        pool.wait_ge(filled[1], 16 * FILLS)
                    pool.wait_ge(a["slot"], a.count("slot", t + 1))
                    for k in range(2):
                        pool.indirect_dma_start(rows[1][:, :], bass.IndirectOffsetOnAxis(slot[s][:, k:k + 1], 0), pay[s][:, k, :], None,
                                                bounds_check=SLOTS - 1, oob_is_err=False).then_inc(sent[s], 16)
                t = i - 5
                if 0 <= t < NT:
                    s = t % 2
                    pool.wait_ge(a["veD"], a.count("veD", t + 1))
                    pool.tensor_tensor(rsD[s], veD[s], mhalf[:, 0:1], ALU.pow).then_inc(a["rsD"], 1)
                t = i - 1
                if 0 <= t < NT:
                    s = t % 2
                    pool.wait_ge(a["veA"], a.count("veA", t + 1))
                    pool.tensor_tensor(rsA[s], veA[s], mhalf[:, 0:1], ALU.pow).then_inc(a["rsA"], 1)
                    pool.wait_ge(a["rsA"], a.count("rsA", t + 1))
                    pool.tensor_scalar(xnA[s], x[:, t, :], mvA[s][:, 0:1], rsA[s], ALU.subtract, ALU.mult).then_inc(a["xnA"], 1)

            def moe(l):
                m = M[l]

                def send(j):
                    pool.wait_ge(m["y"], m.count("y", j + 1))
                    pool.wait_ge(m["back"], m.count("back", j + 1))
                    pool.indirect_dma_start(ys[l][:, :], bass.IndirectOffsetOnAxis(back[j % XB][:, 0:1], 0),
                                            ysb[j % 2], None, bounds_check=2 * T - 1,
                                            oob_is_err=False).then_inc(sentb[j % XB], 16)
                for j in range(NJ + 3):
                    if j < NJ:
                        pool.wait_ge(xs_in[j % XB], 16 * ((NJ // XB) * l + j // XB + 1))
                        if j >= XB:
                            pool.wait_ge(sentb[(j - XB) % XB], sentb_count(l, j - XB))
                        pool.tensor_copy(back[j % XB][:, :], xs[j % XB][:, D:ROW].bitcast(I32)).then_inc(m["back"], 1)
                    if j >= 3:
                        send(j - 3)

            for l in range(2):
                for i in range(NT + LAG[l]):
                    step0(i) if l == 0 else step1(i)
                if l == 0:
                    pool.wait_ge(pro1["cve"], pro1.count("cve", 1))
                    pool.tensor_tensor(crs[:, :], cve[:, :], mhalf[0:KEYS, 0:NBATCH], ALU.pow).then_inc(pro1["crs"], 1)
                moe(l)

        @block.scalar
        def _(act):
            act.dma_start(scl[:, :], scale_log.rearrange("a h b c -> a (h b c)").to_broadcast([KEYS, H])).then_inc(ld["q"], 16)
            act.dma_start(wq0[:, :], Wq0).then_inc(ld["q"], 16)
            act.dma_start(bq_bc[:, :], row_of(bq0, D)).then_inc(ld["q"], 16)
            act.dma_start(bias_sb[:, :, :], bias_in.rearrange("(t p) k -> p t k", p=P)).then_inc(ld["bias"], 16)
            act.dma_start(wo0[:, :], Wo0).then_inc(ld["o"], 16)
            act.dma_start(bo_bc[:, :], row_of(bo0, D)).then_inc(ld["o"], 16)
            act.dma_start(wr[0][:, :], Wr0).then_inc(ld["o"], 16)

            act.wait_ge(pro["ctxT"], pro.count("ctxT", 1))
            act.copy(ctxT[:, :], MD[:, 0:NBATCH * KEYS]).then_inc(pro["ctxTs"], 1)
            act.wait_ge(pro["k"], pro.count("k", 1))
            act.activation(k0sq, MC[0:KEYS, :], ACT.Square).then_inc(pro["ksq"], 1)
            act.wait_ge(pro["scm"], pro.count("scm", 1))
            act.activation(scl[:, :], scl[:, :], ACT.Exp).then_inc(pro["scl"], 1)
            act.wait_ge(pro["v"], pro.count("v", 1))
            act.copy(vT0[:, :], MA[:, 0:NBATCH * KEYS]).then_inc(pro["vT"], 1)
            act.wait_ge(ld["bias"], 16)
            for tt in range(TPB):
                ins = act.copy(bias_r[:, 0, tt, :].rearrange("p (h k) -> p h k", k=KEYS),
                               bias_sb[:, tt, :].unsqueeze(1).to_broadcast([P, G, KEYS]))
            ins.then_inc(pro["bhi"], 1)
            act.wait_ge(const, NCONST)
            act.copy(ident_r[:, :], ident[:, :]).then_inc(pro["identr"], 1)
            for n in range(NBATCH * 3):
                b, g = n // 3, n % 3
                w = min(4, CH - 4 * g)
                act.wait_ge(pro["vtp"], pro.count("vtp", b * CH + 4 * g + w))
                act.copy(vals0[:, b, 4 * g:4 * g + w, :, 0:HD0],
                         TP[n % 2][:, 0:w * P].rearrange("p (c h d) -> p c h d", c=w, h=H)).then_inc(pro["vals0"], 1)

            def step0(i):
                a = A[0]
                t = i - 2
                if 0 <= t < NT:
                    s = t % 2
                    act.wait_ge(a["TxA"], a.count("TxA", t + 1))
                    act.copy(xT[s], MA[:, 0:P]).then_inc(a["xT"], 1)
                t = i - 6
                if 0 <= t < NT:
                    s = t % 2
                    act.wait_ge(a["TP0"], a.count("TP0", t + 1))
                    act.copy(probT[s][:, 0:4 * P], TP[0]).then_inc(a["PT0"], 1)
                    act.wait_ge(a["TP1"], a.count("TP1", t + 1))
                    act.copy(probT[s][:, 4 * P:8 * P], TP[1])
                t = i - 2
                if 0 <= t < NT:
                    s = t % 2
                    act.wait_ge(a["q"], a.count("q", t + 1))
                    act.copy(qb[s], MA[:, P:2 * P]).then_inc(a["qb"], 1)
                t = i - 6
                if 0 <= t < NT:
                    s = t % 2
                    act.wait_ge(a["TP2"], a.count("TP2", t + 1))
                    act.copy(probT[s][:, 8 * P:HKP], TP[0][:, 0:HKP - 8 * P]).then_inc(a["PT2"], 1)
                t = i - 4
                if 0 <= t < NT:
                    s = t % 2
                    act.wait_ge(a["Tq"], a.count("Tq", t + 1))
                    act.copy(qT[s], MA[:, :]).then_inc(a["qT"], 1)
                t = i - 2
                if 0 <= t < NT:
                    s = t % 2
                    act.wait_ge(a["qb"], a.count("qb", t + 1))
                    act.activation(qsq[s], qb[s], ACT.Square).then_inc(a["qsq"], 1)
                t = i - 5
                if 0 <= t < NT:
                    s = t % 2
                    act.wait_ge(a["sub"], a.count("sub", t + 1))
                    act.activation(prob[s][:, 0:HK], prob[s][:, 0:HK], ACT.Exp).then_inc(a["exp"], 1)
                t = i - 3
                if 0 <= t < NT:
                    s = t % 2
                    act.wait_ge(a["qn"], a.count("qn", t + 1))
                    act.copy(qsplit[s][:, :, 0, :, :].bitcast(F32R),
                             qn[s].rearrange("p (h d) -> p h d", h=H).unsqueeze(2).to_broadcast([P, H, 2, HD0])).then_inc(a["hi"], 1)
                t = i - 6
                if 0 <= t < NT:
                    s = t % 2
                    act.wait_ge(a["To"], a.count("To", t + 1))
                    act.copy(oT[s], MC[:, 2 * P:3 * P]).then_inc(a["oT"], 1)
                t = i - 7
                if 0 <= t < NT:
                    s = t % 2
                    act.wait_ge(a["Tx2"], a.count("Tx2", t + 1))
                    act.copy(x2T[s], MD[:, P:2 * P]).then_inc(a["x2T"], 1)

            def step1(i):
                a = A[1]
                t = i - 6
                if 0 <= t < NT:
                    s = t % 2
                    act.wait_ge(a["TP2"], a.count("TP2", t + 1))
                    act.copy(probT[s][:, 8 * P:HKP], TP[0][:, 0:HKP - 8 * P]).then_inc(a["PT2"], 1)
                t = i - 3
                if 0 <= t < NT:
                    s = t % 2
                    act.wait_ge(a["TxA"], a.count("TxA", t + 1))
                    act.activation(xT[s], MA[:, 0:P], ACT.Identity, bias=gb[:, 1:2], scale=gb[:, 0:1]).then_inc(a["xT"], 1)
                t = i - 5
                if 0 <= t < NT:
                    s = t % 2
                    act.wait_ge(a["Tg"], a.count("Tg", t + 1))
                    act.copy(gT[s], TP[1]).then_inc(a["gT"], 1)
                t = i - 7
                if 0 <= t < NT:
                    s = t % 2
                    act.wait_ge(a["Tx2"], a.count("Tx2", t + 1))
                    act.copy(x2T[s], MD[:, P:2 * P]).then_inc(a["x2T"], 1)
                t = i - 5
                if 0 <= t < NT:
                    s = t % 2
                    act.wait_ge(a["TP0"], a.count("TP0", t + 1))
                    act.copy(probT[s][:, 0:4 * P], TP[0]).then_inc(a["PT0"], 1)
                t = i - 3
                if 0 <= t < NT:
                    s = t % 2
                    act.wait_ge(a["ffg"], a.count("ffg", t + 1))
                    act.activation(ffbuf[s], MA[:, :], ACT.Tanh, scale=0.5).then_inc(a["th"], 1)
                t = i - 4
                if 0 <= t < NT:
                    s = t % 2
                    act.wait_ge(a["sub"], a.count("sub", t + 1))
                    act.activation(prob[s][:, 0:HK], prob[s][:, 0:HK], ACT.Exp).then_inc(a["exp"], 1)
                t = i - 5
                if 0 <= t < NT:
                    s = t % 2
                    act.wait_ge(a["TP1"], a.count("TP1", t + 1))
                    act.copy(probT[s][:, 4 * P:8 * P], TP[1])

            def moe(l):
                m = M[l]

                for j in range(NJ + 3):
                    if j < NJ:
                        act.wait_ge(m["Tx"], m.count("Tx", j + 1))
                        if j >= 2:
                            act.wait_ge(m["up"], m.count("up", j - 1))
                        act.copy(xsT[j % 2], MA[:, 0:P]).then_inc(m["xsT"], 1)
                    t = j - 1
                    if 0 <= t < NJ:
                        s = t % 2
                        if l == 0:
                            act.wait_ge(m["up"], m.count("up", t + 1))
                            if t >= 2:
                                act.wait_ge(m["Th"], m.count("Th", t - 1))
                            act.activation(ha[s][:, 0:F0], S[s][:, 0:F0], ACT.Silu).then_inc(m["act1"], 1)
                        else:
                            act.wait_ge(m["act1"], m.count("act1", t + 1))
                            act.activation(ha[s], ha[s], ACT.Gelu_apprx_tanh).then_inc(m["act2"], 1)
                    t = j - 2
                    if 0 <= t < NJ:
                        s = t % 2
                        act.wait_ge(m["Th"], m.count("Th", t + 1))
                        if t >= 2:
                            act.wait_ge(m["down"], m.count("down", t - 1))
                        w = F0 if l == 0 else F1
                        act.copy(hT[s][:, 0:w], TP[s][:, 0:w]).then_inc(m["hT"], 1)

            for l in range(2):
                if l == 1:
                    act.wait_ge(ld["l1b"], 16 * 4)
                for i in range(NT + LAG[l]):
                    step0(i) if l == 0 else step1(i)
                act.wait_ge(M[l]["margin"], M[l].count("margin", 1))
                act.activation(gtmp[:, 0, :], margin[:, :], ACT.Exp).then_inc(M[l]["g1"], 1)
                if l == 0:
                    act.wait_ge(ld["l1"], 16 * 10)
                    act.wait_ge(pro1["cT"], pro1.count("cT", 1))
                    act.activation(ctxT[:, :], MD[:, 0:NBATCH * KEYS], ACT.Identity, bias=gb[:, 3:4], scale=gb[:, 2:3]).then_inc(pro1["cTs"], 1)
                    act.wait_ge(pro1["kv1"], pro1.count("kv1", 1))
                    act.activation(kT1[:, :], MA[:, 0:NBATCH * KEYS], ACT.Copy, scale=float(HD1) ** -0.5).then_inc(pro1["kT1"], 1)
                    act.wait_ge(pro1["kv1"], pro1.count("kv1", 2))
                    act.copy(vT1[:, :], MC[:, 0:NBATCH * KEYS]).then_inc(pro1["vT1"], 1)
                    for g in range(2):
                        act.wait_ge(pro1["wqT"], pro1.count("wqT", g + 1))
                        act.copy(wq1T[:, 4 * g:4 * g + 4, :], TP[g][:, :].rearrange("p (k c) -> p k c", k=4)).then_inc(pro1["wqTs"], 1)
                    for h in range(H):
                        act.wait_ge(pro1["fk"], pro1.count("fk", h + 1))
                        act.copy(keys1[:, :, h * KEYS:(h + 1) * KEYS],
                                 S[h % 2][:, 0:NBATCH * KEYS].rearrange("p (b k) -> p b k", b=NBATCH)).then_inc(pro1["keys1"], 1)
                    for n in range(NBATCH * 3):
                        b, g = n // 3, n % 3
                        w = min(4, CH - 4 * g)
                        act.wait_ge(pro1["fT"], pro1.count("fT", n + 1))
                        act.copy(vals1[:, b, 4 * g:4 * g + w, :],
                                 TP[n % 2][:, 0:w * P].rearrange("p (c d) -> p c d", c=w)).then_inc(pro1["vals1"], 1)
                moe(l)

        @block.vector
        def _(dve):
            dve.wait_ge(ld["q"], 48)
            dve.tensor_scalar(scl[:, :], scl[:, :], MAX_LOG_SCALE, None, ALU.min).then_inc(pro["scm"], 1)
            dve.wait_ge(pro["ksq"], pro.count("ksq", 1))
            dve.reduce_sum(k0ss[:, :], k0sq.rearrange("k (r d) -> k r d", d=HD0), AX).then_inc(pro["kss"], 1)
            dve.wait_ge(pro["kss"], pro.count("kss", 1))
            dve.tensor_scalar(k0sm[:, :], k0ss[:, :], NORM_FLOOR, None, ALU.max).then_inc(pro["ksm"], 1)
            dve.wait_ge(pro["krs"], pro.count("krs", 1))
            dve.tensor_tensor(k0n.rearrange("k (r d) -> k r d", d=HD0), MC[0:KEYS, :].rearrange("k (r d) -> k r d", d=HD0),
                              k0rs[:, :].unsqueeze(2).to_broadcast([KEYS, NBATCH * H, HD0]), ALU.mult).then_inc(pro["kn"], 1)
            dve.wait_ge(pro["kn"], pro.count("kn", 1))
            for half in range(2):
                src = k0n[:, half * 256:half * 256 + 256].rearrange("k (r d) -> k r d", d=HD0)
                for s2 in range(2):
                    ins = dve.tensor_copy(k0split[:, half, :, s2, 0, :].bitcast(F32R), src)
            ins.then_inc(pro["khi"], 1)
            dve.wait_ge(pro["khi"], pro.count("khi", 1))
            for half in range(2):
                src = k0n[:, half * 256:half * 256 + 256].rearrange("k (r d) -> k r d", d=HD0)
                for s2 in range(2):
                    ins = dve.tensor_tensor(k0split[:, half, :, s2, 1, :], src, k0split[:, half, :, s2, 0, :], ALU.subtract)
            ins.then_inc(pro["klo"], 1)
            dve.wait_ge(const, NCONST)
            for b in range(NBATCH):
                dve.wait_ge(pro["kT"], pro.count("kT", b + 1))
                src = (S + [TP[0]])[b]
                for g in range(NG):
                    ins = dve.tensor_tensor(keys0[:, b, g * GK:(g + 1) * GK].rearrange("p (h k) -> p h k", h=G),
                                      src[:, g * KEYS:(g + 1) * KEYS].unsqueeze(1).to_broadcast([P, G, KEYS]),
                                      mask4[:, :].unsqueeze(2).to_broadcast([P, G, KEYS]),
                                      ALU.mult)
                ins.then_inc(pro["keys0"], 1)

            dve.wait_ge(ld["x"], 16)
            dve.wait_ge(ld["o"], 48)

            def step0(i):
                a = A[0]
                t = i
                if 0 <= t < NT:
                    s = t % 2
                    dve.bn_stats(stA[s], x[:, t, :]).then_inc(a["bnA"], 1)
                t = i - 1
                if 0 <= t < NT:
                    s = t % 2
                    dve.wait_ge(a["rsA"], a.count("rsA", t + 1))
                    dve.tensor_scalar(xnA[s], x[:, t, :], mvA[s][:, 0:1], rsA[s], ALU.subtract, ALU.mult).then_inc(a["xnA"], 1)
                t = i
                if 0 <= t < NT:
                    s = t % 2
                    dve.wait_ge(a["bnA"], a.count("bnA", t + 1))
                    dve.bn_aggr(mvA[s], stA[s]).then_inc(a["mvA"], 1)
                t = i - 3
                if 0 <= t < NT:
                    s = t % 2
                    dve.wait_ge(a["qr"], a.count("qr", t + 1))
                    dve.tensor_tensor(qn[s].rearrange("p (h d) -> p h d", h=H), qb[s].rearrange("p (h d) -> p h d", h=H),
                                      qr[s].unsqueeze(2).to_broadcast([P, H, HD0]), ALU.mult).then_inc(a["qn"], 1)
                t = i - 7
                if 0 <= t < NT:
                    s = t % 2
                    dve.wait_ge(a["rsD"], a.count("rsD", t + 1))
                    dve.tensor_scalar(pay[s][:, :, 0:D], x[:, t, :].unsqueeze(1).to_broadcast([P, 2, D]),
                                      mvD[s][:, 0:1], rsD[s], ALU.subtract, ALU.mult).then_inc(a["xnD"], 1)
                t = i
                if 0 <= t < NT:
                    s = t % 2
                    dve.wait_ge(a["mvA"], a.count("mvA", t + 1))
                    dve.tensor_scalar(veA[s], mvA[s][:, 1:2], EPS, None, ALU.add).then_inc(a["veA"], 1)
                t = i - 4
                if 0 <= t < NT:
                    s = t % 2
                    dve.wait_ge(a["S"], a.count("S", t + 1))
                    dve.reduce_max(mx[s][:, 0:2 * HB].rearrange("p (b h) -> p b h", b=2), S01, AX)
                    dve.reduce_max(mx[s][:, 2 * HB:H], S2, AX)
                t = i - 3
                if 0 <= t < NT:
                    s = t % 2
                    dve.wait_ge(a["hi"], a.count("hi", t + 1))
                    dve.tensor_tensor(qsplit[s][:, :, 1, :, :],
                                      qn[s].rearrange("p (h d) -> p h d", h=H).unsqueeze(2).to_broadcast([P, H, 2, HD0]),
                                      qsplit[s][:, :, 0, :, :], ALU.subtract).then_inc(a["lo"], 1)
                t = i - 6
                if 0 <= t < NT:
                    s = t % 2
                    dve.wait_ge(a["Wo"], a.count("Wo", t + 1))
                    dve.tensor_tensor(x[:, t, :], x[:, t, :], MD[:, 0:D], ALU.add).then_inc(a["xa"], 1)
                t = i - 2
                if 0 <= t < NT:
                    s = t % 2
                    dve.wait_ge(a["qsq"], a.count("qsq", t + 1))
                    dve.reduce_sum(qss[s], qsq[s].rearrange("p (h d) -> p h d", h=H), AX).then_inc(a["qss"], 1)
                    dve.wait_ge(a["qss"], a.count("qss", t + 1))
                    dve.tensor_scalar(qsm[s], qss[s], NORM_FLOOR, None, ALU.max).then_inc(a["qsm"], 1)
                t = i - 7
                if 0 <= t < NT:
                    s = t % 2
                    dve.wait_ge(a["route"], a.count("route", t + 1))
                    dve.max(top[:, t, :], MD[:, 2 * P:2 * P + E]).then_inc(a["top"], 1)
                t = i - 6
                if 0 <= t < NT:
                    s = t % 2
                    dve.bn_stats(stD[s], x[:, t, :]).then_inc(a["bnD"], 1)
                t = i - 7
                if 0 <= t < NT:
                    s = t % 2
                    dve.wait_ge(a["top"], a.count("top", t + 1))
                    dve.max_index(topi[s], top[:, t, :], MD[:, 2 * P:2 * P + E]).then_inc(a["topi"], 1)
                t = i - 6
                if 0 <= t < NT:
                    s = t % 2
                    dve.wait_ge(a["bnD"], a.count("bnD", t + 1))
                    dve.bn_aggr(mvD[s], stD[s]).then_inc(a["mvD"], 1)
                t = i - 7
                if 0 <= t < NT:
                    s = t % 2
                    dve.wait_ge(a["topi"], a.count("topi", t + 1))
                    dve.tensor_tensor(oh[s], iota8[:, :].unsqueeze(1).to_broadcast([P, 2, E]),
                                      topi[s][:, 0:2].unsqueeze(2).to_broadcast([P, 2, E]), ALU.is_equal).then_inc(a["oh"], 1)
                t = i - 4
                if 0 <= t < NT:
                    s = t % 2
                    dve.tensor_tensor(prob[s][:, 0:2 * HB * KEYS].rearrange("p (b h k) -> p b h k", b=2, h=HB), S01,
                                      mx[s][:, 0:2 * HB].rearrange("p (b h) -> p b h", b=2).unsqueeze(3).to_broadcast([P, 2, HB, KEYS]), ALU.subtract)
                    dve.tensor_tensor(prob[s][:, 2 * HB * KEYS:HK].rearrange("p (h k) -> p h k", k=KEYS), S2,
                                      mx[s][:, 2 * HB:H].unsqueeze(2).to_broadcast([P, H - 2 * HB, KEYS]), ALU.subtract).then_inc(a["sub"], 1)
                t = i - 7
                if 0 <= t < NT:
                    s = t % 2
                    dve.wait_ge(a["oh"], a.count("oh", t + 1))
                    dve.tensor_tensor(picks[s], oh[s][:, 0, :], oh[s][:, 1, :], ALU.add).then_inc(a["picks"], 1)
                t = i - 6
                if 0 <= t < NT:
                    s = t % 2
                    dve.wait_ge(a["mvD"], a.count("mvD", t + 1))
                    dve.tensor_scalar(veD[s], mvD[s][:, 1:2], EPS, None, ALU.add).then_inc(a["veD"], 1)
                t = i - 7
                if 0 <= t < NT:
                    s = t % 2
                    dve.wait_ge(a["picks"], a.count("picks", t + 1))
                    dve.tensor_tensor(before[1 - s], before[s], picks[s], ALU.add).then_inc(a["bef"], 1)
                t = i - 6
                if 0 <= t < NT:
                    s = t % 2
                    if t >= 2:
                        dve.wait_ge(sent[s], sent_count(0, t - 2))
                    dve.tensor_copy(pay[s][:, :, D:ROW].bitcast(I32), dest[:, t, :].unsqueeze(2))
                t = i - 7
                if 0 <= t < NT:
                    s = t % 2
                    dve.wait_ge(a["rank"], a.count("rank", t + 1))
                    dve.tensor_tensor(rsel[s], oh[s], RANK.unsqueeze(1).to_broadcast([P, 2, E]), ALU.mult).then_inc(a["rsel"], 1)
                t = i - 5
                if 0 <= t < NT:
                    s = t % 2
                    dve.wait_ge(a["AV"], a.count("AV", t + 1))
                    dve.reciprocal(rden[s], AV0[:, :, HD0]).then_inc(a["rden"], 1)
                t = i - 7
                if 0 <= t < NT:
                    s = t % 2
                    dve.wait_ge(a["rsel"], a.count("rsel", t + 1))
                    dve.reduce_sum(slotf[s], rsel[s], AX).then_inc(a["slotf"], 1)
                t = i - 5
                if 0 <= t < NT:
                    s = t % 2
                    dve.wait_ge(a["rden"], a.count("rden", t + 1))
                    dve.tensor_tensor(on[s].rearrange("p (h d) -> p h d", h=H), AV0[:, :, 0:HD0],
                                      rden[s].unsqueeze(2).to_broadcast([P, H, HD0]), ALU.mult).then_inc(a["on"], 1)
                t = i - 7
                if 0 <= t < NT:
                    s = t % 2
                    dve.wait_ge(a["slotf"], a.count("slotf", t + 1))
                    dve.tensor_copy(slot[s], slotf[s]).then_inc(a["slot"], 1)

            def step1(i):
                a = A[1]
                t = i - 7
                if 0 <= t < NT:
                    s = t % 2
                    dve.wait_ge(a["rsel"], a.count("rsel", t + 1))
                    dve.reduce_sum(slotf[s], rsel[s], AX).then_inc(a["slotf"], 1)
                    dve.tensor_copy(pay[s][:, :, D:ROW].bitcast(I32), dest[:, t, :].unsqueeze(2))
                t = i - 4
                if 0 <= t < NT:
                    s = t % 2
                    dve.wait_ge(a["ffh"], a.count("ffh", t + 1))
                    dve.scalar_tensor_tensor(ffbuf[s], ffbuf[s], 0.5, MA[:, :], ALU.mult, ALU.mult).then_inc(a["fo"], 1)
                t = i - 3
                if 0 <= t < NT:
                    s = t % 2
                    dve.wait_ge(a["S"], a.count("S", t + 1))
                    dve.reduce_max(mx[s][:, 0:2 * HB].rearrange("p (b h) -> p b h", b=2), S01, AX)
                    dve.reduce_max(mx[s][:, 2 * HB:H], S2, AX).then_inc(a["mx"], 1)
                t = i - 7
                if 0 <= t < NT:
                    s = t % 2
                    dve.wait_ge(a["slotf"], a.count("slotf", t + 1))
                    dve.tensor_copy(slot[s], slotf[s]).then_inc(a["slot"], 1)
                t = i - 3
                if 0 <= t < NT:
                    s = t % 2
                    dve.wait_ge(a["mx"], a.count("mx", t + 1))
                    dve.tensor_tensor(prob[s][:, 0:2 * HB * KEYS].rearrange("p (b h k) -> p b h k", b=2, h=HB), S01,
                                      mx[s][:, 0:2 * HB].rearrange("p (b h) -> p b h", b=2).unsqueeze(3).to_broadcast([P, 2, HB, KEYS]), ALU.subtract)
                    dve.tensor_tensor(prob[s][:, 2 * HB * KEYS:HK].rearrange("p (h k) -> p h k", k=KEYS), S2,
                                      mx[s][:, 2 * HB:H].unsqueeze(2).to_broadcast([P, H - 2 * HB, KEYS]), ALU.subtract).then_inc(a["sub"], 1)
                t = i - 5
                if 0 <= t < NT:
                    s = t % 2
                    dve.wait_ge(a["AV"], a.count("AV", t + 1))
                    dve.tensor_tensor(x[:, t, :], x[:, t, :], MC[:, 0:D], ALU.add).then_inc(a["xa"], 1)
                t = i - 1
                if 0 <= t < NT:
                    s = t % 2
                    dve.wait_ge(a["comb"], a.count("comb", t + 1))
                    dve.bn_stats(stA[s], x[:, t, :]).then_inc(a["bnA"], 1)
                t = i - 6
                if 0 <= t < NT:
                    s = t % 2
                    dve.wait_ge(a["route"], a.count("route", t + 1))
                    dve.max(top[:, t, :], MD[:, 2 * P:2 * P + E]).then_inc(a["top"], 1)
                t = i - 5
                if 0 <= t < NT:
                    s = t % 2
                    dve.wait_ge(a["xa"], a.count("xa", t + 1))
                    dve.bn_stats(stD[s], x[:, t, :]).then_inc(a["bnD"], 1)
                t = i - 6
                if 0 <= t < NT:
                    s = t % 2
                    dve.wait_ge(a["top"], a.count("top", t + 1))
                    dve.max_index(topi[s], top[:, t, :], MD[:, 2 * P:2 * P + E]).then_inc(a["topi"], 1)
                t = i - 2
                if 0 <= t < NT:
                    s = t % 2
                    dve.wait_ge(a["th"], a.count("th", t + 1))
                    dve.scalar_tensor_tensor(ffbuf[s], ffbuf[s], 1.0, MA[:, :], ALU.add, ALU.mult).then_inc(a["gg"], 1)
                t = i - 5
                if 0 <= t < NT:
                    s = t % 2
                    dve.wait_ge(a["bnD"], a.count("bnD", t + 1))
                    dve.bn_aggr(mvD[s], stD[s]).then_inc(a["mvD"], 1)
                t = i - 6
                if 0 <= t < NT:
                    s = t % 2
                    dve.wait_ge(a["topi"], a.count("topi", t + 1))
                    dve.tensor_tensor(oh[s], iota8[:, :].unsqueeze(1).to_broadcast([P, 2, E]),
                                      topi[s][:, 0:2].unsqueeze(2).to_broadcast([P, 2, E]), ALU.is_equal).then_inc(a["oh"], 1)
                t = i - 5
                if 0 <= t < NT:
                    s = t % 2
                    dve.wait_ge(a["mvD"], a.count("mvD", t + 1))
                    dve.tensor_scalar(veD[s], mvD[s][:, 1:2], EPS, None, ALU.add).then_inc(a["veD"], 1)
                t = i - 1
                if 0 <= t < NT:
                    s = t % 2
                    dve.wait_ge(a["bnA"], a.count("bnA", t + 1))
                    dve.bn_aggr(mvA[s], stA[s]).then_inc(a["mvA"], 1)
                t = i - 7
                if 0 <= t < NT:
                    s = t % 2
                    dve.tensor_tensor(before[1 - s], before[s], picks[s], ALU.add).then_inc(a["bef"], 1)
                t = i - 6
                if 0 <= t < NT:
                    s = t % 2
                    dve.wait_ge(a["oh"], a.count("oh", t + 1))
                    dve.tensor_tensor(picks[s], oh[s][:, 0, :], oh[s][:, 1, :], ALU.add).then_inc(a["picks"], 1)
                t = i - 1
                if 0 <= t < NT:
                    s = t % 2
                    dve.wait_ge(a["mvA"], a.count("mvA", t + 1))
                    dve.tensor_scalar(veA[s], mvA[s][:, 1:2], 1.0 + EPS, EPS * EPS, ALU.mult, ALU.add).then_inc(a["veA"], 1)
                t = i - 3
                if 0 <= t < NT:
                    s = t % 2
                    dve.wait_ge(a["exp"], a.count("exp", t + 1))
                    dve.reduce_sum(den[s], prob[s][:, 0:HK].rearrange("p (h k) -> p h k", h=H), AX).then_inc(a["den"], 1)
                t = i
                if 0 <= t < NT:
                    s = t % 2
                    dve.wait_ge(y_in[t % 4], 16 * (t // 4 + 1))
                    dve.scalar_tensor_tensor(yb[t % 4][:, 0, :], yb[t % 4][:, 0, :], gate[:, 0, t:t + 1], x[:, t, :], ALU.mult, ALU.add).then_inc(a["c1"], 1)
                t = i - 3
                if 0 <= t < NT:
                    s = t % 2
                    dve.wait_ge(a["den"], a.count("den", t + 1))
                    dve.reciprocal(rden[s], den[s]).then_inc(a["rden"], 1)
                t = i - 6
                if 0 <= t < NT:
                    s = t % 2
                    dve.wait_ge(a["rank"], a.count("rank", t + 1))
                    dve.tensor_tensor(rsel[s], oh[s], RANK.unsqueeze(1).to_broadcast([P, 2, E]), ALU.mult).then_inc(a["rsel"], 1)
                t = i
                if 0 <= t < NT:
                    s = t % 2
                    dve.wait_ge(a["c1"], a.count("c1", t + 1))
                    dve.scalar_tensor_tensor(x[:, t, :], yb[t % 4][:, 1, :], gate[:, 1, t:t + 1], yb[t % 4][:, 0, :], ALU.mult, ALU.add).then_inc(a["comb"], 1)
                t = i - 5
                if 0 <= t < NT:
                    s = t % 2
                    dve.wait_ge(a["rsD"], a.count("rsD", t + 1))
                    if t >= 2:
                        dve.wait_ge(sent[s], sent_count(1, t - 2))
                    dve.tensor_scalar(pay[s][:, :, 0:D], x[:, t, :].unsqueeze(1).to_broadcast([P, 2, D]),
                                      mvD[s][:, 0:1], rsD[s], ALU.subtract, ALU.mult).then_inc(a["xnD"], 1)

            def schedule(l):
                m = M[l]
                dve.wait_ge(A[l]["top"], A[l].count("top", NT))
                dve.tensor_tensor(margin[:, :], top[:, :, 1], top[:, :, 0], ALU.subtract).then_inc(m["margin"], 1)
                dve.wait_ge(m["cnt"], m.count("cnt", 1))
                dve.tensor_scalar(cnt_i[:, :], MD[0:1, 2 * P + E:2 * P + 2 * E], float(P - 1), None, ALU.add).then_inc(m["plan"], 1)
                dve.wait_ge(m["plan"], m.count("plan", 1))
                dve.tensor_scalar(cnt_s[:, :], cnt_i[:, :], 7, None, ALU.arith_shift_right).then_inc(m["plan"], 1)
                dve.wait_ge(m["plan"], m.count("plan", 2))
                dve.tensor_copy(ntile[:, :], cnt_s[:, :]).then_inc(m["plan"], 1)
                dve.wait_ge(m["plan"], m.count("plan", 3))
                dve.tensor_scalar(wgt[:, :], ntile[:, :], -float(P), float(REGION), ALU.mult, ALU.add).then_inc(m["plan"], 1)
                dve.tensor_tensor_scan(cum[:, :], ones1[:, :], ntile[:, :], 0.0, ALU.mult, ALU.add).then_inc(m["plan"], 1)
                dve.wait_ge(m["plan"], m.count("plan", 5))
                dve.tensor_tensor(ind[:, :, :], jidx[:, :].unsqueeze(2).to_broadcast([1, NJ, E - 1]),
                                  cum[:, 0:E - 1].unsqueeze(1).to_broadcast([1, NJ, E - 1]), ALU.is_ge).then_inc(m["plan"], 1)
                dve.wait_ge(m["plan"], m.count("plan", 6))
                dve.reduce_sum(ef[:, :], ind[:, :, :], AX)
                dve.tensor_tensor(ind2[:, :, :], ind[:, :, :], wgt[:, 0:E - 1].unsqueeze(1).to_broadcast([1, NJ, E - 1]), ALU.mult).then_inc(m["plan"], 1)
                dve.wait_ge(m["plan"], m.count("plan", 7))
                dve.reduce_sum(rf[:, :], ind2[:, :, :], AX).then_inc(m["plan"], 1)
                dve.wait_ge(m["plan"], m.count("plan", 8))
                dve.scalar_tensor_tensor(rf2[:, :], jidx[:, :], float(P), rf[:, :], ALU.mult, ALU.add).then_inc(m["plan"], 1)
                dve.wait_ge(m["plan"], m.count("plan", 9))
                dve.tensor_copy(sched[l][:, 0, :], ef[:, :])
                dve.tensor_copy(sched[l][:, 1, :], rf2[:, :]).then_inc(m["sched"], 1)
                dve.wait_ge(m["g1"], m.count("g1", 1))
                dve.tensor_scalar(gtmp[:, 1, :], gtmp[:, 0, :], 1.0, None, ALU.add).then_inc(m["gates"], 1)
                dve.wait_ge(m["gates"], m.count("gates", 1))
                dve.reciprocal(gate[:, 0, :], gtmp[:, 1, :]).then_inc(m["gates"], 1)
                dve.wait_ge(m["gates"], m.count("gates", 2))
                dve.tensor_tensor(gate[:, 1, :], gtmp[:, 0, :], gate[:, 0, :], ALU.mult).then_inc(m["gates"], 1)

            def moe(l):
                m = M[l]
                for j in range(NJ + 3):
                    t = j - 1
                    if 0 <= t < NJ:
                        s = t % 2
                        if l == 0:
                            dve.wait_ge(m["act1"], m.count("act1", t + 1))
                            dve.tensor_tensor(ha[s][:, 0:F0], ha[s][:, 0:F0], S[s][:, F0:2 * F0], ALU.mult).then_inc(m["act2"], 1)
                        else:
                            if t == 0:
                                dve.wait_ge(ld["moe1"], 64)
                            dve.wait_ge(m["up"], m.count("up", t + 1))
                            if t >= 2:
                                dve.wait_ge(m["Th"], m.count("Th", t - 1))
                            e = dve.value_load(sched[l][0:1, 0, at(t)], min_val=0, max_val=E - 1)
                            dve.tensor_tensor(ha[s], S[s][:, :], b1bc[:, e, :], ALU.add).then_inc(m["act1"], 1)
                    t = j - 3
                    if 0 <= t < NJ:
                        s = t % 2
                        dve.wait_ge(m["down"], m.count("down", t + 1))
                        if t >= 2:
                            dve.wait_ge(sentb[(t - 2) % XB], sentb_count(l, t - 2))
                        src = (MC, MD)[s][:, 0:D]
                        if l == 0:
                            dve.tensor_copy(ysb[s], src).then_inc(m["y"], 1)
                        else:
                            e = dve.value_load(sched[l][0:1, 0, at(t)], min_val=0, max_val=E - 1)
                            dve.tensor_tensor(ysb[s], src, b2bc[:, e, :], ALU.add).then_inc(m["y"], 1)

            for l in range(2):
                if l == 1:
                    dve.wait_ge(M[0]["gates"], M[0].count("gates", 3))
                    dve.memset(before[0], 0.0).then_inc(M[0]["zero"], 1)
                    dve.wait_ge(M[0]["zero"], M[0].count("zero", 1))
                    dve.wait_ge(ld["l1b"], 16 * 4)
                for i in range(NT + LAG[l]):
                    step0(i) if l == 0 else step1(i)
                schedule(l)
                if l == 0:
                    for b in range(NBATCH):
                        dve.bn_stats(cstat[:, b, :], ctx_sb[:, b, :]).then_inc(pro1["cbn"], 1)
                    for b in range(NBATCH):
                        dve.wait_ge(pro1["cbn"], pro1.count("cbn", b + 1))
                        dve.bn_aggr(cmv[:, b, :], cstat[:, b, :]).then_inc(pro1["cmv"], 1)
                    dve.wait_ge(pro1["cmv"], pro1.count("cmv", NBATCH))
                    dve.tensor_scalar(cve[:, :], cmv[:, :, 1], EPS, None, ALU.add).then_inc(pro1["cve"], 1)
                    dve.wait_ge(pro1["crs"], pro1.count("crs", 1))
                    for b in range(NBATCH):
                        dve.tensor_scalar(cn[:, b, :], ctx_sb[:, b, :], cmv[:, b, 0:1], crs[:, b:b + 1],
                                          ALU.subtract, ALU.mult).then_inc(pro1["cn"], 1)
                    dve.wait_ge(A[0]["AV"], A[0].count("AV", NT))
                    for h in range(H):
                        dve.wait_ge(pro1["fv"], pro1.count("fv", h + 1))
                        dve.tensor_copy(pp[:, :, h * KEYS:(h + 1) * KEYS],
                                        (S[2], MD)[h % 2][:, 0:NBATCH * KEYS].rearrange("p (b k) -> p b k", b=NBATCH)).then_inc(pro1["foldT"], 1)
                moe(l)
            m = M[1]
            dve.wait_ge(m["gates"], m.count("gates", 3))
            for t in range(NT):
                dve.wait_ge(y_in[t % 4], 16 * (NT // 4 + t // 4 + 1))
                dve.scalar_tensor_tensor(yb[t % 4][:, 0, :], yb[t % 4][:, 0, :], gate[:, 0, t:t + 1], x[:, t, :], ALU.mult, ALU.add).then_inc(m["fin0"], 1)
                dve.wait_ge(m["fin0"], m.count("fin0", t + 1))
                dve.scalar_tensor_tensor(x[:, t, :], yb[t % 4][:, 1, :], gate[:, 1, t:t + 1], yb[t % 4][:, 0, :], ALU.mult, ALU.add).then_inc(m["fin"], 1)

        @block.tensor
        def _(pe):
            mm = nc.tensor.matmul
            tr = nc.tensor.transpose
            pe.wait_ge(const, NCONST)
            pe.wait_ge(ld["ctx"], 48)
            for b in range(NBATCH):
                ins = tr(MD[:, b * KEYS:(b + 1) * KEYS], ctx_sb[:, b, :], ident[0:KEYS, 0:KEYS])
            ins.then_inc(pro["ctxT"], 1)
            pe.wait_ge(pro["ctxTs"], pro.count("ctxTs", 1))
            for b in range(NBATCH):
                ins = mm(MC[0:KEYS, b * D:(b + 1) * D], ctxT[:, b * KEYS:(b + 1) * KEYS], wk0[:, :], start=True, stop=True)
            ins.then_inc(pro["k"], 1)
            mm(MA[:, 0:NBATCH * KEYS], wv0[:, :], ctxT[:, :], start=True, stop=True).then_inc(pro["v"], 1)
            pe.wait_ge(pro["klo"], pro.count("klo", 1))
            for b in range(NBATCH):
                dst = (S + [TP[0]])[b]
                for g in range(NG):
                    n = b * NG + g
                    src = k0split[:, n // 8].rearrange("k r s w d -> k (r s w d)")[:, (n % 8) * P:(n % 8 + 1) * P]
                    ins = tr(dst[:, g * KEYS:(g + 1) * KEYS], src, ident[0:KEYS, 0:KEYS])
                ins.then_inc(pro["kT"], 1)
            pe.wait_ge(pro["keys0"], pro.count("keys0", NBATCH))
            for n in range(NBATCH * 3):
                b, g = n // 3, n % 3
                pe.wait_ge(pro["vblk"], pro.count("vblk", b + 1))
                if n >= 2:
                    pe.wait_ge(pro["vals0"], pro.count("vals0", n - 1))
                for c in range(4 * g, min(4 * g + 4, CH)):
                    tr(TP[n % 2][:, (c - 4 * g) * P:(c - 4 * g + 1) * P], vblk[b % 2][:, c * P:(c + 1) * P], ident[:, :]).then_inc(pro["vtp"], 1)
            pe.wait_ge(ld["q"], 48)
            pe.wait_ge(ld["o"], 48)
            pe.wait_ge(pro["identr"], pro.count("identr", 1))
            pe.wait_ge(pro["blo"], pro.count("blo", TPB))

            def step0(i):
                a = A[0]
                t = i - 4
                if 0 <= t < NT:
                    s = t % 2
                    pe.wait_ge(a["qT"], a.count("qT", t + 1))
                    if t >= 1:
                        pe.wait_ge(a["sub"], a.count("sub", t))
                    b, tt = t // TPB, t % TPB
                    for bank, (h0, n) in enumerate(zip(BANK_AT, BANK_HEADS)):
                        for half in range(2):
                            for o in range(0, n * KEYS, GK):
                                w = min(GK, n * KEYS - o)
                                mm(S[bank][:, o:o + w], ident_r[:, :], bias_r[:, half, tt, 0:w], start=half == 0 and o == 0, stop=False)
                        for g, h, e in BANK_PARTS[bank]:
                            ins = mm(S[bank][:, (h - h0) * KEYS:(e - h0) * KEYS], qT[s][:, g * P:(g + 1) * P],
                                     keys0[:, b, h * KEYS:e * KEYS], start=False, stop=e == h0 + n)
                    ins.then_inc(a["S"], 1)
                t = i - 6
                if 0 <= t < NT:
                    s = t % 2
                    pe.wait_ge(a["on"], a.count("on", t + 1))
                    tr(MC[:, 2 * P:3 * P], on[s], ident[:, :]).then_inc(a["To"], 1)
                t = i - 1
                if 0 <= t < NT:
                    s = t % 2
                    pe.wait_ge(a["xnA"], a.count("xnA", t + 1))
                    if t >= 1:
                        pe.wait_ge(a["qb"], a.count("qb", t))
                    tr(MA[:, 0:P], xnA[s], ident[:, :]).then_inc(a["TxA"], 1)
                t = i - 7
                if 0 <= t < NT:
                    s = t % 2
                    pe.wait_ge(a["xnD"], a.count("xnD", t + 1))
                    tr(MD[:, P:2 * P], pay[s][:, 0, 0:D], ident[:, :]).then_inc(a["Tx2"], 1)
                t = i - 5
                if 0 <= t < NT:
                    s = t % 2
                    pe.wait_ge(a["exp"], a.count("exp", t + 1))
                    for c in range(4):
                        ins = tr(TP[0][:, c * P:(c + 1) * P], prob[s][:, c * P:(c + 1) * P], ident[:, :])
                    ins.then_inc(a["TP0"], 1)
                    for c in range(4, 8):
                        ins = tr(TP[1][:, (c - 4) * P:(c - 3) * P], prob[s][:, c * P:(c + 1) * P], ident[:, :])
                    ins.then_inc(a["TP1"], 1)
                t = i - 6
                if 0 <= t < NT:
                    s = t % 2
                    pe.wait_ge(a["oT"], a.count("oT", t + 1))
                    if t >= 1:
                        pe.wait_ge(a["x2T"], a.count("x2T", t))
                    mm(MD[:, 0:D], ones_f[0:1, :], bo_bc[0:1, :], start=True, stop=False)
                    mm(MD[:, 0:D], oT[s], wo0[:, :], start=False, stop=True).then_inc(a["Wo"], 1)
                t = i - 1
                if 0 <= t < NT:
                    s = t % 2
                    pe.wait_ge(a["xT"], a.count("xT", t + 1))
                    mm(MA[:, P:2 * P], ones_f[0:1, :], bq_bc[0:1, :], start=True, stop=False)
                    mm(MA[:, P:2 * P], xT[s], wq0[:, :], start=False, stop=True).then_inc(a["q"], 1)
                t = i - 5
                if 0 <= t < NT:
                    s = t % 2
                    pe.wait_ge(a["PT0"], a.count("PT0", t + 1))
                    for c in range(8, CH):
                        ins = tr(TP[0][:, (c - 8) * P:(c - 7) * P], prob[s][:, c * P:(c + 1) * P], ident[:, :])
                    ins.then_inc(a["TP2"], 1)
                t = i - 3
                if 0 <= t < NT:
                    s = t % 2
                    pe.wait_ge(a["qb"], a.count("qb", min(t + 3, NT)))
                    pe.wait_ge(a["lo"], a.count("lo", t + 1))
                    halves = qsplit[s].rearrange("p h a b d -> p (h a b d)")
                    for g in range(NG):
                        ins = tr(MA[:, g * P:(g + 1) * P], halves[:, g * P:(g + 1) * P], ident[:, :])
                    ins.then_inc(a["Tq"], 1)
                t = i - 7
                if 0 <= t < NT:
                    s = t % 2
                    pe.wait_ge(a["xa"], a.count("xa", min(t + 2, NT)))
                    pe.wait_ge(a["x2T"], a.count("x2T", t + 1))
                    mm(MD[:, 2 * P:2 * P + E], x2T[s], wr[0][:, :], start=True, stop=True).then_inc(a["route"], 1)
                t = i - 5
                if 0 <= t < NT:
                    s = t % 2
                    pe.wait_ge(a["PT2"], a.count("PT2", t + 1))
                    for c in range(CH):
                        ins = mm(MC[:, 0:H * VW], probT[s][:, c * P:(c + 1) * P],
                                 vals0[:, t // TPB, c, :, :].rearrange("p h v -> p (h v)"), start=c == 0, stop=c == CH - 1)
                    ins.then_inc(a["AV"], 1)
                t = i - 7
                if 0 <= t < NT:
                    s = t % 2
                    pe.wait_ge(a["picks"], a.count("picks", t + 1))
                    mm(RANK, upper[:, :], picks[s], start=True, stop=False)
                    mm(RANK, ones_b[:, :], before[s], start=False, stop=False)
                    mm(RANK, ones_b[0:1, :], ebase_b[0:1, :], start=False, stop=True).then_inc(a["rank"], 1)

            def step1(i):
                a = A[1]
                t = i - 7
                if 0 <= t < NT:
                    s = t % 2
                    pe.wait_ge(a["xnD"], a.count("xnD", t + 1))
                    tr(MD[:, P:2 * P], pay[s][:, 0, 0:D], ident[:, :]).then_inc(a["Tx2"], 1)
                t = i - 5
                if 0 <= t < NT:
                    s = t % 2
                    pe.wait_ge(a["norm"], a.count("norm", t + 1))
                    for c in range(4):
                        ins = tr(TP[0][:, c * P:(c + 1) * P], prob[s][:, c * P:(c + 1) * P], ident[:, :])
                    ins.then_inc(a["TP0"], 1)
                t = i - 3
                if 0 <= t < NT:
                    s = t % 2
                    pe.wait_ge(a["xT"], a.count("xT", t + 1))
                    mm(MA[:, :], xT[s], wff1[:, FF:2 * FF], start=True, stop=True).then_inc(a["ffg"], 1)
                t = i - 5
                if 0 <= t < NT:
                    s = t % 2
                    pe.wait_ge(a["gT"], a.count("gT", t + 1))
                    for c in range(4, 8):
                        ins = tr(TP[1][:, (c - 4) * P:(c - 3) * P], prob[s][:, c * P:(c + 1) * P], ident[:, :])
                    ins.then_inc(a["TP1"], 1)
                t = i - 7
                if 0 <= t < NT:
                    s = t % 2
                    pe.wait_ge(a["x2T"], a.count("x2T", t + 1))
                    mm(MD[:, 2 * P:2 * P + E], ones_f[0:1, :], br_bc[0:1, :], start=True, stop=False)
                    mm(MD[:, 2 * P:2 * P + E], x2T[s], wr[1][:, :], start=False, stop=True).then_inc(a["route"], 1)
                t = i - 3
                if 0 <= t < NT:
                    s = t % 2
                    if t >= 1:
                        pe.wait_ge(a["sub"], a.count("sub", t))
                    for bank, (h0, n) in enumerate(zip(BANK_AT, BANK_HEADS)):
                        ins = mm(S[bank][:, 0:n * KEYS], xT[s], keys1[:, t // TPB, h0 * KEYS:(h0 + n) * KEYS], start=True, stop=True)
                    ins.then_inc(a["S"], 1)
                t = i - 5
                if 0 <= t < NT:
                    s = t % 2
                    pe.wait_ge(a["PT0"], a.count("PT0", t + 1))
                    for c in range(8, CH):
                        ins = tr(TP[0][:, (c - 8) * P:(c - 7) * P], prob[s][:, c * P:(c + 1) * P], ident[:, :])
                    ins.then_inc(a["TP2"], 1)
                t = i - 7
                if 0 <= t < NT:
                    s = t % 2
                    pe.wait_ge(a["picks"], a.count("picks", t + 1))
                    mm(RANK, upper[:, :], picks[s], start=True, stop=False)
                    mm(RANK, ones_b[:, :], before[s], start=False, stop=False)
                    mm(RANK, ones_b[0:1, :], ebase_b[0:1, :], start=False, stop=True).then_inc(a["rank"], 1)
                t = i - 4
                if 0 <= t < NT:
                    s = t % 2
                    pe.wait_ge(a["gg"], a.count("gg", min(t + 2, NT)))
                    mm(MA[:, :], xT[s], wff1[:, 0:FF], start=True, stop=True).then_inc(a["ffh"], 1)
                t = i - 5
                if 0 <= t < NT:
                    s = t % 2
                    pe.wait_ge(a["PT2"], a.count("PT2", t + 1))
                    for c in range(CH):
                        mm(MC[:, 0:D], probT[s][:, c * P:(c + 1) * P], vals1[:, t // TPB, c, :], start=c == 0, stop=False)
                    for k in range(FF // P):
                        ins = mm(MC[:, 0:D], gT[s][:, k * P:(k + 1) * P], wff2[:, k, :], start=False, stop=k == FF // P - 1)
                    ins.then_inc(a["AV"], 1)
                t = i - 2
                if 0 <= t < NT:
                    s = t % 2
                    pe.wait_ge(a["xnA"], a.count("xnA", t + 1))
                    if t >= 2:
                        pe.wait_ge(a["fo"], a.count("fo", t - 1))
                    tr(MA[:, 0:P], xnA[s], ident[:, :]).then_inc(a["TxA"], 1)
                t = i - 4
                if 0 <= t < NT:
                    s = t % 2
                    pe.wait_ge(a["fo"], a.count("fo", t + 1))
                    for k in range(FF // P):
                        ins = tr(TP[1][:, k * P:(k + 1) * P], ffbuf[s][:, k * P:(k + 1) * P], ident[:, :])
                    ins.then_inc(a["Tg"], 1)

            def moe(l):
                m = M[l]
                up = w13 if l == 0 else w1b
                w2 = w2a if l == 0 else w2b
                nk = (F0 if l == 0 else F1) // P
                if l == 0:
                    pe.wait_ge(ld["moe0"], 48)
                else:
                    pe.wait_ge(ld["moe1"], 64)
                pe.wait_ge(m["sched"], m.count("sched", 1))
                for j in range(NJ + 3):
                    if j < NJ:
                        pe.wait_ge(xs_in[j % XB], 16 * ((NJ // XB) * l + j // XB + 1))
                        if j >= 1:
                            pe.wait_ge(m["xsT"], m.count("xsT", j))
                        tr(MA[:, 0:P], xs[j % XB][:, 0:D], ident[:, :]).then_inc(m["Tx"], 1)
                    t = j - 1
                    if 0 <= t < NJ:
                        s = t % 2
                        e = pe.value_load(sched[l][0:1, 0, at(t)], min_val=0, max_val=E - 1)
                        pe.wait_ge(m["xsT"], m.count("xsT", t + 1))
                        if t >= 2:
                            pe.wait_ge(m["act2" if l == 0 else "act1"], m.count("act2" if l == 0 else "act1", t - 1))
                        mm(S[s][:, :], xsT[s], up[:, e, :], start=True, stop=True).then_inc(m["up"], 1)
                    t = j - 3
                    if 0 <= t < NJ:
                        s = t % 2
                        e = pe.value_load(sched[l][0:1, 0, at(t)], min_val=0, max_val=E - 1)
                        pe.wait_ge(m["hT"], m.count("hT", t + 1))
                        if t >= 2:
                            pe.wait_ge(m["y"], m.count("y", t - 1))
                        for k in range(nk):
                            ins = mm((MC, MD)[s][:, 0:D], hT[s][:, k * P:(k + 1) * P], w2[:, e, k, :], start=k == 0, stop=k == nk - 1)
                        ins.then_inc(m["down"], 1)
                    t = j - 2
                    if 0 <= t < NJ:
                        s = t % 2
                        pe.wait_ge(m["act2"], m.count("act2", t + 1))
                        if t >= 2:
                            pe.wait_ge(m["hT"], m.count("hT", t - 1))
                        for k in range(nk):
                            ins = tr(TP[s][:, k * P:(k + 1) * P], ha[s][:, k * P:(k + 1) * P], ident[:, :])
                        ins.then_inc(m["Th"], 1)

            for l in range(2):
                for i in range(NT + LAG[l]):
                    step0(i) if l == 0 else step1(i)
                pe.wait_ge(A[l]["rsel"], A[l].count("rsel", NT))
                pe.wait_ge(A[l]["bef"], A[l].count("bef", NT))
                mm(RANK, ones_b[:, :], before[NT % 2], start=True, stop=True).then_inc(M[l]["cnt"], 1)
                if l == 0:
                    pe.wait_ge(M[0]["plan"], M[0].count("plan", 1))
                    pe.wait_ge(pro1["cn"], pro1.count("cn", NBATCH))
                    for b in range(NBATCH):
                        ins = tr(MD[:, b * KEYS:(b + 1) * KEYS], cn[:, b, :], ident[0:KEYS, 0:KEYS])
                    ins.then_inc(pro1["cT"], 1)
                    pe.wait_ge(ld["l1"], 160)
                    for g in range(2):
                        for k in range(4):
                            ins = tr(TP[g][:, k * P:(k + 1) * P], wq1[:, (4 * g + k) * P:(4 * g + k + 1) * P], ident[:, :])
                        ins.then_inc(pro1["wqT"], 1)
                    pe.wait_ge(pro1["cTs"], pro1.count("cTs", 1))
                    mm(MA[:, 0:NBATCH * KEYS], wkk[:, :, :].rearrange("p r d -> p (r d)"), ctxT[:, :], start=True, stop=True).then_inc(pro1["kv1"], 1)
                    mm(MC[:, 0:NBATCH * KEYS], wvv[:, :, :].rearrange("p r d -> p (r d)"), ctxT[:, :], start=True, stop=True).then_inc(pro1["kv1"], 1)
                    pe.wait_ge(pro1["wqTs"], pro1.count("wqTs", 2))
                    pe.wait_ge(pro1["kT1"], pro1.count("kT1", 1))
                    pe.wait_ge(pro1["vT1"], pro1.count("vT1", 1))
                    for h in range(H):
                        r = HD1 * (h % 2)
                        if h >= 2:
                            pe.wait_ge(pro1["keys1"], pro1.count("keys1", h - 1))
                        mm(S[h % 2][:, 0:NBATCH * KEYS], wq1T[r:r + HD1, h // 2, :], kT1[r:r + HD1, :], start=True, stop=True).then_inc(pro1["fk"], 1)
                        if h >= 2:
                            pe.wait_ge(pro1["foldT"], pro1.count("foldT", h - 1))
                        mm((S[2], MD)[h % 2][:, 0:NBATCH * KEYS], wo1[r:r + HD1, h // 2, :], vT1[r:r + HD1, :], start=True, stop=True).then_inc(pro1["fv"], 1)
                    pe.wait_ge(pro1["foldT"], pro1.count("foldT", H))
                    for n in range(NBATCH * 3):
                        b, g = n // 3, n % 3
                        if n >= 2:
                            pe.wait_ge(pro1["vals1"], pro1.count("vals1", n - 1))
                        for c in range(4 * g, min(4 * g + 4, CH)):
                            ins = tr(TP[n % 2][:, (c - 4 * g) * P:(c - 4 * g + 1) * P], foldT[b][:, c * P:(c + 1) * P], ident[:, :])
                        ins.then_inc(pro1["fT"], 1)
                    pe.wait_ge(pro1["vals1"], pro1.count("vals1", 3 * NBATCH))
                moe(l)


_INS = ['x', 'ctx_1024', 'fside_SxS2_0', 'L0_xattn_Wq', 'L0_xattn_bq', 'L0_xattn_Wk', 'L0_xattn_Wv', 'L0_xattn_Wo',
        'L0_xattn_bo', 'L0_xattn_scale_mul_log', 'L0_ffn_Wr', 'L0_ffn_W1', 'L0_ffn_W2', 'L0_ffn_W3', 'L1_xattn_ln_g',
        'L1_xattn_ln_b', 'L1_xattn_cln_g', 'L1_xattn_cln_b', 'L1_xattn_Wq', 'L1_xattn_Wkv', 'L1_xattn_Wo',
        'L1_xattn_Wff1', 'L1_xattn_Wff2', 'L1_ffn_W1', 'L1_ffn_b1', 'L1_ffn_W2', 'L1_ffn_b2', 'L1_ffn_Wr', 'L1_ffn_br']


def kernel(**inputs):
    import numpy as _np
    import concourse.bacc as _bacc
    from concourse import mybir as _mybir
    from concourse.bass_utils import run_bass_kernel_spmd as _run

    nc = _bacc.Bacc("TRN2", target_bir_lowering=False, num_devices=1)
    arrays, args = {}, []
    for name in _INS:
        a = _np.ascontiguousarray(inputs[name])
        arrays[f"in_{name}_dram"] = a
        args.append(nc.dram_tensor(f"in_{name}_dram", a.shape, _mybir.dt.from_np(a.dtype), kind="ExternalInput").ap())
    shape = inputs['x'].shape
    args.append(nc.dram_tensor("out_0_dram", shape, _mybir.dt.from_np(_np.dtype("float32")), kind="ExternalOutput").ap())
    bass_xattn_moe_two_layers(nc, *args)
    r = _run(nc, [arrays], core_ids=[0])
    return r.results[0]["out_0_dram"]
```

```python
from contextlib import ExitStack

import numpy as np
import concourse.bass as bass
from concourse import mybir

F32 = mybir.dt.float32
F32R = mybir.dt.float32r
BF16 = mybir.dt.bfloat16
I32 = mybir.dt.int32
U32 = mybir.dt.uint32
ACT = mybir.ActivationFunctionType
ALU = mybir.AluOpType
AX = mybir.AxisListType.X

P = 128
EPS = 1e-5
NORM_FLOOR = 1e-24
MAX_LOG_SCALE = float(np.log(100.0))
NCONST = 4


def bass_xattn_moe_two_layers(nc, x_in, ctx_in, bias_in, Wq0, bq0, Wk0, Wv0, Wo0, bo0, scale_log,
                              Wr0, W1_0, W2_0, W3_0, ln_g, ln_b, cln_g, cln_b, Wq1, Wkv1, Wo1,
                              Wff1, Wff2, W1_1, b1_1, W2_1, b2_1, Wr1, br1, out):
    NBATCH, SEQ, D = x_in.shape
    KEYS = ctx_in.shape[1]
    H = scale_log.shape[1]
    HD0 = D // H
    HD1 = Wq1.shape[1] // H
    E, _, F0 = W1_0.shape
    F1 = W1_1.shape[2]
    FF = Wff2.shape[0]
    T = NBATCH * SEQ
    NT = T // P
    TPB = SEQ // P
    HK = H * KEYS
    CH = -(-HK // P)
    HKP = CH * P
    G = 4
    NG = H // G
    GK = G * KEYS
    VW = HD0 + 1
    HB = 6
    BANK_AT = range(0, H, HB)
    BANK_HEADS = [min(HB, H - h) for h in BANK_AT]
    BANK_PARTS = [[(g, max(h, g * G), min(h + n, g * G + G)) for g in range(NG) if max(h, g * G) < min(h + n, g * G + G)]
                  for h, n in zip(BANK_AT, BANK_HEADS)]
    CHUNK_HEADS = [(c * P // KEYS, min(-(-(c + 1) * P // KEYS), H)) if c else (0, H) for c in range(CH)]
    ROW = D + 1
    NJ = 2 * T // P + E - 1
    REGION = T
    SLOTS = E * REGION + E * P
    NOWHERE = 1 << 20
    XB = 8
    assert XB == NT // 2 and D == P and H * HD0 == P and G * 4 * HD0 == P and F0 * 2 == F1 == 512 and TPB == 4 and FF == 512

    def at(i):
        return bass.ds(i, 1)

    with ExitStack() as ctx:
        def sb(name, shape, dt=F32):
            return ctx.enter_context(nc.sbuf_tensor(name, shape, dt))

        def sem(name):
            return ctx.enter_context(nc.semaphore(name))

        x = sb("x", [P, NT, D])
        with ExitStack() as early:
            def sb_early(name, shape, dt=F32):
                return early.enter_context(nc.sbuf_tensor(name, shape, dt))

            keys0 = sb_early("keys0", [P, NBATCH, HK], F32R)
            bias_r = sb_early("bias_r", [P, 2, TPB, GK], F32R)
            qT_both = sb_early("qT", [P, 2, NG * P], F32R)
        qT = [qT_both[:, 0], qT_both[:, 1]]
        w2b = sb("w2b", [P, E, F1 // P, D])
        vals1 = sb("vals1", [P, NBATCH, CH, D])
        region_a = sb("region_a", [P, NBATCH * CH * H * VW])
        vals0 = region_a[:, :].rearrange("p (b c h v) -> p b c h v", b=NBATCH, c=CH, h=H)
        w1b = region_a[:, 0:E * F1].rearrange("p (e f) -> p e f", e=E)
        b2bc = region_a[:, E * F1:E * F1 + E * D].rearrange("p (e d) -> p e d", e=E)
        region_b = sb("region_b", [P, E * 2 * F0])
        w13 = region_b[:, :].rearrange("p (e f) -> p e f", e=E)
        b1bc = region_b[:, :].rearrange("p (e f) -> p e f", e=E)
        w2a = sb("w2a", [P, E, F0 // P, D])
        keys1 = sb("keys1", [P, NBATCH, HK])
        ylast = [keys1[:, :, :].rearrange("p b k -> p (b k)")[:, n * 4 * D:(n + 1) * 4 * D]
                 .rearrange("p (t k d) -> p t k d", k=2, d=D) for n in range(NT // 2)]
        pp = sb("pp", [P, 4, HKP])
        prob = [pp[:, 0, :], pp[:, 1, :]]
        probT = [pp[:, 2, :], pp[:, 3, :]]
        ident = sb("ident", [P, P])
        ident_r = sb("ident_r", [P, P], F32R)
        mask16 = sb("mask16", [P, H])
        mask4 = sb("mask4", [P, G])
        headsel = sb("headsel", [P, CH, H])
        upper = sb("upper", [P, P], BF16)
        ones_b = sb("ones_b", [P, P], BF16)
        mhalf = sb("mhalf", [P, NBATCH * H])
        iota8 = sb("iota8", [P, E])
        iota8i = sb("iota8i", [P, E], I32)
        ebase_b = sb("ebase_b", [P, E], BF16)
        ones_f = sb("ones_f", [P, P])
        ebasei = sb("ebasei", [P, E], I32)
        dest = sb("dest", [P, NT, 2], I32)
        jidx = sb("jidx", [1, NJ])
        jidxi = sb("jidxi", [1, NJ], I32)
        ones1 = sb("ones1", [1, E])
        empty = sb("empty", [P, 4, ROW])
        ctx_sb = sb("ctx_sb", [KEYS, NBATCH, D])
        ctxT = sb("ctxT", [P, NBATCH * KEYS])
        bias_sb = sb("bias_sb", [P, TPB, KEYS])
        wk0 = sb("wk0", [P, D])
        wv0 = sb("wv0", [P, D])
        wq0 = sb("wq0", [P, D])
        wo0 = sb("wo0", [P, D])
        bq_bc = sb("bq_bc", [P, D])
        bo_bc = sb("bo_bc", [P, D])
        scl = sb("scl", [KEYS, H])
        wr = [sb("wr0", [P, E]), sb("wr1", [P, E])]
        br_bc = sb("br_bc", [P, E])
        yb_all = sb("yb_all", [P, 4, 2, D])
        yb = [yb_all[:, k] for k in range(4)]
        wq1 = yb_all[:, :, :, :].rearrange("p a b d -> p (a b d)")
        big1 = sb("big1", [P, 2, F1])
        big2 = sb("big2", [P, 2, F1])
        wq1T = big1[:, :, :].rearrange("p a (k c) -> p (a k) c", c=D)
        wkk = sb("wkk", [P, 2, HD1])
        wvv = sb("wvv", [P, 2, HD1])
        wo1 = big2[:, :, :].rearrange("p a (k c) -> p (a k) c", c=D)
        wff1 = sb("wff1", [P, 2 * FF])
        wff2 = sb("wff2", [P, FF // P, D])
        gb = sb("gb", [P, 4])
        kT1 = sb("kT1", [P, NBATCH * KEYS])
        vT1 = sb("vT1", [P, NBATCH * KEYS])
        vT0 = sb("vT0", [P, NBATCH * KEYS])
        k0sq = pp[0:KEYS, 2, 0:NBATCH * D]
        k0n = pp[0:KEYS, 2, NBATCH * D:2 * NBATCH * D]
        k0split = pp[0:KEYS, 0:2, 0:1024].rearrange("p a (r s w d) -> p a r s w d", s=2, w=2, d=HD0)
        vblk = [pp[:, k, :] for k in (3, 2, 0, 1)]
        foldT = [pp[:, b, :] for b in range(NBATCH)]
        k0ss = sb("k0ss", [KEYS, NBATCH * H])
        k0sm = sb("k0sm", [KEYS, NBATCH * H])
        k0r = sb("k0r", [KEYS, NBATCH * H])
        k0rs = sb("k0rs", [KEYS, NBATCH * H])
        k0h = sb("k0h", [KEYS, NBATCH * H], I32)
        k0t = sb("k0t", [KEYS, NBATCH * H])
        cstat = sb("cstat", [KEYS, NBATCH, 6])
        cmv = sb("cmv", [KEYS, NBATCH, 2])
        cve = sb("cve", [KEYS, NBATCH])
        crs = sb("crs", [KEYS, NBATCH])
        cn = sb("cn", [KEYS, NBATCH, D])
        def two(name, shape, dt=F32):
            t = sb(name, [shape[0], 2] + shape[1:], dt)
            return [t[:, 0], t[:, 1]]
        stA, mvA, veA, rsA, xnA = two("stA", [P, 6]), two("mvA", [P, 2]), two("veA", [P, 1]), two("rsA", [P, 1]), two("xnA", [P, D])
        stD, mvD, veD, rsD = two("stD", [P, 6]), two("mvD", [P, 2]), two("veD", [P, 1]), two("rsD", [P, 1])
        xT = two("xT", [P, P])
        qb, qsq, qn = two("qb", [P, D]), two("qsq", [P, D]), two("qn", [P, D])
        qss, qsm, qr = two("qss", [P, H]), two("qsm", [P, H]), two("qr", [P, H])
        qsplit = [big1[:, k].rearrange("p (h a b d) -> p h a b d", a=2, b=2, d=HD0) for k in range(2)]
        mx, den, rden = two("mx", [P, H]), two("den", [P, H]), two("rden", [P, H])
        on, oT = two("on", [P, D]), two("oT", [P, P])
        pay = two("pay", [P, 2, ROW])
        x2T = two("x2T", [P, P])
        top = sb("top", [P, NT, 8])
        scr, topi = two("scr", [P, E]), two("topi", [P, 8], U32)
        oh = two("oh", [P, 2, E])
        picks, before = two("picks", [P, E], BF16), two("before", [P, E], BF16)
        rsel, slotf = two("rsel", [P, 2, E]), two("slotf", [P, 2])
        slot = two("slot", [P, 2], I32)
        margin = sb("margin", [P, NT])
        spare = sb("spare", [P, 1])
        gate = sb("gate", [P, 2, NT])
        gtmp = sb("gtmp", [P, 2, NT])
        ffbuf = [big1[:, 0], big1[:, 1]]
        gated = w2a[:, :, :, :].rearrange("p e k d -> p (e k d)").rearrange("p (n f) -> p n f", n=4)
        cnt_i = sb("cnt_i", [1, E], I32)
        cnt_s = sb("cnt_s", [1, E], I32)
        ntile = sb("ntile", [1, E])
        cum = sb("cum", [1, E])
        wgt = sb("wgt", [1, E])
        ind = sb("ind", [1, NJ, E - 1])
        ind2 = sb("ind2", [1, NJ, E - 1])
        ef = sb("ef", [1, NJ])
        rf = sb("rf", [1, NJ])
        rf2 = sb("rf2", [1, NJ])
        sched = [sb("sched0", [1, 2, NJ], I32), sb("sched1", [1, 2, NJ], I32)]
        xs = [sb(f"xs{i}", [P, ROW]) for i in range(XB)]
        back = [sb(f"back{i}", [P, 1], I32) for i in range(XB)]
        xsT = two("xsT", [P, P])
        ha = [big1[:, 0], big1[:, 1]]
        hT = [big2[:, 0], big2[:, 1]]
        ysb = two("ysb", [P, D])

        ps = ctx.enter_context(nc.psum_tensor("ps", [P, 8, 512], F32))
        S = [ps[:, k, :] for k in range(3)]
        TP = [ps[:, 3, :], ps[:, 4, :]]
        MA, MC, MD = ps[:, 5, :], ps[:, 6, :], ps[:, 7, :]

        rows = [nc.dram_tensor(f"rows{l}", (SLOTS, ROW), F32, kind="Internal").ap() for l in range(2)]
        ys = [nc.dram_tensor(f"ys{l}", (2 * T, D), F32, kind="Internal").ap() for l in range(2)]

        x_v = x_in.rearrange("b (t p) c -> p (b t) c", p=P)
        out_v = out.rearrange("b (t p) c -> p (b t) c", p=P)
        y_v = ys[0].rearrange("(t p k) d -> t p k d", p=P, k=2)
        ylast_v = ys[1].rearrange("(n t p k) d -> n p t k d", t=2, p=P, k=2)

        class Stage:
            def __init__(self, tag, names, again=None):
                self.s, self.base = {}, {}
                for n in names:
                    name, self.base[n] = again[n] if again and n in again else (None, 0)
                    self.s[n] = sem(f"{n}_{tag}") if name is None else name

            def __getitem__(self, n):
                return self.s[n]

            def count(self, n, v):
                return self.base[n] + v

        BOTH = ["bnA", "mvA", "veA", "rsA", "xnA", "TxA", "xT", "S", "mx", "sub", "exp", "TP0", "PT0", "TP1", "TP2",
                "PT2", "AV", "rden", "xa", "bnD", "mvD", "veD", "rsD", "xnD", "Tx2", "x2T", "route", "top", "topi",
                "oh", "picks", "bef", "rank", "rsel", "slotf", "slot"]
        ONLY0 = ["q", "qb", "qsq", "qss", "qsm", "qr", "qn", "hi", "lo", "Tq", "qT", "on", "To", "oT", "Wo"]
        ONLY1 = ["c1", "comb", "ffg", "th", "gg", "ffh", "fo", "den", "norm", "scr"]
        MOE = ["back", "Tx", "xsT", "up", "act1", "act2", "Th", "hT", "down", "y"]
        ONCE = {"margin": 1, "cnt": 1, "plan": 9, "sched": 1, "g1": 1, "gates": 3, "zero": 1}
        PRO0 = {"ctxT": 1, "ctxTs": 1, "k": 1, "ksq": 1, "kss": 1, "ksm": 1, "kr": 11, "krs": 1, "kn": 1, "khi": 1,
                "klo": 1, "kT": NBATCH, "keys0": NBATCH, "v": 1, "vT": 1, "vblk": 2, "vblko": 2, "vtp": NBATCH * CH,
                "vals0": NBATCH * 3, "ones": 1, "identr": 1, "bhi": 1, "blo": TPB, "scl": 1, "scm": 1,
                "cbn": 1, "cmv": 1, "cve": 1, "crs": 1, "cn": 1, "cT": 1, "cTs": 1, "kv1": 2, "kT1": 1, "vT1": 1,
                "wqT": 2, "wqTs": 2, "fk": H, "keys1": H}
        PRO1 = ["fv", "foldT", "fT", "vals1", "vals1o"]
        att0 = Stage("a", BOTH + ONLY0)
        again = {n: (att0[n], NT) for n in BOTH}
        again.update({n: (att0[o], NT) for n, o in zip(ONLY1, ONLY0)})
        A = [att0, Stage("a", BOTH + ONLY1, again)]
        moe0 = Stage("m", MOE + list(ONCE))
        again = {n: (moe0[n], NJ) for n in MOE}
        again.update({n: (moe0[n], c) for n, c in ONCE.items()})
        M = [moe0, Stage("m", MOE + list(ONCE) + ["fin", "fin0"], again)]
        pro = Stage("p", PRO0)
        pro1 = Stage("p", PRO1, {n: (pro[o], PRO0[o]) for n, o in zip(PRO1, list(PRO0))})
        ld = {n: sem(f"ld_{n}") for n in ("x", "ctx", "q", "o", "moe0", "l1", "l1b", "moe1", "bias")}
        filled = [sem("filled0"), sem("filled1")]
        xs_in = [sem(f"xs_in{i}") for i in range(XB)]
        sent = [sem(f"sent{i}") for i in range(2)]
        sentb = [sem(f"sentb{i}") for i in range(XB)]
        y_in = [sem(f"y_in{i}") for i in range(4)]
        stored = sem("stored")
        const = sem("const")

        def sent_count(l, t):
            return 32 * (l * NT // 2 + t // 2 + 1)

        def ring_uses(k):
            return -(-(NJ - k) // XB)

        def sentb_count(l, j):
            return 16 * (l * ring_uses(j % XB) + j // XB + 1)

        def xs_count(l, j):
            return 16 * (l * ring_uses(j % XB) + j // XB + 1)

        LAG = (8, 8)
        FILLS = SLOTS // P // 4
        S01 = ps[:, 0:2, 0:HB * KEYS].rearrange("p b (h k) -> p b h k", k=KEYS)
        S2 = ps[:, 2, 0:(H - 2 * HB) * KEYS].rearrange("p (h k) -> p h k", k=KEYS)
        AV0 = MC[:, 0:H * VW].rearrange("p (h v) -> p h v", h=H)
        RANK = MD[:, 2 * P + E:2 * P + 2 * E]
        FOLD = [S[0], S[1], S[2], TP[0]]

        def row_of(ap, n):
            return ap.rearrange("(a n) -> a n", a=1).to_broadcast([P, n])

        block = ctx.enter_context(nc.Block())

        @block.sync
        def _(sp):
            sp.dma_start(ctx_sb[:, :, :], ctx_in.rearrange("b k c -> k b c")).then_inc(ld["ctx"], 16)
            sp.dma_start(wk0[:, :], Wk0).then_inc(ld["ctx"], 16)
            sp.dma_start(wv0[:, :], Wv0).then_inc(ld["ctx"], 16)
            sp.dma_start(x[:, :, :], x_v).then_inc(ld["x"], 16)
            sp.dma_start(wq1[:, :], Wq1).then_inc(ld["l1"], 16)
            for r in range(2):
                sp.dma_start(wkk[:, r, :], Wkv1[:, 0:HD1]).then_inc(ld["l1"], 16)
                sp.dma_start(wvv[:, r, :], Wkv1[:, HD1:2 * HD1]).then_inc(ld["l1"], 16)
            sp.dma_start(wo1[:, :, :], Wo1.rearrange("(k p) d -> p k d", p=P)).then_inc(ld["l1"], 16)
            for n, v in enumerate((ln_g, ln_b, cln_g, cln_b)):
                sp.dma_start(gb[:, n:n + 1], v.rearrange("(c a) -> c a", a=1)).then_inc(ld["l1"], 16)
            sp.wait_ge(const, 1)
            for l in range(2):
                dst = rows[l].rearrange("(n p r) c -> n p (r c)", p=P, r=4)
                for n in range(SLOTS // P // 4):
                    sp.dma_start(dst[n], empty[:, :, :].rearrange("p r c -> p (r c)")).then_inc(filled[l], 16)
                if l == 0:
                    sp.dma_start(w13[:, :, 0:F0], W1_0.rearrange("e c f -> c e f")).then_inc(ld["moe0"], 16)
                    sp.dma_start(w13[:, :, F0:2 * F0], W3_0.rearrange("e c f -> c e f")).then_inc(ld["moe0"], 16)
                    sp.dma_start(w2a[:, :, :, :], W2_0.rearrange("e (k p) d -> p e k d", p=P)).then_inc(ld["moe0"], 16)
                    sp.dma_start(wff1[:, :], Wff1).then_inc(ld["l1b"], 16)
                    sp.dma_start(wff2[:, :, :], Wff2.rearrange("(k p) d -> p k d", p=P)).then_inc(ld["l1b"], 16)
                    sp.dma_start(wr[1][:, :], Wr1).then_inc(ld["l1b"], 16)
                    sp.dma_start(br_bc[:, :], row_of(br1, E)).then_inc(ld["l1b"], 16)
            for l in range(2):
                m = M[l]
                if l == 0:
                    sp.wait_ge(A[0]["AV"], A[0].count("AV", NT))
                    sp.dma_start(w2b[:, :, :, :], W2_1.rearrange("e (k p) d -> p e k d", p=P)).then_inc(ld["moe1"], 16)
                    sp.dma_start(w1b, W1_1.rearrange("e c f -> c e f")).then_inc(ld["moe1"], 16)
                    sp.dma_start(b2bc, b2_1.rearrange("(a e) d -> a e d", a=1).to_broadcast([P, E, D])).then_inc(ld["moe1"], 16)
                else:
                    sp.wait_ge(M[0]["up"], M[0].count("up", NJ))
                    sp.dma_start(b1bc, b1_1.rearrange("(a e) f -> a e f", a=1).to_broadcast([P, E, F1])).then_inc(ld["moe1"], 16)
                sp.wait_ge(m["sched"], m.count("sched", 1))
                for t in (NT - 2, NT - 1):
                    sp.wait_ge(sent[t % 2], sent_count(l, t))
                sp.wait_ge(filled[l], 16 * FILLS)
                for j in range(NJ):
                    k = j % XB
                    if j >= XB:
                        sp.wait_ge(m["Tx"], m.count("Tx", j - XB + 1))
                    if j >= XB:
                        sp.wait_ge(m["back"], m.count("back", j - XB + 1))
                    r = sp.value_load(sched[l][0:1, 1, at(j)], min_val=0, max_val=SLOTS - P)
                    sp.dma_start(xs[k][:, :], rows[l][bass.ds(r, P), :]).then_inc(xs_in[k], 16)
                for j in range(NJ - XB, NJ):
                    sp.wait_ge(sentb[j % XB], sentb_count(l, j))
                if l == 0:
                    for t in range(NT):
                        if t >= 4:
                            sp.wait_ge(A[1]["comb"], A[1].count("comb", t - 3))
                        sp.dma_start(yb[t % 4][:, :, :], y_v[t]).then_inc(y_in[t % 4], 16)
            for n in range(NT // 2):
                sp.dma_start(ylast[n], ylast_v[n]).then_inc(xs_in[n], 16)
            for n in range(NT // 2):
                sp.wait_ge(M[1]["fin"], M[1].count("fin", 2 * (n + 1)))
                sp.dma_start(out_v[:, 2 * n:2 * n + 2, :], x[:, 2 * n:2 * n + 2, :]).then_inc(stored, 16)
            sp.wait_ge(stored, 16 * (NT // 2))

        @block.gpsimd
        def _(pool):
            pool.memset(empty[:, :, 0:D], 0.0)
            pool.iota(empty[:, :, D:ROW].bitcast(I32), [[0, 4], [0, 1]], base=NOWHERE, channel_multiplier=0).then_inc(const, 1)
            pool.memset(ident[:, :], 0.0)
            pool.memset(mask16[:, :], 1.0)
            pool.memset(mask4[:, :], 1.0)
            pool.memset(headsel[:, :, :], 1.0)
            pool.memset(upper[:, :], 1.0)
            pool.memset(ones_b[:, :], 1.0)
            pool.memset(ones_f[:, :], 1.0)
            pool.memset(before[0], 0.0)
            pool.memset(ones1[:, :], 1.0)
            pool.memset(mhalf[:, :], -0.5)
            pool.memset(pp[:, :, HK:HKP], 0.0)
            pool.iota(iota8i[:, :], [[1, E]], base=0, channel_multiplier=0)
            pool.iota(ebasei[:, :], [[REGION, E]], base=0, channel_multiplier=0)
            pool.iota(dest[:, :, :], [[2 * P, NT], [1, 2]], base=0, channel_multiplier=2)
            pool.iota(jidxi[:, :], [[1, NJ]], base=0, channel_multiplier=0).then_inc(const, 1)
            pool.wait_ge(const, 2)
            pool.affine_select(out=ident[:, :], in_=ident[:, :], compare_op=ALU.not_equal, fill=1.0,
                               base=0, pattern=[[-1, P]], channel_multiplier=1)
            pool.affine_select(out=upper[:, :], in_=upper[:, :], compare_op=ALU.is_gt, fill=0.0,
                               base=0, pattern=[[1, P]], channel_multiplier=-1)
            pool.affine_select(out=mask16[:, :], in_=mask16[:, :], compare_op=ALU.is_ge, fill=0.0,
                               base=0, pattern=[[-HD0, H]], channel_multiplier=1)
            pool.affine_select(out=mask4[:, :], in_=mask4[:, :], compare_op=ALU.is_ge, fill=0.0,
                               base=0, pattern=[[-4 * HD0, G]], channel_multiplier=1)
            pool.affine_select(out=headsel[:, :, :], in_=headsel[:, :, :], compare_op=ALU.is_ge, fill=0.0,
                               base=0, pattern=[[P, CH], [-KEYS, H]], channel_multiplier=1).then_inc(const, 1)
            pool.wait_ge(const, 3)
            pool.affine_select(out=mask16[:, :], in_=mask16[:, :], compare_op=ALU.is_ge, fill=0.0,
                               base=HD0 - 1, pattern=[[HD0, H]], channel_multiplier=-1)
            pool.affine_select(out=mask4[:, :], in_=mask4[:, :], compare_op=ALU.is_ge, fill=0.0,
                               base=4 * HD0 - 1, pattern=[[4 * HD0, G]], channel_multiplier=-1)
            pool.affine_select(out=headsel[:, :, :], in_=headsel[:, :, :], compare_op=ALU.is_ge, fill=0.0,
                               base=KEYS - 1, pattern=[[-P, CH], [KEYS, H]], channel_multiplier=-1)
            pool.tensor_copy(iota8[:, :], iota8i[:, :])
            pool.tensor_copy(ebase_b[:, :], ebasei[:, :])
            pool.tensor_copy(jidx[:, :], jidxi[:, :]).then_inc(const, 1)
            pool.wait_ge(const, NCONST)
            pool.wait_ge(ld["o"], 48)
            pool.tensor_copy(vals0[:, :, :, :, HD0], headsel[:, :, :].unsqueeze(1).to_broadcast([P, NBATCH, CH, H])).then_inc(pro["ones"], 1)
            pool.wait_ge(pro["cve"], pro.count("cve", 1))
            pool.tensor_tensor(crs[:, :], cve[:, :], mhalf[0:KEYS, 0:NBATCH], ALU.pow).then_inc(pro["crs"], 1)
            def low_bias():
                pool.wait_ge(pro["bhi"], pro.count("bhi", 1))
                for tt in range(TPB):
                    pool.tensor_tensor(bias_r[:, 1, tt, :].rearrange("p (h k) -> p h k", k=KEYS),
                                       bias_sb[:, tt, :].unsqueeze(1).to_broadcast([P, G, KEYS]),
                                       bias_r[:, 0, tt, :].bitcast(F32).rearrange("p (h k) -> p h k", k=KEYS),
                                       ALU.subtract).then_inc(pro["blo"], 1)

            def values():
                pool.wait_ge(pro["vT"], pro.count("vT", 1))
                for b in range(0, NBATCH, 2):
                    if b == 2:
                        pool.wait_ge(pro["kT"], pro.count("kT", NBATCH))
                    pool.tensor_tensor(vblk[b][:, 0:HK].rearrange("p (h k) -> p h k", h=H),
                                       mask16[:, :].unsqueeze(2).to_broadcast([P, H, KEYS]),
                                       vT0[:, b * KEYS:(b + 1) * KEYS].unsqueeze(1).to_broadcast([P, H, KEYS]),
                                       ALU.mult).then_inc(pro["vblk"], 1)

            def step0(i):
                a = A[0]
                t = i - 6
                if 0 <= t < NT:
                    s = t % 2
                    pool.wait_ge(a["veD"], a.count("veD", t + 1))
                    pool.tensor_tensor(rsD[s], veD[s], mhalf[:, 0:1], ALU.pow).then_inc(a["rsD"], 1)
                t = i
                if 0 <= t < NT:
                    s = t % 2
                    pool.wait_ge(a["veA"], a.count("veA", t + 1))
                    pool.tensor_tensor(rsA[s], veA[s], mhalf[:, 0:1], ALU.pow).then_inc(a["rsA"], 1)
                t = i - 4
                if 0 <= t < NT:
                    s = t % 2
                    pool.tensor_tensor(x[:, t, :], x[:, t, :], bo_bc[:, :], ALU.add)
                t = i - 7
                if 0 <= t < NT:
                    s = t % 2
                    if t == 0:
                        pool.wait_ge(filled[0], 16 * FILLS)
                    pool.wait_ge(a["slot"], a.count("slot", t + 1))
                    for k in range(2):
                        pool.indirect_dma_start(rows[0][:, :], bass.IndirectOffsetOnAxis(slot[s][:, k:k + 1], 0), pay[s][:, k, :], None,
                                                bounds_check=SLOTS - 1, oob_is_err=False).then_inc(sent[s], 16)
                t = i - 1
                if 0 <= t < NT:
                    s = t % 2
                    pool.wait_ge(a["qsm"], a.count("qsm", t + 1))
                    pool.tensor_tensor(qr[s], qsm[s], mhalf[:, 0:H], ALU.pow).then_inc(a["qr"], 1)

            def step1(i):
                a = A[1]
                t = i - 5
                if 0 <= t < NT:
                    s = t % 2
                    pool.wait_ge(a["rden"], a.count("rden", t + 1))
                    p3 = prob[s][:, 0:HK].rearrange("p (h k) -> p h k", h=H)
                    pool.tensor_tensor(p3, p3, rden[s].unsqueeze(2).to_broadcast([P, H, KEYS]), ALU.mult).then_inc(a["norm"], 1)
                t = i - 8
                if 0 <= t < NT:
                    s = t % 2
                    if t == 0:
                        pool.wait_ge(filled[1], 16 * FILLS)
                    pool.wait_ge(a["slot"], a.count("slot", t + 1))
                    for k in range(2):
                        pool.indirect_dma_start(rows[1][:, :], bass.IndirectOffsetOnAxis(slot[s][:, k:k + 1], 0), pay[s][:, k, :], None,
                                                bounds_check=SLOTS - 1, oob_is_err=False).then_inc(sent[s], 16)
                t = i - 2
                if 0 <= t < NT:
                    s = t % 2
                    pool.wait_ge(a["veA"], a.count("veA", t + 1))
                    pool.tensor_tensor(rsA[s], veA[s], mhalf[:, 0:1], ALU.pow).then_inc(a["rsA"], 1)
                t = i - 6
                if 0 <= t < NT:
                    s = t % 2
                    pool.wait_ge(a["veD"], a.count("veD", t + 1))
                    pool.tensor_tensor(rsD[s], veD[s], mhalf[:, 0:1], ALU.pow).then_inc(a["rsD"], 1)
                t = i - 2
                if 0 <= t < NT:
                    s = t % 2
                    pool.wait_ge(a["rsA"], a.count("rsA", t + 1))
                    pool.tensor_scalar(xnA[s], x[:, t, :], mvA[s][:, 0:1], rsA[s], ALU.subtract, ALU.mult).then_inc(a["xnA"], 1)

            def moe(l):
                m = M[l]

                def send(j):
                    pool.wait_ge(m["y"], m.count("y", j + 1))
                    pool.wait_ge(m["back"], m.count("back", j + 1))
                    pool.indirect_dma_start(ys[l][:, :], bass.IndirectOffsetOnAxis(back[j % XB][:, 0:1], 0),
                                            ysb[j % 2], None, bounds_check=2 * T - 1,
                                            oob_is_err=False).then_inc(sentb[j % XB], 16)
                for j in range(NJ + 3):
                    if j >= 3:
                        send(j - 3)
                    if j < NJ:
                        pool.wait_ge(xs_in[j % XB], xs_count(l, j))
                        if j >= XB:
                            pool.wait_ge(sentb[j % XB], sentb_count(l, j - XB))
                        pool.tensor_copy(back[j % XB][:, :], xs[j % XB][:, D:ROW].bitcast(I32)).then_inc(m["back"], 1)

            for l in range(2):
                for i in range(NT + LAG[l]):
                    step0(i) if l == 0 else step1(i)
                    if l == 0 and i == 0:
                        values()
                    if l == 0 and i == 1:
                        low_bias()
                moe(l)

        @block.scalar
        def _(act):
            act.dma_start(scl[:, :], scale_log.rearrange("a h b c -> a (h b c)").to_broadcast([KEYS, H])).then_inc(ld["q"], 16)
            act.dma_start(wq0[:, :], Wq0).then_inc(ld["q"], 16)
            act.dma_start(bq_bc[:, :], row_of(bq0, D)).then_inc(ld["q"], 16)
            act.dma_start(bias_sb[:, :, :], bias_in.rearrange("(t p) k -> p t k", p=P)).then_inc(ld["bias"], 16)
            act.dma_start(wo0[:, :], Wo0).then_inc(ld["o"], 16)
            act.dma_start(bo_bc[:, :], row_of(bo0, D)).then_inc(ld["o"], 16)
            act.dma_start(wr[0][:, :], Wr0).then_inc(ld["o"], 16)

            act.wait_ge(const, 1)
            act.activation(spare[:, :], empty[:, 0, 0:1], ACT.Exp)
            act.wait_ge(pro["ctxT"], pro.count("ctxT", 1))
            act.copy(ctxT[:, :], MD[:, 0:NBATCH * KEYS]).then_inc(pro["ctxTs"], 1)
            act.wait_ge(pro["k"], pro.count("k", 1))
            act.activation(k0sq, MC[0:KEYS, :], ACT.Square).then_inc(pro["ksq"], 1)
            act.wait_ge(pro["scm"], pro.count("scm", 1))
            act.activation(scl[:, :], scl[:, :], ACT.Exp).then_inc(pro["scl"], 1)
            act.wait_ge(pro["v"], pro.count("v", 1))
            act.copy(vT0[:, :], MA[:, 0:NBATCH * KEYS]).then_inc(pro["vT"], 1)
            act.wait_ge(ld["bias"], 16)
            for tt in range(TPB):
                ins = act.copy(bias_r[:, 0, tt, :].rearrange("p (h k) -> p h k", k=KEYS),
                               bias_sb[:, tt, :].unsqueeze(1).to_broadcast([P, G, KEYS]))
            ins.then_inc(pro["bhi"], 1)
            act.wait_ge(const, NCONST)
            act.copy(ident_r[:, :], ident[:, :]).then_inc(pro["identr"], 1)
            act.wait_ge(ld["l1"], 16 * 10)
            act.wait_ge(pro["cT"], pro.count("cT", 1))
            act.activation(ctxT[:, :], MD[:, 0:NBATCH * KEYS], ACT.Identity, bias=gb[:, 3:4], scale=gb[:, 2:3]).then_inc(pro["cTs"], 1)
            act.wait_ge(pro["kv1"], pro.count("kv1", 1))
            act.activation(kT1[:, :], TP[0][:, 0:NBATCH * KEYS], ACT.Copy, scale=float(HD1) ** -0.5).then_inc(pro["kT1"], 1)
            act.wait_ge(pro["kv1"], pro.count("kv1", 2))
            act.copy(vT1[:, :], TP[1][:, 0:NBATCH * KEYS]).then_inc(pro["vT1"], 1)
            for g in range(2):
                act.wait_ge(pro["wqT"], pro.count("wqT", g + 1))
                act.copy(wq1T[:, 4 * g:4 * g + 4, :], S[g][:, :].rearrange("p (k c) -> p k c", k=4)).then_inc(pro["wqTs"], 1)
            for h in range(H):
                act.wait_ge(pro["fk"], pro.count("fk", h + 1))
                act.copy(keys1[:, :, h * KEYS:(h + 1) * KEYS],
                         S[h % 2][:, 0:NBATCH * KEYS].rearrange("p (b k) -> p b k", b=NBATCH)).then_inc(pro["keys1"], 1)
            def values(n0, n1):
                for n in range(n0, n1):
                    b, g = n // 3, n % 3
                    w = min(4, CH - 4 * g)
                    act.wait_ge(pro["vtp"], pro.count("vtp", b * CH + 4 * g + w))
                    act.copy(vals0[:, b, 4 * g:4 * g + w, :, 0:HD0],
                             TP[n % 2][:, 0:w * P].rearrange("p (c h d) -> p c h d", c=w, h=H)).then_inc(pro["vals0"], 1)

            def step0(i):
                a = A[0]
                t = i - 3
                if 0 <= t < NT:
                    s = t % 2
                    act.wait_ge(a["TxA"], a.count("TxA", t + 1))
                    act.copy(xT[s], MA[:, 0:P]).then_inc(a["xT"], 1)
                t = i - 8
                if 0 <= t < NT:
                    s = t % 2
                    act.wait_ge(a["To"], a.count("To", t + 1))
                    act.copy(oT[s], MC[:, 2 * P:3 * P]).then_inc(a["oT"], 1)
                t = i - 7
                if 0 <= t < NT:
                    s = t % 2
                    act.wait_ge(a["TP0"], a.count("TP0", t + 1))
                    act.copy(probT[s][:, 0:4 * P], TP[0]).then_inc(a["PT0"], 1)
                    act.wait_ge(a["TP1"], a.count("TP1", t + 1))
                    act.copy(probT[s][:, 4 * P:8 * P], TP[1])
                    act.wait_ge(a["TP2"], a.count("TP2", t + 1))
                    act.copy(probT[s][:, 8 * P:HKP], TP[0][:, 0:HKP - 8 * P]).then_inc(a["PT2"], 1)
                t = i - 3
                if 0 <= t < NT:
                    s = t % 2
                    act.wait_ge(a["qb"], a.count("qb", t + 1))
                    act.activation(qsq[s], qb[s], ACT.Square).then_inc(a["qsq"], 1)
                t = i - 5
                if 0 <= t < NT:
                    s = t % 2
                    act.wait_ge(a["Tq"], a.count("Tq", t + 1))
                    act.copy(qT[s], MA[:, :]).then_inc(a["qT"], 1)
                t = i - 6
                if 0 <= t < NT:
                    s = t % 2
                    act.wait_ge(a["sub"], a.count("sub", t + 1))
                    act.activation(prob[s][:, 0:HK], prob[s][:, 0:HK], ACT.Exp).then_inc(a["exp"], 1)
                t = i - 4
                if 0 <= t < NT:
                    s = t % 2
                    act.wait_ge(a["qn"], a.count("qn", t + 1))
                    act.copy(qsplit[s][:, :, 0, :, :].bitcast(F32R),
                             qn[s].rearrange("p (h d) -> p h d", h=H).unsqueeze(2).to_broadcast([P, H, 2, HD0])).then_inc(a["hi"], 1)
                t = i - 8
                if 0 <= t < NT:
                    s = t % 2
                    act.wait_ge(a["Tx2"], a.count("Tx2", t + 1))
                    act.copy(x2T[s], MD[:, P:2 * P]).then_inc(a["x2T"], 1)

            def step1(i):
                a = A[1]
                t = i - 7
                if 0 <= t < NT:
                    s = t % 2
                    act.wait_ge(a["TP1"], a.count("TP1", t + 1))
                    act.copy(probT[s][:, 4 * P:8 * P], TP[1])
                    act.wait_ge(a["TP0"], a.count("TP0", t + 1))
                    act.copy(probT[s][:, 0:4 * P], TP[0]).then_inc(a["PT0"], 1)
                t = i - 8
                if 0 <= t < NT:
                    s = t % 2
                    act.wait_ge(a["Tx2"], a.count("Tx2", t + 1))
                    act.copy(x2T[s], MD[:, P:2 * P]).then_inc(a["x2T"], 1)
                t = i - 4
                if 0 <= t < NT:
                    s = t % 2
                    act.wait_ge(a["TxA"], a.count("TxA", t + 1))
                    act.activation(xT[s], MA[:, 0:P], ACT.Identity, bias=gb[:, 1:2], scale=gb[:, 0:1]).then_inc(a["xT"], 1)
                t = i - 6
                if 0 <= t < NT:
                    s = t % 2
                    act.wait_ge(a["TP2"], a.count("TP2", t + 1))
                    act.copy(probT[s][:, 8 * P:HKP], TP[0][:, 0:HKP - 8 * P]).then_inc(a["PT2"], 1)
                t = i - 4
                if 0 <= t < NT:
                    s = t % 2
                    act.wait_ge(a["ffg"], a.count("ffg", t + 1))
                    act.activation(ffbuf[s], MA[:, :], ACT.Tanh, scale=0.5).then_inc(a["th"], 1)
                t = i - 5
                if 0 <= t < NT:
                    s = t % 2
                    act.wait_ge(a["sub"], a.count("sub", t + 1))
                    act.activation(prob[s][:, 0:HK], prob[s][:, 0:HK], ACT.Exp).then_inc(a["exp"], 1)

            def fold(h0, h1):
                for h in range(h0, h1):
                    act.wait_ge(pro1["fv"], pro1.count("fv", h + 1))
                    act.copy(pp[:, :, h * KEYS:(h + 1) * KEYS],
                             FOLD[h % 4][:, 0:NBATCH * KEYS].rearrange("p (b k) -> p b k", b=NBATCH)).then_inc(pro1["foldT"], 1)

            def moe(l):
                m = M[l]

                for j in range(NJ + 3):
                    if j < NJ:
                        act.wait_ge(m["Tx"], m.count("Tx", j + 1))
                        if j >= 2:
                            act.wait_ge(m["up"], m.count("up", j - 1))
                        act.copy(xsT[j % 2], MA[:, 0:P]).then_inc(m["xsT"], 1)
                    t = j - 1
                    if 0 <= t < NJ:
                        s = t % 2
                        if l == 0:
                            act.wait_ge(m["up"], m.count("up", t + 1))
                            if t >= 2:
                                act.wait_ge(m["Th"], m.count("Th", t - 1))
                            act.activation(ha[s][:, 0:F0], S[s][:, 0:F0], ACT.Silu).then_inc(m["act1"], 1)
                        else:
                            act.wait_ge(m["act1"], m.count("act1", t + 1))
                            act.activation(ha[s], ha[s], ACT.Gelu_apprx_tanh).then_inc(m["act2"], 1)
                    t = j - 2
                    if 0 <= t < NJ:
                        s = t % 2
                        act.wait_ge(m["Th"], m.count("Th", t + 1))
                        if t >= 2:
                            act.wait_ge(m["down"], m.count("down", t - 1))
                        w = F0 if l == 0 else F1
                        act.copy(hT[s][:, 0:w], TP[s][:, 0:w]).then_inc(m["hT"], 1)

            for l in range(2):
                if l == 1:
                    act.wait_ge(ld["l1b"], 16 * 4)
                for i in range(NT + LAG[l]):
                    step0(i) if l == 0 else step1(i)
                    if l == 0 and i in (3, 4):
                        values(6 * (i - 3), 6 * (i - 2))
                    if l == 0 and i == NT - 1 + 7:
                        fold(0, 4)
                    if l == 0 and i == NT + 7:
                        fold(4, 8)
                act.wait_ge(M[l]["margin"], M[l].count("margin", 1))
                act.activation(gtmp[:, 0, :], margin[:, :], ACT.Exp).then_inc(M[l]["g1"], 1)
                if l == 0:
                    fold(8, H)
                    for n in range(0, NBATCH * 3, 2):
                        b, g = n // 3, n % 3
                        w = min(4, CH - 4 * g)
                        act.wait_ge(pro1["fT"], pro1.count("fT", n + 1))
                        act.copy(vals1[:, b, 4 * g:4 * g + w, :],
                                 TP[0][:, 0:w * P].rearrange("p (c d) -> p c d", c=w)).then_inc(pro1["vals1"], 1)
                act.activation(spare[:, :], empty[:, 0, 0:1], ACT.Silu if l == 0 else ACT.Gelu_apprx_tanh)
                moe(l)
                if l == 0:
                    act.activation(spare[:, :], empty[:, 0, 0:1], ACT.Exp)

        @block.vector
        def _(dve):
            dve.wait_ge(ld["q"], 48)
            dve.tensor_scalar(scl[:, :], scl[:, :], MAX_LOG_SCALE, None, ALU.min).then_inc(pro["scm"], 1)
            dve.wait_ge(ld["ctx"], 48)
            for b in range(NBATCH):
                ins = dve.bn_stats(cstat[:, b, :], ctx_sb[:, b, :])
            ins.then_inc(pro["cbn"], 1)
            dve.wait_ge(pro["cbn"], pro.count("cbn", 1))
            for b in range(NBATCH):
                ins = dve.bn_aggr(cmv[:, b, :], cstat[:, b, :])
            ins.then_inc(pro["cmv"], 1)
            dve.wait_ge(pro["cmv"], pro.count("cmv", 1))
            dve.tensor_scalar(cve[:, :], cmv[:, :, 1], EPS, None, ALU.add).then_inc(pro["cve"], 1)
            dve.wait_ge(pro["ksq"], pro.count("ksq", 1))
            dve.reduce_sum(k0ss[:, :], k0sq.rearrange("k (r d) -> k r d", d=HD0), AX).then_inc(pro["kss"], 1)
            dve.wait_ge(pro["kss"], pro.count("kss", 1))
            dve.tensor_scalar(k0sm[:, :], k0ss[:, :], NORM_FLOOR, None, ALU.max).then_inc(pro["ksm"], 1)
            dve.wait_ge(pro["ksm"], pro.count("ksm", 1))
            dve.tensor_scalar(k0h[:, :], k0sm[:, :].bitcast(I32), 1, None, ALU.arith_shift_right).then_inc(pro["kr"], 1)
            dve.wait_ge(pro["kr"], pro.count("kr", 1))
            dve.tensor_scalar(k0r[:, :].bitcast(I32), k0h[:, :], -1.0, float(0x5F3759DF), ALU.mult, ALU.add).then_inc(pro["kr"], 1)
            for n in range(3):
                dve.wait_ge(pro["kr"], pro.count("kr", 3 * n + 2))
                dve.scalar_tensor_tensor(k0t[:, :], k0r[:, :], -0.5, k0r[:, :], ALU.mult, ALU.mult).then_inc(pro["kr"], 1)
                dve.wait_ge(pro["kr"], pro.count("kr", 3 * n + 3))
                dve.tensor_tensor(k0t[:, :], k0t[:, :], k0sm[:, :], ALU.mult).then_inc(pro["kr"], 1)
                dve.wait_ge(pro["kr"], pro.count("kr", 3 * n + 4))
                dve.scalar_tensor_tensor(k0r[:, :], k0t[:, :], 1.5, k0r[:, :], ALU.add, ALU.mult).then_inc(pro["kr"], 1)
            dve.wait_ge(pro["kr"], pro.count("kr", 11))
            dve.wait_ge(pro["scl"], pro.count("scl", 1))
            dve.tensor_tensor(k0rs[:, :].rearrange("k (b h) -> k b h", b=NBATCH),
                              k0r[:, :].rearrange("k (b h) -> k b h", b=NBATCH),
                              scl[:, :].unsqueeze(1).to_broadcast([KEYS, NBATCH, H]), ALU.mult).then_inc(pro["krs"], 1)
            dve.wait_ge(pro["crs"], pro.count("crs", 1))
            for b in range(NBATCH):
                ins = dve.tensor_scalar(cn[:, b, :], ctx_sb[:, b, :], cmv[:, b, 0:1], crs[:, b:b + 1], ALU.subtract, ALU.mult)
            ins.then_inc(pro["cn"], 1)
            dve.wait_ge(pro["krs"], pro.count("krs", 1))
            dve.tensor_tensor(k0n.rearrange("k (r d) -> k r d", d=HD0), MC[0:KEYS, :].rearrange("k (r d) -> k r d", d=HD0),
                              k0rs[:, :].unsqueeze(2).to_broadcast([KEYS, NBATCH * H, HD0]), ALU.mult).then_inc(pro["kn"], 1)
            dve.wait_ge(pro["kn"], pro.count("kn", 1))
            for half in range(2):
                src = k0n[:, half * 256:half * 256 + 256].rearrange("k (r d) -> k r d", d=HD0)
                for s2 in range(2):
                    ins = dve.tensor_copy(k0split[:, half, :, s2, 0, :].bitcast(F32R), src)
            ins.then_inc(pro["khi"], 1)
            dve.wait_ge(pro["khi"], pro.count("khi", 1))
            for half in range(2):
                src = k0n[:, half * 256:half * 256 + 256].rearrange("k (r d) -> k r d", d=HD0)
                for s2 in range(2):
                    ins = dve.tensor_tensor(k0split[:, half, :, s2, 1, :], src, k0split[:, half, :, s2, 0, :], ALU.subtract)
            ins.then_inc(pro["klo"], 1)
            dve.wait_ge(ld["x"], 16)
            dve.wait_ge(ld["o"], 48)

            def keys_and_values():
                dve.wait_ge(const, NCONST)
                for b in range(NBATCH):
                    dve.wait_ge(pro["kT"], pro.count("kT", b + 1))
                    src = (S[2], MC, TP[0], TP[1])[b]
                    for g in range(NG):
                        ins = dve.tensor_tensor(keys0[:, b, g * GK:(g + 1) * GK].rearrange("p (h k) -> p h k", h=G),
                                          src[:, g * KEYS:(g + 1) * KEYS].unsqueeze(1).to_broadcast([P, G, KEYS]),
                                          mask4[:, :].unsqueeze(2).to_broadcast([P, G, KEYS]),
                                          ALU.mult)
                    ins.then_inc(pro["keys0"], 1)

                dve.wait_ge(pro["vT"], pro.count("vT", 1))
                for b in range(1, NBATCH, 2):
                    dve.tensor_tensor(vblk[b][:, 0:HK].rearrange("p (h k) -> p h k", h=H),
                                      mask16[:, :].unsqueeze(2).to_broadcast([P, H, KEYS]),
                                      vT0[:, b * KEYS:(b + 1) * KEYS].unsqueeze(1).to_broadcast([P, H, KEYS]),
                                      ALU.mult).then_inc(pro["vblko"], 1)


            def step0(i):
                a = A[0]
                t = i - 3
                if 0 <= t < NT:
                    s = t % 2
                    dve.wait_ge(a["qss"], a.count("qss", t + 1))
                    dve.tensor_scalar(qsm[s], qss[s], NORM_FLOOR, None, ALU.max).then_inc(a["qsm"], 1)
                t = i - 1
                if 0 <= t < NT:
                    s = t % 2
                    dve.wait_ge(a["bnA"], a.count("bnA", t + 1))
                    dve.bn_aggr(mvA[s], stA[s]).then_inc(a["mvA"], 1)
                t = i - 2
                if 0 <= t < NT:
                    s = t % 2
                    dve.wait_ge(a["rsA"], a.count("rsA", t + 1))
                    dve.tensor_scalar(xnA[s], x[:, t, :], mvA[s][:, 0:1], rsA[s], ALU.subtract, ALU.mult).then_inc(a["xnA"], 1)
                t = i - 4
                if 0 <= t < NT:
                    s = t % 2
                    dve.wait_ge(a["hi"], a.count("hi", t + 1))
                    dve.tensor_tensor(qsplit[s][:, :, 1, :, :],
                                      qn[s].rearrange("p (h d) -> p h d", h=H).unsqueeze(2).to_broadcast([P, H, 2, HD0]),
                                      qsplit[s][:, :, 0, :, :], ALU.subtract).then_inc(a["lo"], 1)
                t = i - 5
                if 0 <= t < NT:
                    s = t % 2
                    dve.wait_ge(a["S"], a.count("S", t + 1))
                    dve.reduce_max(mx[s][:, 0:2 * HB].rearrange("p (b h) -> p b h", b=2), S01, AX)
                    dve.reduce_max(mx[s][:, 2 * HB:H], S2, AX).then_inc(a["mx"], 1)
                t = i - 2
                if 0 <= t < NT:
                    s = t % 2
                    dve.wait_ge(a["q"], a.count("q", t + 1))
                    dve.tensor_tensor(qb[s], MA[:, P:2 * P], bq_bc[:, :], ALU.add).then_inc(a["qb"], 1)
                t = i - 7
                if 0 <= t < NT:
                    s = t % 2
                    dve.wait_ge(a["Wo"], a.count("Wo", t + 1))
                    dve.tensor_tensor(x[:, t, :], x[:, t, :], MD[:, 0:D], ALU.add).then_inc(a["xa"], 1)
                t = i - 5
                if 0 <= t < NT:
                    s = t % 2
                    dve.wait_ge(a["mx"], a.count("mx", t + 1))
                    dve.tensor_tensor(prob[s][:, 0:2 * HB * KEYS].rearrange("p (b h k) -> p b h k", b=2, h=HB), S01,
                                      mx[s][:, 0:2 * HB].rearrange("p (b h) -> p b h", b=2).unsqueeze(3).to_broadcast([P, 2, HB, KEYS]), ALU.subtract)
                    dve.tensor_tensor(prob[s][:, 2 * HB * KEYS:HK].rearrange("p (h k) -> p h k", k=KEYS), S2,
                                      mx[s][:, 2 * HB:H].unsqueeze(2).to_broadcast([P, H - 2 * HB, KEYS]), ALU.subtract).then_inc(a["sub"], 1)
                t = i - 7
                if 0 <= t < NT:
                    s = t % 2
                    dve.wait_ge(a["xa"], a.count("xa", t + 1))
                    dve.bn_stats(stD[s], x[:, t, :]).then_inc(a["bnD"], 1)
                t = i - 8
                if 0 <= t < NT:
                    s = t % 2
                    dve.wait_ge(a["route"], a.count("route", t + 1))
                    dve.max(top[:, t, :], MD[:, 2 * P:2 * P + E]).then_inc(a["top"], 1)
                t = i - 7
                if 0 <= t < NT:
                    s = t % 2
                    dve.wait_ge(a["bnD"], a.count("bnD", t + 1))
                    dve.bn_aggr(mvD[s], stD[s]).then_inc(a["mvD"], 1)
                t = i - 8
                if 0 <= t < NT:
                    s = t % 2
                    dve.wait_ge(a["top"], a.count("top", t + 1))
                    dve.max_index(topi[s], top[:, t, :], MD[:, 2 * P:2 * P + E]).then_inc(a["topi"], 1)
                t = i - 7
                if 0 <= t < NT:
                    s = t % 2
                    dve.wait_ge(a["mvD"], a.count("mvD", t + 1))
                    dve.tensor_scalar(veD[s], mvD[s][:, 1:2], EPS, None, ALU.add).then_inc(a["veD"], 1)
                t = i - 1
                if 0 <= t < NT:
                    s = t % 2
                    dve.wait_ge(a["mvA"], a.count("mvA", t + 1))
                    dve.tensor_scalar(veA[s], mvA[s][:, 1:2], EPS, None, ALU.add).then_inc(a["veA"], 1)
                t = i - 8
                if 0 <= t < NT:
                    s = t % 2
                    dve.wait_ge(a["topi"], a.count("topi", t + 1))
                    dve.tensor_tensor(oh[s], iota8[:, :].unsqueeze(1).to_broadcast([P, 2, E]),
                                      topi[s][:, 0:2].unsqueeze(2).to_broadcast([P, 2, E]), ALU.is_equal).then_inc(a["oh"], 1)
                    dve.tensor_copy(pay[s][:, :, D:ROW].bitcast(I32), dest[:, t, :].unsqueeze(2))
                    dve.wait_ge(a["oh"], a.count("oh", t + 1))
                    dve.tensor_tensor(picks[s], oh[s][:, 0, :], oh[s][:, 1, :], ALU.add).then_inc(a["picks"], 1)
                t = i
                if 0 <= t < NT:
                    s = t % 2
                    dve.bn_stats(stA[s], x[:, t, :]).then_inc(a["bnA"], 1)
                t = i - 2
                if 0 <= t < NT:
                    s = t % 2
                    dve.wait_ge(a["qsq"], a.count("qsq", t + 1))
                    dve.reduce_sum(qss[s], qsq[s].rearrange("p (h d) -> p h d", h=H), AX).then_inc(a["qss"], 1)
                t = i - 8
                if 0 <= t < NT:
                    s = t % 2
                    dve.wait_ge(a["picks"], a.count("picks", t + 1))
                    dve.tensor_tensor(before[1 - s], before[s], picks[s], ALU.add).then_inc(a["bef"], 1)
                t = i - 6
                if 0 <= t < NT:
                    s = t % 2
                    dve.wait_ge(a["AV"], a.count("AV", t + 1))
                    dve.reciprocal(rden[s], AV0[:, :, HD0]).then_inc(a["rden"], 1)
                t = i - 8
                if 0 <= t < NT:
                    s = t % 2
                    dve.wait_ge(a["rank"], a.count("rank", t + 1))
                    dve.tensor_tensor(rsel[s], oh[s], RANK.unsqueeze(1).to_broadcast([P, 2, E]), ALU.mult).then_inc(a["rsel"], 1)
                t = i - 7
                if 0 <= t < NT:
                    s = t % 2
                    dve.wait_ge(a["rsD"], a.count("rsD", t + 1))
                    if t >= 2:
                        dve.wait_ge(sent[s], sent_count(0, t - 2))
                    dve.tensor_scalar(pay[s][:, :, 0:D], x[:, t, :].unsqueeze(1).to_broadcast([P, 2, D]),
                                      mvD[s][:, 0:1], rsD[s], ALU.subtract, ALU.mult).then_inc(a["xnD"], 1)
                t = i - 8
                if 0 <= t < NT:
                    s = t % 2
                    dve.wait_ge(a["rsel"], a.count("rsel", t + 1))
                    dve.reduce_sum(slotf[s], rsel[s], AX).then_inc(a["slotf"], 1)
                t = i - 6
                if 0 <= t < NT:
                    s = t % 2
                    dve.wait_ge(a["rden"], a.count("rden", t + 1))
                    dve.tensor_tensor(on[s].rearrange("p (h d) -> p h d", h=H), AV0[:, :, 0:HD0],
                                      rden[s].unsqueeze(2).to_broadcast([P, H, HD0]), ALU.mult).then_inc(a["on"], 1)
                t = i - 8
                if 0 <= t < NT:
                    s = t % 2
                    dve.wait_ge(a["slotf"], a.count("slotf", t + 1))
                    dve.tensor_copy(slot[s], slotf[s]).then_inc(a["slot"], 1)
                t = i - 3
                if 0 <= t < NT:
                    s = t % 2
                    dve.wait_ge(a["qr"], a.count("qr", t + 1))
                    dve.tensor_tensor(qn[s].rearrange("p (h d) -> p h d", h=H), qb[s].rearrange("p (h d) -> p h d", h=H),
                                      qr[s].unsqueeze(2).to_broadcast([P, H, HD0]), ALU.mult).then_inc(a["qn"], 1)

            def step1(i):
                a = A[1]
                t = i - 3
                if 0 <= t < NT:
                    s = t % 2
                    dve.wait_ge(a["exp"], a.count("exp", t + 1))
                    dve.reduce_sum(den[s], prob[s][:, 0:HK].rearrange("p (h k) -> p h k", h=H), AX).then_inc(a["den"], 1)
                    dve.wait_ge(a["den"], a.count("den", t + 1))
                    dve.reciprocal(rden[s], den[s]).then_inc(a["rden"], 1)
                t = i
                if 0 <= t < NT:
                    s = t % 2
                    dve.wait_ge(y_in[t % 4], 16 * (t // 4 + 1))
                    dve.scalar_tensor_tensor(yb[t % 4][:, 0, :], yb[t % 4][:, 0, :], gate[:, 0, t:t + 1], x[:, t, :], ALU.mult, ALU.add).then_inc(a["c1"], 1)
                t = i - 5
                if 0 <= t < NT:
                    s = t % 2
                    dve.wait_ge(a["rsD"], a.count("rsD", t + 1))
                    if t >= 2:
                        dve.wait_ge(sent[s], sent_count(1, t - 2))
                    dve.tensor_scalar(pay[s][:, :, 0:D], x[:, t, :].unsqueeze(1).to_broadcast([P, 2, D]),
                                      mvD[s][:, 0:1], rsD[s], ALU.subtract, ALU.mult).then_inc(a["xnD"], 1)
                t = i - 6
                if 0 <= t < NT:
                    s = t % 2
                    dve.wait_ge(a["rank"], a.count("rank", t + 1))
                    dve.tensor_tensor(rsel[s], oh[s], RANK.unsqueeze(1).to_broadcast([P, 2, E]), ALU.mult).then_inc(a["rsel"], 1)
                t = i
                if 0 <= t < NT:
                    s = t % 2
                    dve.wait_ge(a["c1"], a.count("c1", t + 1))
                    dve.scalar_tensor_tensor(x[:, t, :], yb[t % 4][:, 1, :], gate[:, 1, t:t + 1], yb[t % 4][:, 0, :], ALU.mult, ALU.add).then_inc(a["comb"], 1)
                t = i - 2
                if 0 <= t < NT:
                    s = t % 2
                    dve.wait_ge(a["S"], a.count("S", t + 1))
                    dve.reduce_max(mx[s][:, 0:2 * HB].rearrange("p (b h) -> p b h", b=2), S01, AX)
                    dve.reduce_max(mx[s][:, 2 * HB:H], S2, AX).then_inc(a["mx"], 1)
                t = i - 6
                if 0 <= t < NT:
                    s = t % 2
                    dve.wait_ge(a["rsel"], a.count("rsel", t + 1))
                    dve.reduce_sum(slotf[s], rsel[s], AX).then_inc(a["slotf"], 1)
                t = i - 3
                if 0 <= t < NT:
                    s = t % 2
                    dve.wait_ge(a["ffh"], a.count("ffh", t + 1))
                    dve.scalar_tensor_tensor(gated[:, t % 4, :], ffbuf[s], 0.5, MA[:, :], ALU.mult, ALU.mult).then_inc(a["fo"], 1)
                t = i - 6
                if 0 <= t < NT:
                    s = t % 2
                    dve.wait_ge(a["slotf"], a.count("slotf", t + 1))
                    dve.tensor_copy(slot[s], slotf[s]).then_inc(a["slot"], 1)
                t = i - 2
                if 0 <= t < NT:
                    s = t % 2
                    dve.wait_ge(a["mx"], a.count("mx", t + 1))
                    dve.tensor_tensor(prob[s][:, 0:2 * HB * KEYS].rearrange("p (b h k) -> p b h k", b=2, h=HB), S01,
                                      mx[s][:, 0:2 * HB].rearrange("p (b h) -> p b h", b=2).unsqueeze(3).to_broadcast([P, 2, HB, KEYS]), ALU.subtract)
                    dve.tensor_tensor(prob[s][:, 2 * HB * KEYS:HK].rearrange("p (h k) -> p h k", k=KEYS), S2,
                                      mx[s][:, 2 * HB:H].unsqueeze(2).to_broadcast([P, H - 2 * HB, KEYS]), ALU.subtract).then_inc(a["sub"], 1)
                t = i - 4
                if 0 <= t < NT:
                    s = t % 2
                    dve.wait_ge(a["AV"], a.count("AV", t + 1))
                    dve.tensor_tensor(x[:, t, :], x[:, t, :], MC[:, 0:D], ALU.add).then_inc(a["xa"], 1)
                t = i - 5
                if 0 <= t < NT:
                    s = t % 2
                    dve.tensor_copy(pay[s][:, :, D:ROW].bitcast(I32), dest[:, t, :].unsqueeze(2))
                t = i - 6
                if 0 <= t < NT:
                    s = t % 2
                    dve.tensor_tensor(before[1 - s], before[s], picks[s], ALU.add).then_inc(a["bef"], 1)
                t = i - 4
                if 0 <= t < NT:
                    s = t % 2
                    dve.wait_ge(a["xa"], a.count("xa", t + 1))
                    dve.bn_stats(stD[s], x[:, t, :]).then_inc(a["bnD"], 1)
                t = i - 5
                if 0 <= t < NT:
                    s = t % 2
                    dve.wait_ge(a["route"], a.count("route", t + 1))
                    dve.tensor_tensor(scr[s], MD[:, 2 * P:2 * P + E], br_bc[:, :], ALU.add).then_inc(a["scr"], 1)
                t = i - 4
                if 0 <= t < NT:
                    s = t % 2
                    dve.wait_ge(a["bnD"], a.count("bnD", t + 1))
                    dve.bn_aggr(mvD[s], stD[s]).then_inc(a["mvD"], 1)
                t = i - 5
                if 0 <= t < NT:
                    s = t % 2
                    dve.wait_ge(a["scr"], a.count("scr", t + 1))
                    dve.max(top[:, t, :], scr[s]).then_inc(a["top"], 1)
                t = i - 4
                if 0 <= t < NT:
                    s = t % 2
                    dve.wait_ge(a["mvD"], a.count("mvD", t + 1))
                    dve.tensor_scalar(veD[s], mvD[s][:, 1:2], EPS, None, ALU.add).then_inc(a["veD"], 1)
                t = i - 5
                if 0 <= t < NT:
                    s = t % 2
                    dve.wait_ge(a["top"], a.count("top", t + 1))
                    dve.max_index(topi[s], top[:, t, :], scr[s]).then_inc(a["topi"], 1)
                t = i
                if 0 <= t < NT:
                    s = t % 2
                    dve.wait_ge(a["comb"], a.count("comb", t + 1))
                    dve.bn_stats(stA[s], x[:, t, :]).then_inc(a["bnA"], 1)
                t = i - 1
                if 0 <= t < NT:
                    s = t % 2
                    dve.wait_ge(a["th"], a.count("th", t + 1))
                    dve.scalar_tensor_tensor(ffbuf[s], ffbuf[s], 1.0, MA[:, :], ALU.add, ALU.mult).then_inc(a["gg"], 1)
                t = i
                if 0 <= t < NT:
                    s = t % 2
                    dve.wait_ge(a["bnA"], a.count("bnA", t + 1))
                    dve.bn_aggr(mvA[s], stA[s]).then_inc(a["mvA"], 1)
                t = i - 5
                if 0 <= t < NT:
                    s = t % 2
                    dve.wait_ge(a["topi"], a.count("topi", t + 1))
                    dve.tensor_tensor(oh[s], iota8[:, :].unsqueeze(1).to_broadcast([P, 2, E]),
                                      topi[s][:, 0:2].unsqueeze(2).to_broadcast([P, 2, E]), ALU.is_equal).then_inc(a["oh"], 1)
                t = i
                if 0 <= t < NT:
                    s = t % 2
                    dve.wait_ge(a["mvA"], a.count("mvA", t + 1))
                    dve.tensor_scalar(veA[s], mvA[s][:, 1:2], 1.0 + EPS, EPS * EPS, ALU.mult, ALU.add).then_inc(a["veA"], 1)
                t = i - 5
                if 0 <= t < NT:
                    s = t % 2
                    dve.wait_ge(a["oh"], a.count("oh", t + 1))
                    dve.tensor_tensor(picks[s], oh[s][:, 0, :], oh[s][:, 1, :], ALU.add).then_inc(a["picks"], 1)

            def schedule(l):
                m = M[l]
                dve.wait_ge(A[l]["top"], A[l].count("top", NT))
                dve.tensor_tensor(margin[:, :], top[:, :, 1], top[:, :, 0], ALU.subtract).then_inc(m["margin"], 1)
                dve.wait_ge(m["cnt"], m.count("cnt", 1))
                dve.tensor_scalar(cnt_i[:, :], MD[0:1, 2 * P + E:2 * P + 2 * E], float(P - 1), None, ALU.add).then_inc(m["plan"], 1)
                dve.wait_ge(m["plan"], m.count("plan", 1))
                dve.tensor_scalar(cnt_s[:, :], cnt_i[:, :], 7, None, ALU.arith_shift_right).then_inc(m["plan"], 1)
                dve.wait_ge(m["plan"], m.count("plan", 2))
                dve.tensor_copy(ntile[:, :], cnt_s[:, :]).then_inc(m["plan"], 1)
                dve.wait_ge(m["plan"], m.count("plan", 3))
                dve.tensor_scalar(wgt[:, :], ntile[:, :], -float(P), float(REGION), ALU.mult, ALU.add).then_inc(m["plan"], 1)
                dve.tensor_tensor_scan(cum[:, :], ones1[:, :], ntile[:, :], 0.0, ALU.mult, ALU.add).then_inc(m["plan"], 1)
                dve.wait_ge(m["plan"], m.count("plan", 5))
                dve.tensor_tensor(ind[:, :, :], jidx[:, :].unsqueeze(2).to_broadcast([1, NJ, E - 1]),
                                  cum[:, 0:E - 1].unsqueeze(1).to_broadcast([1, NJ, E - 1]), ALU.is_ge).then_inc(m["plan"], 1)
                dve.wait_ge(m["plan"], m.count("plan", 6))
                dve.reduce_sum(ef[:, :], ind[:, :, :], AX)
                dve.tensor_tensor(ind2[:, :, :], ind[:, :, :], wgt[:, 0:E - 1].unsqueeze(1).to_broadcast([1, NJ, E - 1]), ALU.mult).then_inc(m["plan"], 1)
                dve.wait_ge(m["plan"], m.count("plan", 7))
                dve.reduce_sum(rf[:, :], ind2[:, :, :], AX).then_inc(m["plan"], 1)
                dve.wait_ge(m["plan"], m.count("plan", 8))
                dve.scalar_tensor_tensor(rf2[:, :], jidx[:, :], float(P), rf[:, :], ALU.mult, ALU.add).then_inc(m["plan"], 1)
                dve.wait_ge(m["plan"], m.count("plan", 9))
                dve.tensor_copy(sched[l][:, 0, :], ef[:, :])
                dve.tensor_copy(sched[l][:, 1, :], rf2[:, :]).then_inc(m["sched"], 1)
                dve.wait_ge(m["g1"], m.count("g1", 1))
                dve.tensor_scalar(gtmp[:, 1, :], gtmp[:, 0, :], 1.0, None, ALU.add).then_inc(m["gates"], 1)
                dve.wait_ge(m["gates"], m.count("gates", 1))
                dve.reciprocal(gate[:, 0, :], gtmp[:, 1, :]).then_inc(m["gates"], 1)
                dve.wait_ge(m["gates"], m.count("gates", 2))
                dve.tensor_tensor(gate[:, 1, :], gtmp[:, 0, :], gate[:, 0, :], ALU.mult).then_inc(m["gates"], 1)

            def moe(l):
                m = M[l]
                if l == 1:
                    dve.wait_ge(ld["moe1"], 64)
                    expert = [dve.value_load(sched[1][0:1, 0, at(0)], min_val=0, max_val=E - 1)]
                for j in range(NJ + 3):
                    t = j - 1
                    if 0 <= t < NJ:
                        s = t % 2
                        if l == 0:
                            dve.wait_ge(m["act1"], m.count("act1", t + 1))
                            dve.tensor_tensor(ha[s][:, 0:F0], ha[s][:, 0:F0], S[s][:, F0:2 * F0], ALU.mult).then_inc(m["act2"], 1)
                        else:
                            dve.wait_ge(m["up"], m.count("up", t + 1))
                            if t >= 2:
                                dve.wait_ge(m["Th"], m.count("Th", t - 1))
                            dve.tensor_tensor(ha[s], S[s][:, :], b1bc[:, expert[t], :], ALU.add).then_inc(m["act1"], 1)
                    t = j - 3
                    if 0 <= t < NJ:
                        s = t % 2
                        dve.wait_ge(m["down"], m.count("down", t + 1))
                        if t >= 2:
                            dve.wait_ge(sentb[(t - 2) % XB], sentb_count(l, t - 2))
                        src = (MC, MD)[s][:, 0:D]
                        if l == 0:
                            dve.tensor_copy(ysb[s], src).then_inc(m["y"], 1)
                        else:
                            dve.tensor_tensor(ysb[s], src, b2bc[:, expert[t], :], ALU.add).then_inc(m["y"], 1)
                    if l == 1 and j + 1 < NJ:
                        expert.append(dve.value_load(sched[1][0:1, 0, at(j + 1)], min_val=0, max_val=E - 1))

            for l in range(2):
                if l == 1:
                    dve.wait_ge(M[0]["gates"], M[0].count("gates", 3))
                    dve.memset(before[0], 0.0).then_inc(M[0]["zero"], 1)
                    dve.wait_ge(M[0]["zero"], M[0].count("zero", 1))
                    dve.wait_ge(ld["l1b"], 16 * 4)
                for i in range(NT + LAG[l]):
                    step0(i) if l == 0 else step1(i)
                    if l == 0 and i == 1:
                        keys_and_values()
                schedule(l)
                if l == 0:
                    for n in range(1, NBATCH * 3, 2):
                        b, g = n // 3, n % 3
                        w = min(4, CH - 4 * g)
                        dve.wait_ge(pro1["fT"], pro1.count("fT", n + 1))
                        dve.tensor_copy(vals1[:, b, 4 * g:4 * g + w, :],
                                        TP[1][:, 0:w * P].rearrange("p (c d) -> p c d", c=w)).then_inc(pro1["vals1o"], 1)
                moe(l)
            m = M[1]
            dve.wait_ge(m["gates"], m.count("gates", 3))
            for t in range(NT):
                if t % 2 == 0:
                    dve.wait_ge(xs_in[t // 2], 16 * (2 * ring_uses(t // 2) + 1))
                y0, y1 = ylast[t // 2][:, t % 2, 0, :], ylast[t // 2][:, t % 2, 1, :]
                dve.scalar_tensor_tensor(y0, y0, gate[:, 0, t:t + 1], x[:, t, :], ALU.mult, ALU.add).then_inc(m["fin0"], 1)
                dve.wait_ge(m["fin0"], m.count("fin0", t + 1))
                dve.scalar_tensor_tensor(x[:, t, :], y1, gate[:, 1, t:t + 1], y0, ALU.mult, ALU.add).then_inc(m["fin"], 1)

        @block.tensor
        def _(pe):
            mm = nc.tensor.matmul
            tr = nc.tensor.transpose
            pe.wait_ge(const, NCONST)
            pe.wait_ge(ld["ctx"], 48)
            for b in range(NBATCH):
                ins = tr(MD[:, b * KEYS:(b + 1) * KEYS], ctx_sb[:, b, :], ident[0:KEYS, 0:KEYS])
            ins.then_inc(pro["ctxT"], 1)
            pe.wait_ge(pro["ctxTs"], pro.count("ctxTs", 1))
            for b in range(NBATCH):
                ins = mm(MC[0:KEYS, b * D:(b + 1) * D], ctxT[:, b * KEYS:(b + 1) * KEYS], wk0[:, :], start=True, stop=True)
            ins.then_inc(pro["k"], 1)
            mm(MA[:, 0:NBATCH * KEYS], wv0[:, :], ctxT[:, :], start=True, stop=True).then_inc(pro["v"], 1)
            pe.wait_ge(pro["cn"], pro.count("cn", 1))
            for b in range(NBATCH):
                ins = tr(MD[:, b * KEYS:(b + 1) * KEYS], cn[:, b, :], ident[0:KEYS, 0:KEYS])
            ins.then_inc(pro["cT"], 1)
            pe.wait_ge(ld["l1"], 160)
            for g in range(2):
                for k in range(4):
                    ins = tr(S[g][:, k * P:(k + 1) * P], wq1[:, (4 * g + k) * P:(4 * g + k + 1) * P], ident[:, :])
                ins.then_inc(pro["wqT"], 1)
            pe.wait_ge(pro["cTs"], pro.count("cTs", 1))
            mm(TP[0][:, 0:NBATCH * KEYS], wkk[:, :, :].rearrange("p r d -> p (r d)"), ctxT[:, :], start=True, stop=True).then_inc(pro["kv1"], 1)
            mm(TP[1][:, 0:NBATCH * KEYS], wvv[:, :, :].rearrange("p r d -> p (r d)"), ctxT[:, :], start=True, stop=True).then_inc(pro["kv1"], 1)
            pe.wait_ge(pro["vT1"], pro.count("vT1", 1))
            pe.wait_ge(pro["klo"], pro.count("klo", 1))
            for b in range(NBATCH):
                dst = (S[2], MC, TP[0], TP[1])[b]
                for g in range(NG):
                    n = b * NG + g
                    src = k0split[:, n // 8].rearrange("k r s w d -> k (r s w d)")[:, (n % 8) * P:(n % 8 + 1) * P]
                    ins = tr(dst[:, g * KEYS:(g + 1) * KEYS], src, ident[0:KEYS, 0:KEYS])
                ins.then_inc(pro["kT"], 1)
            pe.wait_ge(pro["wqTs"], pro.count("wqTs", 2))
            for h in range(H):
                r = HD1 * (h % 2)
                if h >= 2:
                    pe.wait_ge(pro["keys1"], pro.count("keys1", h - 1))
                mm(S[h % 2][:, 0:NBATCH * KEYS], wq1T[r:r + HD1, h // 2, :], kT1[r:r + HD1, :], start=True, stop=True).then_inc(pro["fk"], 1)
            pe.wait_ge(ld["q"], 48)
            pe.wait_ge(ld["o"], 48)

            def values(n0, n1):
                if n0 == 0:
                    pe.wait_ge(pro["keys0"], pro.count("keys0", NBATCH))
                for n in range(n0, n1):
                    b, g = n // 3, n % 3
                    filled_by = "vblk" if b % 2 == 0 else "vblko"
                    pe.wait_ge(pro[filled_by], pro.count(filled_by, b // 2 + 1))
                    if n >= 2:
                        pe.wait_ge(pro["vals0"], pro.count("vals0", n - 1))
                    for c in range(4 * g, min(4 * g + 4, CH)):
                        tr(TP[n % 2][:, (c - 4 * g) * P:(c - 4 * g + 1) * P], vblk[b][:, c * P:(c + 1) * P], ident[:, :]).then_inc(pro["vtp"], 1)

            def step0(i):
                a = A[0]
                t = i - 5
                if 0 <= t < NT:
                    s = t % 2
                    pe.wait_ge(a["qT"], a.count("qT", t + 1))
                    if t >= 1:
                        pe.wait_ge(a["sub"], a.count("sub", t))
                    b, tt = t // TPB, t % TPB
                    for bank, (h0, n) in enumerate(zip(BANK_AT, BANK_HEADS)):
                        for half in range(2):
                            for o in range(0, n * KEYS, GK):
                                w = min(GK, n * KEYS - o)
                                mm(S[bank][:, o:o + w], ident_r[:, :], bias_r[:, half, tt, 0:w], start=half == 0 and o == 0, stop=False)
                        for g, h, e in BANK_PARTS[bank]:
                            ins = mm(S[bank][:, (h - h0) * KEYS:(e - h0) * KEYS], qT[s][:, g * P:(g + 1) * P],
                                     keys0[:, b, h * KEYS:e * KEYS], start=False, stop=e == h0 + n)
                    ins.then_inc(a["S"], 1)
                t = i - 8
                if 0 <= t < NT:
                    s = t % 2
                    pe.wait_ge(a["xnD"], a.count("xnD", t + 1))
                    tr(MD[:, P:2 * P], pay[s][:, 0, 0:D], ident[:, :]).then_inc(a["Tx2"], 1)
                t = i - 2
                if 0 <= t < NT:
                    s = t % 2
                    pe.wait_ge(a["xnA"], a.count("xnA", t + 1))
                    tr(MA[:, 0:P], xnA[s], ident[:, :]).then_inc(a["TxA"], 1)
                t = i - 7
                if 0 <= t < NT:
                    s = t % 2
                    pe.wait_ge(a["on"], a.count("on", t + 1))
                    tr(MC[:, 2 * P:3 * P], on[s], ident[:, :]).then_inc(a["To"], 1)
                t = i - 6
                if 0 <= t < NT:
                    s = t % 2
                    pe.wait_ge(a["exp"], a.count("exp", t + 1))
                    for c in range(4):
                        ins = tr(TP[0][:, c * P:(c + 1) * P], prob[s][:, c * P:(c + 1) * P], ident[:, :])
                    ins.then_inc(a["TP0"], 1)
                t = i - 2
                if 0 <= t < NT:
                    s = t % 2
                    pe.wait_ge(a["xT"], a.count("xT", t + 1))
                    mm(MA[:, P:2 * P], xT[s], wq0[:, :], start=True, stop=True).then_inc(a["q"], 1)
                t = i - 6
                if 0 <= t < NT:
                    s = t % 2
                    for c in range(4, 8):
                        ins = tr(TP[1][:, (c - 4) * P:(c - 3) * P], prob[s][:, c * P:(c + 1) * P], ident[:, :])
                    ins.then_inc(a["TP1"], 1)
                t = i - 7
                if 0 <= t < NT:
                    s = t % 2
                    pe.wait_ge(a["oT"], a.count("oT", t + 1))
                    mm(MD[:, 0:D], oT[s], wo0[:, :], start=True, stop=True).then_inc(a["Wo"], 1)
                t = i - 6
                if 0 <= t < NT:
                    s = t % 2
                    pe.wait_ge(a["PT0"], a.count("PT0", t + 1))
                    for c in range(8, CH):
                        ins = tr(TP[0][:, (c - 8) * P:(c - 7) * P], prob[s][:, c * P:(c + 1) * P], ident[:, :])
                    ins.then_inc(a["TP2"], 1)
                t = i - 4
                if 0 <= t < NT:
                    s = t % 2
                    pe.wait_ge(a["qb"], a.count("qb", min(t + 3, NT)))
                    pe.wait_ge(a["lo"], a.count("lo", t + 1))
                    halves = qsplit[s].rearrange("p h a b d -> p (h a b d)")
                    for g in range(NG):
                        ins = tr(MA[:, g * P:(g + 1) * P], halves[:, g * P:(g + 1) * P], ident[:, :])
                    ins.then_inc(a["Tq"], 1)
                t = i - 8
                if 0 <= t < NT:
                    s = t % 2
                    pe.wait_ge(a["xa"], a.count("xa", min(t + 2, NT)))
                    pe.wait_ge(a["x2T"], a.count("x2T", t + 1))
                    mm(MD[:, 2 * P:2 * P + E], x2T[s], wr[0][:, :], start=True, stop=True).then_inc(a["route"], 1)
                t = i - 6
                if 0 <= t < NT:
                    s = t % 2
                    pe.wait_ge(a["PT2"], a.count("PT2", t + 1))
                    for c, (h, e) in enumerate(CHUNK_HEADS):
                        ins = mm(MC[:, h * VW:e * VW], probT[s][:, c * P:(c + 1) * P],
                                 vals0[:, t // TPB, c, h:e, :].rearrange("p h v -> p (h v)"), start=c == 0, stop=c == CH - 1)
                    ins.then_inc(a["AV"], 1)
                t = i - 8
                if 0 <= t < NT:
                    s = t % 2
                    pe.wait_ge(a["picks"], a.count("picks", t + 1))
                    mm(RANK, upper[:, :], picks[s], start=True, stop=False)
                    mm(RANK, ones_b[:, :], before[s], start=False, stop=False)
                    mm(RANK, ones_b[0:1, :], ebase_b[0:1, :], start=False, stop=True).then_inc(a["rank"], 1)

            def step1(i):
                a = A[1]
                t = i - 8
                if 0 <= t < NT:
                    s = t % 2
                    pe.wait_ge(a["xnD"], a.count("xnD", t + 1))
                    if t >= 1:
                        pe.wait_ge(a["rsel"], a.count("rsel", t))
                    tr(MD[:, P:2 * P], pay[s][:, 0, 0:D], ident[:, :]).then_inc(a["Tx2"], 1)
                t = i - 4
                if 0 <= t < NT:
                    s = t % 2
                    pe.wait_ge(a["xnA"], a.count("xnA", t + 1))
                    if t >= 2:
                        pe.wait_ge(a["fo"], a.count("fo", t - 1))
                    tr(MA[:, 0:P], xnA[s], ident[:, :]).then_inc(a["TxA"], 1)
                t = i - 6
                if 0 <= t < NT:
                    s = t % 2
                    pe.wait_ge(a["norm"], a.count("norm", t + 1))
                    for c in range(8, CH):
                        ins = tr(TP[0][:, (c - 8) * P:(c - 7) * P], prob[s][:, c * P:(c + 1) * P], ident[:, :])
                    ins.then_inc(a["TP2"], 1)
                    for c in range(4, 8):
                        ins = tr(TP[1][:, (c - 4) * P:(c - 3) * P], prob[s][:, c * P:(c + 1) * P], ident[:, :])
                    ins.then_inc(a["TP1"], 1)
                t = i - 4
                if 0 <= t < NT:
                    s = t % 2
                    pe.wait_ge(a["xT"], a.count("xT", t + 1))
                    for k in range(FF // P):
                        ins = mm(MA[:, k * P:(k + 1) * P], wff1[:, FF + k * P:FF + (k + 1) * P], xT[s], start=True, stop=True)
                    ins.then_inc(a["ffg"], 1)
                t = i - 8
                if 0 <= t < NT:
                    s = t % 2
                    pe.wait_ge(a["x2T"], a.count("x2T", t + 1))
                    mm(MD[:, 2 * P:2 * P + E], x2T[s], wr[1][:, :], start=True, stop=True).then_inc(a["route"], 1)
                t = i - 6
                if 0 <= t < NT:
                    s = t % 2
                    pe.wait_ge(a["PT2"], a.count("PT2", t + 1))
                    for c in range(4):
                        ins = tr(TP[0][:, c * P:(c + 1) * P], prob[s][:, c * P:(c + 1) * P], ident[:, :])
                    ins.then_inc(a["TP0"], 1)
                t = i - 4
                if 0 <= t < NT:
                    s = t % 2
                    if t >= 1:
                        pe.wait_ge(a["sub"], a.count("sub", t))
                    for bank, (h0, n) in enumerate(zip(BANK_AT, BANK_HEADS)):
                        ins = mm(S[bank][:, 0:n * KEYS], xT[s], keys1[:, t // TPB, h0 * KEYS:(h0 + n) * KEYS], start=True, stop=True)
                    ins.then_inc(a["S"], 1)
                t = i - 8
                if 0 <= t < NT:
                    s = t % 2
                    pe.wait_ge(a["picks"], a.count("picks", t + 1))
                    mm(RANK, upper[:, :], picks[s], start=True, stop=False)
                    mm(RANK, ones_b[:, :], before[s], start=False, stop=False)
                    mm(RANK, ones_b[0:1, :], ebase_b[0:1, :], start=False, stop=True).then_inc(a["rank"], 1)
                t = i - 5
                if 0 <= t < NT:
                    s = t % 2
                    pe.wait_ge(a["gg"], a.count("gg", min(t + 2, NT)))
                    for k in range(FF // P):
                        ins = mm(MA[:, k * P:(k + 1) * P], wff1[:, k * P:(k + 1) * P], xT[s], start=True, stop=True)
                    ins.then_inc(a["ffh"], 1)
                t = i - 6
                if 0 <= t < NT:
                    s = t % 2
                    pe.wait_ge(a["PT0"], a.count("PT0", t + 1))
                    for c in range(CH):
                        mm(MC[:, 0:D], probT[s][:, c * P:(c + 1) * P], vals1[:, t // TPB, c, :], start=c == 0, stop=False)
                    for k in range(FF // P):
                        ins = mm(MC[:, 0:D], gated[:, t % 4, k * P:(k + 1) * P], wff2[:, k, :], start=False, stop=k == FF // P - 1)
                    ins.then_inc(a["AV"], 1)

            def fold(h0, h1):
                for h in range(h0, h1):
                    r = HD1 * (h % 2)
                    if h >= 4:
                        pe.wait_ge(pro1["foldT"], pro1.count("foldT", h - 3))
                    mm(FOLD[h % 4][:, 0:NBATCH * KEYS], wo1[r:r + HD1, h // 2, :], vT1[r:r + HD1, :], start=True, stop=True).then_inc(pro1["fv"], 1)

            def moe(l):
                m = M[l]
                up = w13 if l == 0 else w1b
                w2 = w2a if l == 0 else w2b
                nk = (F0 if l == 0 else F1) // P
                if l == 0:
                    pe.wait_ge(ld["moe0"], 48)
                else:
                    pe.wait_ge(ld["moe1"], 64)
                pe.wait_ge(m["sched"], m.count("sched", 1))
                expert = [pe.value_load(sched[l][0:1, 0, at(0)], min_val=0, max_val=E - 1)]
                for j in range(NJ + 3):
                    if j < NJ:
                        pe.wait_ge(xs_in[j % XB], xs_count(l, j))
                        if j >= 1:
                            pe.wait_ge(m["xsT"], m.count("xsT", j))
                        tr(MA[:, 0:P], xs[j % XB][:, 0:D], ident[:, :]).then_inc(m["Tx"], 1)
                    t = j - 1
                    if 0 <= t < NJ:
                        s = t % 2
                        pe.wait_ge(m["xsT"], m.count("xsT", t + 1))
                        if t >= 2:
                            read = "act2" if l == 0 else "act1"
                            pe.wait_ge(m[read], m.count(read, t - 1))
                        mm(S[s][:, :], xsT[s], up[:, expert[t], :], start=True, stop=True).then_inc(m["up"], 1)
                        if t + 1 < NJ:
                            expert.append(pe.value_load(sched[l][0:1, 0, at(t + 1)], min_val=0, max_val=E - 1))
                    t = j - 3
                    if 0 <= t < NJ:
                        s = t % 2
                        pe.wait_ge(m["hT"], m.count("hT", t + 1))
                        if t >= 2:
                            pe.wait_ge(m["y"], m.count("y", t - 1))
                        for k in range(nk):
                            ins = mm((MC, MD)[s][:, 0:D], hT[s][:, k * P:(k + 1) * P], w2[:, expert[t], k, :], start=k == 0, stop=k == nk - 1)
                        ins.then_inc(m["down"], 1)
                    t = j - 2
                    if 0 <= t < NJ:
                        s = t % 2
                        pe.wait_ge(m["act2"], m.count("act2", t + 1))
                        if t >= 2:
                            pe.wait_ge(m["hT"], m.count("hT", t - 1))
                        for k in range(nk):
                            ins = tr(TP[s][:, k * P:(k + 1) * P], ha[s][:, k * P:(k + 1) * P], ident[:, :])
                        ins.then_inc(m["Th"], 1)

            for l in range(2):
                for i in range(NT + LAG[l]):
                    step0(i) if l == 0 else step1(i)
                    if l == 0 and i in (2, 3):
                        values(6 * (i - 2), 6 * (i - 1))
                    if l == 0 and i == 4:
                        pe.wait_ge(pro["identr"], pro.count("identr", 1))
                        pe.wait_ge(pro["blo"], pro.count("blo", TPB))
                    if l == 0 and i == NT - 1 + 6:
                        fold(0, 4)
                    if l == 0 and i == NT + 6:
                        fold(4, 8)
                pe.wait_ge(A[l]["rsel"], A[l].count("rsel", NT))
                pe.wait_ge(A[l]["bef"], A[l].count("bef", NT))
                mm(RANK, ones_b[:, :], before[NT % 2], start=True, stop=True).then_inc(M[l]["cnt"], 1)
                if l == 0:
                    fold(8, H)
                    pe.wait_ge(pro1["foldT"], pro1.count("foldT", H))
                    for n in range(NBATCH * 3):
                        b, g = n // 3, n % 3
                        if n >= 2:
                            read = "vals1" if n % 2 == 0 else "vals1o"
                            pe.wait_ge(pro1[read], pro1.count(read, n // 2))
                        for c in range(4 * g, min(4 * g + 4, CH)):
                            ins = tr(TP[n % 2][:, (c - 4 * g) * P:(c - 4 * g + 1) * P], foldT[b][:, c * P:(c + 1) * P], ident[:, :])
                        ins.then_inc(pro1["fT"], 1)
                moe(l)


_INS = ['x', 'ctx_1024', 'fside_SxS2_0', 'L0_xattn_Wq', 'L0_xattn_bq', 'L0_xattn_Wk', 'L0_xattn_Wv', 'L0_xattn_Wo',
        'L0_xattn_bo', 'L0_xattn_scale_mul_log', 'L0_ffn_Wr', 'L0_ffn_W1', 'L0_ffn_W2', 'L0_ffn_W3', 'L1_xattn_ln_g',
        'L1_xattn_ln_b', 'L1_xattn_cln_g', 'L1_xattn_cln_b', 'L1_xattn_Wq', 'L1_xattn_Wkv', 'L1_xattn_Wo',
        'L1_xattn_Wff1', 'L1_xattn_Wff2', 'L1_ffn_W1', 'L1_ffn_b1', 'L1_ffn_W2', 'L1_ffn_b2', 'L1_ffn_Wr', 'L1_ffn_br']


def kernel(**inputs):
    import numpy as _np
    import concourse.bacc as _bacc
    from concourse import mybir as _mybir
    from concourse.bass_utils import run_bass_kernel_spmd as _run

    nc = _bacc.Bacc("TRN2", target_bir_lowering=False, num_devices=1)
    arrays, args = {}, []
    for name in _INS:
        a = _np.ascontiguousarray(inputs[name])
        arrays[f"in_{name}_dram"] = a
        args.append(nc.dram_tensor(f"in_{name}_dram", a.shape, _mybir.dt.from_np(a.dtype), kind="ExternalInput").ap())
    shape = inputs['x'].shape
    args.append(nc.dram_tensor("out_0_dram", shape, _mybir.dt.from_np(_np.dtype("float32")), kind="ExternalOutput").ap())
    bass_xattn_moe_two_layers(nc, *args)
    r = _run(nc, [arrays], core_ids=[0])
    return r.results[0]["out_0_dram"]
```
